# Optimizing a Trainium2 kernel written in Bass

```python
import numpy as np
import jax
import jax.numpy as jnp

def _softmax(x, axis=-1):
    return jax.nn.softmax(x, axis=axis)

def _gelu(x):
    return jax.nn.gelu(x, approximate=True)

def _silu(x):
    return jax.nn.silu(x)

def _sigmoid(x):
    return jax.nn.sigmoid(x)

def _layernorm(x, axis=-1, eps=1e-05):
    m = jnp.mean(x, axis=axis, keepdims=True)
    v = jnp.var(x, axis=axis, keepdims=True)
    return (x - m) / jnp.sqrt(v + eps)

def _scatter_add(tgt, idx, src, axis=0):
    return tgt.at[idx].add(src)

def _segment_sum(src, seg, n):
    return jax.ops.segment_sum(src, seg, n)
kernel_name = 'mk_adaln_d1_jaxref_r8_bfe797'

def setup_inputs(seed: int=0):
    np.random.seed(seed)
    _w = jnp.asarray

    def _L0_attn_setup():
        import jax, jax.numpy as jnp
        import numpy as np
        D_MODEL = 128
        D_STATE = 64
        D_CONV = 4
        EXPAND = 2
        HEADDIM = 128
        D_INNER = EXPAND * D_MODEL
        NHEADS = D_INNER // HEADDIM
        CONV_DIM = D_INNER + 2 * D_STATE
        D_IN_PROJ = 2 * D_INNER + 2 * D_STATE + NHEADS
        EPS = 1e-05

        def _silu(x):
            return x * jax.nn.sigmoid(x)

        def _causal_conv_silu(x, w, b):
            L = x.shape[1]
            xp = jnp.pad(x, ((0, 0), (D_CONV - 1, 0), (0, 0)))
            out = b
            for k in range(D_CONV):
                out = out + xp[:, k:k + L, :] * w[:, k]
            return _silu(out)

        def _ssd_scan(x, dt, A, B, C):
            bsz = x.shape[0]

            def step(h, inp):
                x_t, dt_t, B_t, C_t = inp
                dA = jnp.exp(dt_t * A)
                h = h * dA[:, :, None, None] + jnp.einsum('bh,bhp,bn->bhpn', dt_t, x_t, B_t)
                y = jnp.einsum('bhpn,bn->bhp', h, C_t)
                return (h, y)
            h0 = jnp.zeros((bsz, NHEADS, HEADDIM, D_STATE), x.dtype)
            xs = (jnp.moveaxis(x, 1, 0), jnp.moveaxis(dt, 1, 0), jnp.moveaxis(B, 1, 0), jnp.moveaxis(C, 1, 0))
            _, y = jax.lax.scan(step, h0, xs)
            return jnp.moveaxis(y, 0, 1)

        def _branch(zxbcdt, conv_w, conv_b, dt_bias, A_log, D, norm_w):
            b, l, _ = zxbcdt.shape
            z = zxbcdt[..., :D_INNER]
            xBC = zxbcdt[..., D_INNER:D_INNER + CONV_DIM]
            dt = jax.nn.softplus(zxbcdt[..., -NHEADS:] + dt_bias)
            A = -jnp.exp(A_log)
            xBC = _causal_conv_silu(xBC, conv_w, conv_b)
            x = xBC[..., :D_INNER].reshape(b, l, NHEADS, HEADDIM)
            Bm = xBC[..., D_INNER:D_INNER + D_STATE]
            Cm = xBC[..., D_INNER + D_STATE:]
            y = _ssd_scan(x, dt, A, Bm, Cm) + D[None, None, :, None] * x
            y = y.reshape(b, l, D_INNER)
            yz = y * _silu(z)
            return yz * jax.lax.rsqrt(jnp.mean(yz * yz, axis=-1, keepdims=True) + EPS) * norm_w
        key = jax.random.key(seed)
        ks = jax.random.split(key, 12)
        B, L = (2, 512)

        def gauss(k, shape, scale):
            return jax.random.normal(k, shape, jnp.float32) * scale

        def dt_bias_init(k):
            lo, hi = (np.log(0.001), np.log(0.1))
            dt = jnp.exp(jax.random.uniform(k, (NHEADS,)) * (hi - lo) + lo)
            dt = jnp.clip(dt, 0.0001, None)
            return dt + jnp.log(-jnp.expm1(-dt))
        return {'u': jax.random.normal(ks[0], (B, L, D_MODEL), jnp.float32), 'in_proj_w': gauss(ks[1], (D_IN_PROJ, D_MODEL), 0.02), 'conv_w': gauss(ks[2], (CONV_DIM, D_CONV), 0.2), 'conv_b': jnp.zeros((CONV_DIM,), jnp.float32), 'conv_w_bw': gauss(ks[3], (CONV_DIM, D_CONV), 0.2), 'conv_b_bw': jnp.zeros((CONV_DIM,), jnp.float32), 'dt_bias': dt_bias_init(ks[4]), 'dt_bias_bw': dt_bias_init(ks[5]), 'A_log': jnp.log(jax.random.uniform(ks[6], (NHEADS,), minval=1.0, maxval=16.0)), 'A_b_log': jnp.log(jax.random.uniform(ks[7], (NHEADS,), minval=1.0, maxval=16.0)), 'D': jnp.ones((NHEADS,), jnp.float32), 'D_b': jnp.ones((NHEADS,), jnp.float32), 'norm_w': jnp.ones((D_INNER,), jnp.float32), 'out_proj_w': gauss(ks[8], (D_MODEL, D_INNER), 0.02)}
    _L0_attn_in = _L0_attn_setup()

    def _L0_ffn_setup():
        import jax, jax.numpy as jnp
        import numpy as np
        D_MODEL = 128
        D_FF = 512
        NUM_EXPERTS = 8
        key = jax.random.key(seed)
        ks = jax.random.split(key, 8)
        scale_in = 1.0 / np.sqrt(D_MODEL)
        scale_ff = 1.0 / np.sqrt(D_FF)
        x = jax.random.normal(ks[0], (4, 256, D_MODEL), dtype=jnp.float32)
        gate_w = jax.random.uniform(ks[1], (NUM_EXPERTS, D_MODEL), jnp.float32, -scale_in, scale_in)
        gate_b = jax.random.uniform(ks[2], (NUM_EXPERTS,), jnp.float32, -scale_in, scale_in)
        expert_bias = jnp.zeros((NUM_EXPERTS,), dtype=jnp.float32)
        w1 = jax.random.uniform(ks[3], (NUM_EXPERTS, D_MODEL, D_FF), jnp.float32, -scale_in, scale_in)
        b1 = jax.random.uniform(ks[4], (NUM_EXPERTS, D_FF), jnp.float32, -scale_in, scale_in)
        w2 = jax.random.uniform(ks[5], (NUM_EXPERTS, D_FF, D_MODEL), jnp.float32, -scale_ff, scale_ff)
        b2 = jax.random.uniform(ks[6], (NUM_EXPERTS, D_MODEL), jnp.float32, -scale_ff, scale_ff)
        return {'x': x, 'gate_w': gate_w, 'gate_b': gate_b, 'expert_bias': expert_bias, 'w1': w1, 'b1': b1, 'w2': w2, 'b2': b2}
    _L0_ffn_in = _L0_ffn_setup()
    _L0_c = _w((lambda *s: np.random.randn(*s).astype(np.float32) * 0.05)(2, 128))
    _L0_wmod = _w((lambda *s: np.random.randn(*s).astype(np.float32) * 0.05)(128, 6 * 128) * 128 ** (-0.5))
    _d = {'L0_attn_u': _L0_attn_in['u'], 'L0_attn_in_proj_w': _L0_attn_in['in_proj_w'], 'L0_attn_conv_w': _L0_attn_in['conv_w'], 'L0_attn_conv_b': _L0_attn_in['conv_b'], 'L0_attn_conv_w_bw': _L0_attn_in['conv_w_bw'], 'L0_attn_conv_b_bw': _L0_attn_in['conv_b_bw'], 'L0_attn_dt_bias': _L0_attn_in['dt_bias'], 'L0_attn_dt_bias_bw': _L0_attn_in['dt_bias_bw'], 'L0_attn_A_log': _L0_attn_in['A_log'], 'L0_attn_A_b_log': _L0_attn_in['A_b_log'], 'L0_attn_D': _L0_attn_in['D'], 'L0_attn_D_b': _L0_attn_in['D_b'], 'L0_attn_norm_w': _L0_attn_in['norm_w'], 'L0_attn_out_proj_w': _L0_attn_in['out_proj_w'], 'L0_ffn_gate_w': _L0_ffn_in['gate_w'], 'L0_ffn_gate_b': _L0_ffn_in['gate_b'], 'L0_ffn_expert_bias': _L0_ffn_in['expert_bias'], 'L0_ffn_w1': _L0_ffn_in['w1'], 'L0_ffn_b1': _L0_ffn_in['b1'], 'L0_ffn_w2': _L0_ffn_in['w2'], 'L0_ffn_b2': _L0_ffn_in['b2'], 'L0_c': _L0_c, 'L0_wmod': _L0_wmod}
    _x0 = _d['L0_attn_u']
    _d['L0_attn_u'] = jax.random.normal(jax.random.fold_in(jax.random.key(seed), 1), (2, 2048, 128), dtype=_x0.dtype)
    del _x0
    return _d

def reference(L0_attn_u, L0_attn_in_proj_w, L0_attn_conv_w, L0_attn_conv_b, L0_attn_conv_w_bw, L0_attn_conv_b_bw, L0_attn_dt_bias, L0_attn_dt_bias_bw, L0_attn_A_log, L0_attn_A_b_log, L0_attn_D, L0_attn_D_b, L0_attn_norm_w, L0_attn_out_proj_w, L0_ffn_gate_w, L0_ffn_gate_b, L0_ffn_expert_bias, L0_ffn_w1, L0_ffn_b1, L0_ffn_w2, L0_ffn_b2, L0_c, L0_wmod):

    def _L0_attn_ref(u, in_proj_w, conv_w, conv_b, conv_w_bw, conv_b_bw, dt_bias, dt_bias_bw, A_log, A_b_log, D, D_b, norm_w, out_proj_w):
        import jax, jax.numpy as jnp
        import numpy as np
        D_MODEL = 128
        D_STATE = 64
        D_CONV = 4
        EXPAND = 2
        HEADDIM = 128
        D_INNER = EXPAND * D_MODEL
        NHEADS = D_INNER // HEADDIM
        CONV_DIM = D_INNER + 2 * D_STATE
        D_IN_PROJ = 2 * D_INNER + 2 * D_STATE + NHEADS
        EPS = 1e-05

        def _silu(x):
            return x * jax.nn.sigmoid(x)

        def _causal_conv_silu(x, w, b):
            L = x.shape[1]
            xp = jnp.pad(x, ((0, 0), (D_CONV - 1, 0), (0, 0)))
            out = b
            for k in range(D_CONV):
                out = out + xp[:, k:k + L, :] * w[:, k]
            return _silu(out)

        def _ssd_scan(x, dt, A, B, C):
            bsz = x.shape[0]

            def step(h, inp):
                x_t, dt_t, B_t, C_t = inp
                dA = jnp.exp(dt_t * A)
                h = h * dA[:, :, None, None] + jnp.einsum('bh,bhp,bn->bhpn', dt_t, x_t, B_t)
                y = jnp.einsum('bhpn,bn->bhp', h, C_t)
                return (h, y)
            h0 = jnp.zeros((bsz, NHEADS, HEADDIM, D_STATE), x.dtype)
            xs = (jnp.moveaxis(x, 1, 0), jnp.moveaxis(dt, 1, 0), jnp.moveaxis(B, 1, 0), jnp.moveaxis(C, 1, 0))
            _, y = jax.lax.scan(step, h0, xs)
            return jnp.moveaxis(y, 0, 1)

        def _branch(zxbcdt, conv_w, conv_b, dt_bias, A_log, D, norm_w):
            b, l, _ = zxbcdt.shape
            z = zxbcdt[..., :D_INNER]
            xBC = zxbcdt[..., D_INNER:D_INNER + CONV_DIM]
            dt = jax.nn.softplus(zxbcdt[..., -NHEADS:] + dt_bias)
            A = -jnp.exp(A_log)
            xBC = _causal_conv_silu(xBC, conv_w, conv_b)
            x = xBC[..., :D_INNER].reshape(b, l, NHEADS, HEADDIM)
            Bm = xBC[..., D_INNER:D_INNER + D_STATE]
            Cm = xBC[..., D_INNER + D_STATE:]
            y = _ssd_scan(x, dt, A, Bm, Cm) + D[None, None, :, None] * x
            y = y.reshape(b, l, D_INNER)
            yz = y * _silu(z)
            return yz * jax.lax.rsqrt(jnp.mean(yz * yz, axis=-1, keepdims=True) + EPS) * norm_w
        zxbcdt = u @ in_proj_w.T
        y_fw = _branch(zxbcdt, conv_w, conv_b, dt_bias, A_log, D, norm_w)
        y_bw = _branch(zxbcdt[:, ::-1, :], conv_w_bw, conv_b_bw, dt_bias_bw, A_b_log, D_b, norm_w)
        return (y_fw + y_bw[:, ::-1, :]) @ out_proj_w.T

    def _L0_ffn_ref(x, gate_w, gate_b, expert_bias, w1, b1, w2, b2):
        import jax, jax.numpy as jnp
        import numpy as np
        D_MODEL = 128
        D_FF = 512
        NUM_EXPERTS = 8
        gate_logits = jnp.einsum('bsd,ed->bse', x, gate_w) + gate_b + expert_bias
        top_idx = jnp.argmax(gate_logits, axis=-1)
        out = jnp.zeros_like(x)
        for e in range(NUM_EXPERTS):
            mask = (top_idx == e)[..., None].astype(x.dtype)
            h = jax.nn.relu(jnp.einsum('bsd,df->bsf', x, w1[e]) + b1[e])
            y = jnp.einsum('bsf,fd->bsd', h, w2[e]) + b2[e]
            out = out + mask * y
        return out
    x = L0_attn_u
    mod = (_silu(L0_c) @ L0_wmod).reshape(L0_c.shape[0], 6, 1, -1)
    sa, ca, ga, sb, cb, gb = (mod[:, 0], mod[:, 1], mod[:, 2], mod[:, 3], mod[:, 4], mod[:, 5])
    ga = (2 * (ga >= 0) - 1) * jnp.maximum(jnp.abs(ga), 0.25)
    gb = (2 * (gb >= 0) - 1) * jnp.maximum(jnp.abs(gb), 0.25)
    h = _layernorm(x, axis=-1) * (1 + ca) + sa
    x = x + ga * _L0_attn_ref(h, L0_attn_in_proj_w, L0_attn_conv_w, L0_attn_conv_b, L0_attn_conv_w_bw, L0_attn_conv_b_bw, L0_attn_dt_bias, L0_attn_dt_bias_bw, L0_attn_A_log, L0_attn_A_b_log, L0_attn_D, L0_attn_D_b, L0_attn_norm_w, L0_attn_out_proj_w)
    h = _layernorm(x, axis=-1) * (1 + cb) + sb
    x = x + gb * _L0_ffn_ref(h, L0_ffn_gate_w, L0_ffn_gate_b, L0_ffn_expert_bias, L0_ffn_w1, L0_ffn_b1, L0_ffn_w2, L0_ffn_b2)
    return x

_drawn_inputs = setup_inputs


def setup_inputs(seed=0):
    import zlib

    import numpy as np

    out = dict(_drawn_inputs(seed))
    spreads = {'L0_attn_conv_b': (0.0, 0.1),
     'L0_attn_conv_b_bw': (0.0, 0.1),
     'L0_attn_D': (1.0, 0.6),
     'L0_attn_D_b': (1.0, 0.6),
     'L0_attn_norm_w': (1.0, 0.6),
     'L0_ffn_expert_bias': (0.0, 0.1)}
    factors = {'L0_attn_dt_bias': 64.0,
     'L0_attn_dt_bias_bw': 64.0,
     'L0_attn_A_log': 8.0,
     'L0_attn_A_b_log': 8.0,
     'L0_ffn_gate_b': 3.121,
     'L0_ffn_b1': 8.0,
     'L0_ffn_b2': 8.0}
    for name, (base, spread) in spreads.items():
        noise = np.random.default_rng([zlib.crc32(name.encode()), seed]).standard_normal(out[name].shape)
        drawn = base * np.exp(spread * noise) if base else spread * noise
        out[name] = jnp.asarray(drawn.astype(out[name].dtype))
    for name, factor in factors.items():
        out[name] = (out[name] * factor).astype(out[name].dtype)
    return out
```

```python
from contextlib import ExitStack

import numpy as np

import concourse.bass as bass
from concourse import mybir

F32 = mybir.dt.float32
BF16 = mybir.dt.bfloat16
ALU = mybir.AluOpType
ACT = mybir.ActivationFunctionType
AX_X = mybir.AxisListType.X

P = 128
B, L, DM = 2, 2048, 128
NH, HD, NS = 2, 128, 64
DI = NH * HD
KC = 4
HALO = KC - 1
NE, FF = 8, 512
EPS = 1e-5
TPB = L // P
BT = 4
BLK = BT * P
NBLK = TPB // BT
NG = 3
STEPS = 2 * NBLK
CHUNKS = STEPS * BT
NDT = NH
ZW = DI + NDT
FC = FF // P
MASKED = -30000.0
NTOK = B * L
REGION = NTOK + P
NSLOT = NTOK // P + NE - 1
ROW = 2 * DM + 4


def step_of(s):
    return (1, NBLK - 1 - s) if s < NBLK else (0, s - NBLK)


def chunk_of(q):
    return (1, TPB - 1 - q) if q < TPB else (0, q - TPB)


def build(nc, u, w_xbc, w_zdt, conv_w, conv_b, dt_bias, a_log, d_skip, norm_w, w_out, gate_w, gate_b,
          w1, b1, w2, b2, c_t, wmod, out):
    ctx = ExitStack()
    with ctx:
        def sb(name, shape, dt=F32):
            return ctx.enter_context(nc.sbuf_tensor(name, shape, dt))

        def sem(name):
            return ctx.enter_context(nc.semaphore(name))

        bank = [ctx.enter_context(nc.psum_tensor(f"bank{i}", [P, 512], F32)) for i in range(8)]

        wx = sb("wx", [P, NG * P])
        wz = sb("wz", [P, ZW])
        cw = sb("cw", [P, 2, NG, KC])
        cb = sb("cb", [P, 2, NG])
        dtb = sb("dtb", [P, 2 * NH])
        alog = sb("alog", [P, 2 * NH])
        dsk = sb("dsk", [P, 2 * NH])
        nw = sb("nw", [P, NH])
        wo = sb("wo", [P, NH, DM])
        won = sb("won", [P, NH, DM])
        gw = sb("gw", [P, NE])
        gbias = sb("gbias", [P, 2, NE])
        gb_sum = sb("gb_sum", [P, NE])
        ct_in = sb("ct_in", [P, B])
        csil = sb("csil", [P, B])
        csil_bc = sb("csil_bc", [P, B, P])
        wm = sb("wm", [P, 6 * DM])
        modc = sb("modc", [P, 2, B])
        row = sb("row", [P, B, 6, DM])
        gtmp = sb("gtmp", [P, B, 2, DM])
        ident = sb("ident", [P, P])
        identb = sb("identb", [P, P], BF16)
        incl = sb("incl", [P, 2, P])
        strict = sb("strict", [P, 2, P])
        negm = sb("negm", [P, 2, 2, P], BF16)
        ones = sb("ones", [P, P])
        w1s = sb("w1s", [P, NE, FF])
        w2s = sb("w2s", [P, NE, FC, DM])
        b2s = sb("b2s", [P, NE, DM])
        padrow = sb("padrow", [P, ROW])
        pcol = sb("pcol", [P, 1])

        xs = sb("xs", [P, B * TPB, DM])
        ids = sb("ids", [P, B * TPB])
        count = sb("count", [P, NE])
        base = sb("base", [P, NE])
        region0 = sb("region0", [P, NE])

        ARENA = sb("arena", [P, 2 * TPB * DI + NG * (L + 2 * HALO)])
        yz = ARENA[:, 0:2 * TPB * DI].rearrange("p (d t c) -> p d t c", d=2, t=TPB)
        raw = ARENA[:, 2 * TPB * DI:].rearrange("p (g c) -> p g c", g=NG)
        zs = sb("zs", [P, TPB, DI])
        stat = sb("stat", [P, TPB, 6])
        mv = sb("mv", [P, TPB, 2])
        ve = sb("ve", [P, TPB])
        rstd = sb("rstd", [P, TPB])
        mhalf = sb("mhalf", [P, 2 * TPB])
        dtr = sb("dtr", [P, TPB, NDT])
        NQ = 2 * NH * TPB
        sp = sb("sp", [P, 8, NQ])
        biasb = sb("biasb", [P, 2 * NH, TPB])
        ab = sb("ab", [P, 2 * NH, TPB])
        dtv = sb("dtv", [P, NQ])
        av = sb("av", [P, NQ])
        etab = sb("etab", [P, 3, NQ])
        wB = sb("wB", [P, NQ])
        ssq = sb("ssq", [P, 2, TPB])
        rn = sb("rn", [P, 2, TPB])
        rt = sb("rt", [P, 2, TPB])

        xn = sb("xn", [P, 4, DM])
        hT = sb("hT", [P, 2, BLK])
        acc = sb("acc", [P, NG, BLK])
        cx = sb("cx", [P, 2, NH, BLK])
        bT = sb("bT", [NS, 2, BLK])
        cT = sb("cT", [NS, 2, BLK])
        lseg = sb("lseg", [P, 2, NH, P])
        xt = sb("xt", [P, 2, DI])
        bs = sb("bs", [P, 2, NH, NS])
        es = sb("es", [P, 2, NH, P])
        ms = sb("ms", [P, 2, NH, P])
        st = sb("st", [NS, 2, DI])
        us = sb("us", [P, 2, DI])
        ws = sb("ws", [P, 2, DI])
        vs = sb("vs", [P, 2, DI])
        junk = sb("junk", [P, DI])
        y1 = acc[:, 0, :].rearrange("p (a c) -> p a c", a=2)
        ysum = acc[:, 1, :].rearrange("p (a c) -> p a c", a=2)
        yT = acc[:, 2, :].rearrange("p (a c) -> p a c", a=2)
        o1 = sb("o1", [P, 2, DM])
        st2 = sb("st2", [P, 2, 6])
        mv2 = sb("mv2", [P, 2, 2])
        ve2 = sb("ve2", [P, 2, 1])
        rs2 = sb("rs2", [P, 2, 1])
        xn2 = sb("xn2", [P, 2, DM])
        rows = sb("rows", [P, 4, ROW])
        rowat = sb("rowat", [P, 4, 1], mybir.dt.int32)
        hot = sb("hot", [P, 2, NE])
        pos = sb("pos", [P, 2, NE])
        posf = sb("posf", [P, 2, 1])
        posj = sb("posj", [P, 2, NE])
        h2c = sb("h2c", [P, 2, P])
        lg = sb("lg", [P, 2, NE])
        mx = sb("mx", [P, 2, 2])
        rank8 = sb("rank8", [P, NE])
        cand = sb("cand", [P, 2, NE])

        s_load = sem("s_load")
        s_x = sem("s_x")
        s_wf = sem("s_wf")
        s_pool0 = sem("s_pool0")
        s_act0 = sem("s_act0")
        s_pe0 = sem("s_pe0")
        s_dve0 = sem("s_dve0")
        s_phase = sem("s_phase")
        s_st = sem("s_st")
        s_mv = sem("s_mv")
        s_ve = sem("s_ve")
        s_rstd = sem("s_rstd")
        s_xn = sem("s_xn")
        s_xT = sem("s_xT")
        s_hT = sem("s_hT")
        s_rawmm = sem("s_rawmm")
        s_raw = sem("s_raw")
        s_zmm = sem("s_zmm")
        s_z = sem("s_z")
        s_dve = sem("s_dve")
        s_spe = sem("s_spe")
        s_a = sem("s_a")
        s_pfx = sem("s_pfx")
        s_etab = sem("s_etab")
        s_wB = sem("s_wB")
        s_tap0 = sem("s_tap0")
        s_tap = sem("s_tap")
        s_silu = sem("s_silu")
        s_L = sem("s_L")
        s_tx = sem("s_tx")
        s_sg = sem("s_sg")
        s_ys = sem("s_ys")
        s_yo = sem("s_yo")
        s_xt = sem("s_xt")
        s_e = sem("s_e")
        s_u = sem("s_u")
        s_m = sem("s_m")
        s_S = sem("s_S")
        s_v = sem("s_v")
        s_yz = sem("s_yz")
        s_sq = sem("s_sq")
        s_w = sem("s_w")
        s_wu = sem("s_wu")
        s_rt = sem("s_rt")
        s_rn = sem("s_rn")
        s_y1 = sem("s_y1")
        s_ysum = sem("s_ysum")
        s_yTm = sem("s_yTm")
        s_yT = sem("s_yT")
        s_o = sem("s_o")
        s_o1 = sem("s_o1")
        s_st2 = sem("s_st2")
        s_mv2 = sem("s_mv2")
        s_ve2 = sem("s_ve2")
        s_rs2 = sem("s_rs2")
        s_xn2 = sem("s_xn2")
        s_h2a = sem("s_h2a")
        s_h2 = sem("s_h2")
        s_h2m = sem("s_h2m")
        s_h2c = sem("s_h2c")
        s_lgm = sem("s_lgm")
        s_rt_dve = sem("s_rt_dve")
        s_hot = sem("s_hot")
        s_rank = sem("s_rank")
        s_pos = sem("s_pos")
        s_x1r = sem("s_x1r")
        s_id = sem("s_id")
        s_scat = [sem(f"s_scat{i}") for i in range(4)]
        s_tab = sem("s_tab")
        s_tabv = sem("s_tabv")
        s_padi = sem("s_padi")
        s_pad = sem("s_pad")
        s_rb = [sem(f"s_rb{i}") for i in range(4)]
        s_eT = sem("s_eT")
        s_eTc = sem("s_eTc")
        s_h1 = sem("s_h1")
        s_hb = sem("s_hb")
        s_hx = sem("s_hx")
        s_hr = sem("s_hr")
        s_y2 = sem("s_y2")
        s_flag = sem("s_flag")
        s_gs = sem("s_gs")
        s_tok = sem("s_tok")
        s_gd = sem("s_gd")
        s_yo1 = sem("s_yo1")
        s_yo2 = sem("s_yo2")
        s_ob = sem("s_ob")
        s_out = [sem(f"s_out{i}") for i in range(4)]

        b1s = zs[:, :, :].rearrange("p t c -> p (t c)").rearrange("p (e f) -> p e f", e=NE)
        at = [0]

        def over(n):
            at[0] += n
            return ARENA[:, at[0] - n:at[0]]

        NM = NTOK // P
        tiles_gt = over(NE * NM).rearrange("p (e m) -> p e m", e=NE)
        m128 = over(NM)
        ntile = over(NE)
        cum = over(NE)
        coef = over(NE)
        slot_i = over(NSLOT)
        behind = over(2 * NE * NSLOT).rearrange("p (k e s) -> p k e s", k=2, e=NE)
        slot_v = over(2 * NSLOT).rearrange("p (k s) -> p k s", k=2)
        slot_r = over(2 * NSLOT).bitcast(mybir.dt.int32).rearrange("p (k s) -> p k s", k=2)
        padf = over(NE)
        padi = over(NE).bitcast(mybir.dt.int32)
        rh = over(4 * DM).rearrange("p (a c) -> p a c", a=4)
        XR = ROW - DM
        xr = over(NSLOT * XR).rearrange("p (s c) -> p s c", s=NSLOT)
        gdiff = over(DM)
        hTs = over(2 * P).rearrange("p (a c) -> p a c", a=2)
        hb = over(2 * FF).rearrange("p (a c) -> p a c", a=2)
        hr = over(2 * FF).rearrange("p (a c) -> p a c", a=2)
        flag = over(2).rearrange("p (a c) -> p a c", a=2)
        gsel = over(2 * DM).rearrange("p (a c) -> p a c", a=2)
        tok = over(4).bitcast(mybir.dt.int32).rearrange("p (a c) -> p a c", a=4)
        yo1 = over(2 * DM).rearrange("p (a c) -> p a c", a=2)
        yo2 = over(2 * DM).rearrange("p (a c) -> p a c", a=2)
        ob = over(4 * DM).rearrange("p (a c) -> p a c", a=4)

        routed = nc.dram_tensor("routed_rows", (NE * REGION + P, ROW), F32, kind="Internal").ap()
        N_POOL0 = 11 + 2 * (2 + 2 * NH) + 2 + 2 * 2 * NH
        N_DVE0 = 15

        s_held = sem("s_held")

        def hold(eng, signal, value):
            eng.wait_ge(signal, value)
            eng.sem_inc(s_held, 1)

        def phase_end(eng, b, n):
            eng.sem_inc(s_held, 1)
            eng.drain().then_inc(s_phase, 1)
            hold(eng, s_phase, b * 12 + 4 * (n + 1))

        def col(d, h, t):
            c = (d * NH + h) * TPB + t
            return slice(c, c + 1)

        out_rows = out.rearrange("b t d -> (b t) d")
        NR = 9

        block = ctx.enter_context(nc.Block())

        @block.sync
        def _(sp_):
            n = 0
            u_rows = u.rearrange("b (t p) d -> p (b t) d", p=P)
            for i in range(2 * B):
                h = TPB // 2
                sp_.dma_start(xs[:, i * h:(i + 1) * h, :], u_rows[:, i * h:(i + 1) * h, :]).then_inc(s_x, 16)
            for dst, src in (
                (wx[:, :], w_xbc), (wz[:, :], w_zdt), (cw[:, :, :, :], conv_w), (cb[:, :, :], conv_b),
                (dtb[:, :], dt_bias.partition_broadcast(P)), (alog[:, :], a_log.partition_broadcast(P)),
                (dsk[:, :], d_skip.partition_broadcast(P)),
                (nw[:, :], norm_w), (wo[:, :, :], w_out), (gw[:, :], gate_w),
                (gbias[:, :, :], gate_b.partition_broadcast(P)),
                (ct_in[:, :], c_t), (wm[:, :], wmod),
            ):
                sp_.dma_start(dst, src).then_inc(s_load, 16)
                n += 1
            assert n == 13
            for dst, src in ((w1s[:, :, :], w1), (w2s[:, :, :, :], w2), (b2s[:, :, :], b2.partition_broadcast(P))):
                sp_.dma_start(dst, src).then_inc(s_wf, 16)
            sp_.wait_ge(s_phase, 12 * (B - 1) + 8)
            sp_.dma_start(b1s, b1.partition_broadcast(P)).then_inc(s_wf, 16)

            sp_.wait_ge(s_phase, 12 * B)
            for i in range(4):
                sp_.wait_ge(s_scat[i], 16 * B * TPB // 4)
            sp_.wait_ge(s_pad, 16 * (NE + 1))
            sp_.wait_ge(s_tabv, 1)

            def load_rows(s, k):
                first = sp_.value_load(slot_r[0:1, 0, bass.ds(s, 1)], min_val=0, max_val=NE * REGION)
                sp_.dma_start(rh[:, k, :], routed[bass.ds(first, P), 0:DM]).then_inc(s_rb[k], 16)
                sp_.dma_start(xr[:, bass.ds(s, 1), :].rearrange("p a c -> p (a c)"),
                              routed[bass.ds(first, P), DM:ROW]).then_inc(s_rb[k], 16)

            for s in range(4):
                load_rows(s, s)
            with sp_.Fori(1, NSLOT // 4) as it:
                for k in range(4):
                    sp_.wait_ge(s_eT, 4 * it + k - 3)
                    load_rows(4 * it + k, k)
            for s in range(NSLOT // 4 * 4, NSLOT):
                sp_.wait_ge(s_eT, s - 3)
                load_rows(s, s % 4)

        NLOAD = 13 * 16

        @block.gpsimd
        def _(pool):
            n = [0]

            def link(ins):
                n[0] += 1
                ins.then_inc(s_pool0, 1)
                hold(pool, s_pool0, n[0])

            link(pool.memset(ident[:, :], 0.0))
            link(pool.affine_select(out=ident[:, :], in_=ident[:, :], compare_op=ALU.not_equal, fill=1.0, base=0,
                                    pattern=[[-1, P]], channel_multiplier=1))
            link(pool.tensor_copy(identb[:, :], ident[:, :]))
            link(pool.memset(ones[:, :], 1.0))
            for d in range(2):
                sgn = 1 - 2 * d
                link(pool.affine_select(out=incl[:, d, :], in_=ones[:, :], compare_op=ALU.is_ge, fill=0.0, base=0,
                                        pattern=[[sgn, P]], channel_multiplier=-sgn))
                link(pool.affine_select(out=strict[:, d, :], in_=ones[:, :], compare_op=ALU.is_gt, fill=0.0, base=0,
                                        pattern=[[-sgn, P]], channel_multiplier=sgn))
                for h in range(NH):
                    link(pool.memset(negm[:, d, h, :], 0.0))
                    link(pool.affine_select(out=negm[:, d, h, :], in_=negm[:, d, h, :], compare_op=ALU.is_ge,
                                            fill=MASKED, base=0, pattern=[[sgn, P]], channel_multiplier=-sgn))
            link(pool.memset(mhalf[:, :], -0.5))
            link(pool.iota(rank8[:, :], pattern=[[-1, NE]], base=NE, channel_multiplier=0,
                           allow_small_or_imprecise_dtypes=True))
            link(pool.iota(ids[:, :], pattern=[[P, B * TPB]], base=0, channel_multiplier=1,
                           allow_small_or_imprecise_dtypes=True))
            link(pool.iota(pcol[:, :], pattern=[[0, 1]], base=0, channel_multiplier=1,
                           allow_small_or_imprecise_dtypes=True))
            link(pool.iota(region0[:, :], pattern=[[REGION, NE]], base=0, channel_multiplier=0,
                           allow_small_or_imprecise_dtypes=True))
            link(pool.memset(count[:, :], 0.0))
            link(pool.memset(padrow[:, :], 0.0))
            link(pool.memset(padrow[:, 2 * DM:2 * DM + 1], float(NTOK)))
            link(pool.memset(rows[:, :, 2 * DM:], 0.0))
            hold(pool, s_load, NLOAD)
            for k in range(2 * NH):
                link(pool.memset(biasb[:, k, :], 0.0))
                link(pool.tensor_scalar(biasb[:, k, :], biasb[:, k, :], dtb[:, k:k + 1], 1.0, ALU.add, ALU.mult))
            assert n[0] == N_POOL0
            hold(pool, s_dve0, N_DVE0)

            with pool.Fori(0, B) as b:
                hold(pool, s_mv, b * TPB + TPB)
                pool.tensor_scalar(ve[:, :], mv[:, :, 1], EPS, 1.0, ALU.add, ALU.mult).then_inc(s_ve, 1)
                hold(pool, s_ve, b + 1)
                pool.tensor_tensor(rstd[:, :], ve[:, :], mhalf[:, 0:TPB], ALU.pow).then_inc(s_rstd, 1)
                phase_end(pool, b, 0)

                def decay_rows(q):
                    d, t = chunk_of(q)
                    if q >= 2:
                        hold(pool, s_sg, b * CHUNKS + q - 1)
                    for h in range(NH):
                        last = pool.tensor_scalar(lseg[:, q % 2, h, :], strict[:, d, :],
                                                  av[:, col(d, h, t)], 1.0, ALU.mult, ALU.mult)
                    last.then_inc(s_L, 1)

                decay_rows(0)
                decay_rows(1)
                for q in range(CHUNKS):
                    d, t = chunk_of(q)
                    if q + 2 < CHUNKS:
                        decay_rows(q + 2)
                    hold(pool, s_xt, b * CHUNKS + q + 1)
                    if q >= 2:
                        hold(pool, s_v, b * CHUNKS + q - 1)
                    for h in range(NH):
                        last = pool.tensor_scalar(ws[:, q % 2, h * HD:(h + 1) * HD], xt[:, q % 2, h * HD:(h + 1) * HD],
                                                  dsk[:, d * NH + h:d * NH + h + 1], 1.0, ALU.mult, ALU.mult)
                    last.then_inc(s_w, 1)
                    hold(pool, s_w, b * CHUNKS + q + 1)
                    hold(pool, s_u, b * CHUNKS + q + 1)
                    pool.tensor_tensor(ws[:, q % 2, :], ws[:, q % 2, :], us[:, q % 2, :], ALU.add).then_inc(s_wu, 1)
                phase_end(pool, b, 1)

                pool.tensor_scalar(rt[:, :, :], ssq[:, :, :], 1.0 / DI, EPS, ALU.mult, ALU.add).then_inc(s_rt, 1)
                hold(pool, s_rt, b + 1)
                pool.tensor_tensor(rn[:, :, :], rt[:, :, :], mhalf[:, :].rearrange("p (d t) -> p d t", d=2),
                                   ALU.pow).then_inc(s_rn, 1)

                def scatter(t, m):
                    k = t % 4
                    hold(pool, s_pos, m + 1)
                    hold(pool, s_x1r, m + 1)
                    hold(pool, s_h2, m + 1)
                    hold(pool, s_id, m + 1)
                    pool.indirect_dma_start(routed[:, :], bass.IndirectOffsetOnAxis(ap=rowat[:, k, :].bitcast(mybir.dt.uint32), axis=0),
                                            rows[:, k, :], None).then_inc(s_scat[k], 16)

                for t in range(TPB):
                    m = b * TPB + t
                    a = t % 2
                    hold(pool, s_mv2, m + 1)
                    pool.tensor_scalar(ve2[:, a, :], mv2[:, a, 1:2], EPS, 1.0, ALU.add, ALU.mult).then_inc(s_ve2, 1)
                    hold(pool, s_ve2, m + 1)
                    pool.tensor_tensor(rs2[:, a, :], ve2[:, a, :], mhalf[:, 0:1], ALU.pow).then_inc(s_rs2, 1)
                    k = t % 4
                    hold(pool, s_xn2, m + 1)
                    if t >= 4:
                        hold(pool, s_scat[k], b * 64 + 16 * (t // 4))
                    pool.tensor_tensor(rows[:, k, 0:DM], xn2[:, a, :], row[:, b, 4, :], ALU.mult).then_inc(s_h2a, 1)
                    hold(pool, s_h2a, m + 1)
                    pool.tensor_tensor(rows[:, k, 0:DM], rows[:, k, 0:DM], row[:, b, 3, :], ALU.add).then_inc(s_h2, 1)
                    pool.tensor_copy(rows[:, k, 2 * DM:2 * DM + 1], ids[:, bass.ds(m, 1)]).then_inc(s_id, 1)
                    if t >= 1:
                        scatter(t - 1, m - 1)
                scatter(TPB - 1, b * TPB + TPB - 1)
                phase_end(pool, b, 2)

            pool.dma_start(routed[NE * REGION:NE * REGION + P, :], padrow[:, :]).then_inc(s_pad, 16)
            pool.iota(m128, pattern=[[P, NM]], base=0, channel_multiplier=0,
                      allow_small_or_imprecise_dtypes=True).then_inc(s_tab, 1)
            pool.iota(slot_i, pattern=[[1, NSLOT]], base=0, channel_multiplier=0,
                      allow_small_or_imprecise_dtypes=True).then_inc(s_tab, 1)
            hold(pool, s_padi, 1)
            for e in range(NE):
                pool.indirect_dma_start(routed[:, :], bass.IndirectOffsetOnAxis(ap=padi[:, e:e + 1].bitcast(mybir.dt.uint32), axis=0),
                                        padrow[:, :], None).then_inc(s_pad, 16)

            def token_numbers(s, k, rk, free16):
                hold(pool, s_rb[k], rk)
                if free16 is not None:
                    hold(pool, s_out[k], free16)
                pool.tensor_copy(tok[:, k, :], xr[:, bass.ds(s, 1), DM:DM + 1].rearrange("p a c -> p (a c)")).then_inc(s_tok, 1)

            def put(s, k):
                hold(pool, s_ob, s + 1)
                hold(pool, s_tok, s + 1)
                pool.indirect_dma_start(out_rows, bass.IndirectOffsetOnAxis(ap=tok[:, k, :].bitcast(mybir.dt.uint32), axis=0),
                                        ob[:, k, :], None, bounds_check=NTOK - 1, oob_is_err=False).then_inc(s_out[k], 16)

            for s in range(4):
                token_numbers(s, s, 32, None)
                if s >= 1:
                    put(s - 1, s - 1)
            with pool.Fori(1, NSLOT // 4) as it:
                for k in range(4):
                    token_numbers(4 * it + k, k, 32 * it + 32, 16 * it)
                    put(4 * it + k - 1, (k + 3) % 4)
            for s in range(NSLOT // 4 * 4, NSLOT):
                token_numbers(s, s % 4, 32 * (s // 4) + 32, 16 * (s // 4))
                put(s - 1, (s - 1) % 4)
            put(NSLOT - 1, (NSLOT - 1) % 4)
            for k in range(4):
                hold(pool, s_out[k], 16 * ((NSLOT - k + 3) // 4))

        @block.scalar
        def _(act):
            act.wait_ge(s_load, NLOAD)
            act.activation(csil[:, :], ct_in[:, :], ACT.Silu).then_inc(s_act0, 1)
            act.activation(ab[:, :, 0], alog[:, :], ACT.Exp).then_inc(s_act0, 1)
            act.wait_ge(s_dve0, N_DVE0)

            with act.Fori(0, B) as b:
                def modulate(i):
                    hold(act, s_xT, b * TPB + 4 * i + 4)
                    if i >= 2:
                        hold(act, s_zmm, b * TPB + 4 * (i - 1))
                    act.activation(hT[:, i % 2, :], bank[i % 2][:, :], ACT.Identity,
                                   bias=modc[:, 0, bass.ds(b, 1)], scale=modc[:, 1, bass.ds(b, 1)]).then_inc(s_hT, 1)

                modulate(0)
                for i in range(NBLK):
                    if i + 1 < NBLK:
                        modulate(i + 1)
                    for j in range(BT):
                        n, t = BT * i + j, BT * (NBLK - 1 - i) + j
                        pz = bank[5 + n % 3]
                        act.wait_ge(s_zmm, b * TPB + n + 1)
                        act.activation(zs[:, t, :], pz[:, 0:DI], ACT.Silu)
                        act.activation(dtr[:, t, :], pz[:, DI:ZW], ACT.Identity).then_inc(s_z, 1)
                act.wait_ge(s_spe, b * 4 + 1)
                act.activation(sp[:, 2, :], sp[:, 1, :], ACT.Exp, scale=-1.0).then_inc(s_spe, 1)
                act.wait_ge(s_spe, b * 4 + 3)
                act.activation(sp[:, 4, :], sp[:, 3, :], ACT.Ln).then_inc(s_spe, 1)
                act.wait_ge(s_pfx, b + 1)
                act.activation(etab[:, :, :], bank[5][:, 0:3 * NQ].rearrange("p (k c) -> p k c", k=3),
                               ACT.Exp).then_inc(s_etab, 1)
                phase_end(act, b, 0)

                def tap0(s):
                    d, k = step_of(s)
                    if s >= 1:
                        act.wait_ge(s_silu, b * STEPS + s)
                    for g in range(NG):
                        act.activation(acc[:, g, :], raw[:, g, HALO + k * BLK:HALO + (k + 1) * BLK], ACT.Identity,
                                       bias=cb[:, d, g:g + 1], scale=cw[:, d, g, KC - 1:KC]).then_inc(s_tap0, 1)

                def silu(s):
                    act.wait_ge(s_tap, b * STEPS * 9 + 9 * (s + 1))
                    if s >= 2:
                        act.wait_ge(s_tx, b * CHUNKS + BT * (s - 1))
                        act.wait_ge(s_yo, b * CHUNKS + BT * (s - 1))
                    for g in range(NH):
                        act.activation(cx[:, s % 2, g, :], acc[:, g, :], ACT.Silu)
                    act.activation(bT[:, s % 2, :], acc[0:NS, NH, :], ACT.Silu)
                    act.activation(cT[:, s % 2, :], acc[NS:2 * NS, NH, :], ACT.Silu).then_inc(s_silu, 1)

                def tokens_major(q):
                    d, t = chunk_of(q)
                    tx = bank[q % 2]
                    act.wait_ge(s_tx, b * CHUNKS + q + 1)
                    if q >= 2:
                        act.wait_ge(s_ys, b * CHUNKS + q - 1)
                        act.wait_ge(s_w, b * CHUNKS + q - 1)
                    act.activation(xt[:, q % 2, :], tx[:, 0:DI], ACT.Copy)
                    for h in range(NH):
                        last = act.activation(bs[:, q % 2, h, :], tx[:, DI:DI + NS], ACT.Copy, scale=wB[:, col(d, h, t)])
                    last.then_inc(s_xt, 1)

                def decays(q):
                    act.wait_ge(s_sg, b * CHUNKS + q + 1)
                    if q >= 2:
                        act.wait_ge(s_m, b * CHUNKS + q - 1)
                    act.activation(es[:, q % 2, :, :], bank[2 + q % 2][:, 0:DI].rearrange("p (h i) -> p h i", h=NH),
                                   ACT.Exp).then_inc(s_e, 1)

                def carried(q):
                    d, t = chunk_of(q)
                    act.wait_ge(s_yo, b * CHUNKS + q + 1)
                    if q >= 2:
                        act.wait_ge(s_wu, b * CHUNKS + q - 1)
                    for h in range(NH):
                        last = act.activation(us[:, q % 2, h * HD:(h + 1) * HD],
                                              bank[6 + q % 2][:, h * HD:(h + 1) * HD], ACT.Copy,
                                              scale=etab[:, 0, col(d, h, t)])
                    last.then_inc(s_u, 1)

                def squares(q):
                    d, t = chunk_of(q)
                    act.wait_ge(s_yz, b * CHUNKS + q + 1)
                    if q >= 1:
                        act.wait_ge(s_sq, b * CHUNKS + q)
                    act.activation(junk[:, :], yz[:, d, t, :], ACT.Square,
                                   accum_out=ssq[:, d, t:t + 1]).then_inc(s_sq, 1)

                tap0(0)
                silu(0)
                tap0(1)
                tokens_major(0)
                decays(0)
                for q in range(CHUNKS):
                    s, j = q // BT, q % BT
                    if q + 1 < CHUNKS:
                        tokens_major(q + 1)
                        decays(q + 1)
                    if q >= 2:
                        squares(q - 2)
                    carried(q)
                    if j == 2 and s + 1 < STEPS:
                        silu(s + 1)
                        if s + 2 < STEPS:
                            tap0(s + 2)
                squares(CHUNKS - 2)
                squares(CHUNKS - 1)
                phase_end(act, b, 1)

                for t in range(TPB):
                    m, a = b * TPB + t, t % 2

                    def out_T(t, m):
                        act.wait_ge(s_yTm, m + 1)
                        if t >= 2:
                            act.wait_ge(s_o, m - 1)
                        act.activation(yT[:, t % 2, :], bank[t % 2][:, 0:DI], ACT.Copy).then_inc(s_yT, 1)

                    if t == 0:
                        out_T(0, m)
                    if t + 1 < TPB:
                        out_T(t + 1, m + 1)
                    act.wait_ge(s_h2m, m + 1)
                    if t >= 2:
                        act.wait_ge(s_lgm, m - 1)
                    act.activation(h2c[:, a, :], bank[4 + a][:, 0:P], ACT.Copy).then_inc(s_h2c, 1)
                phase_end(act, b, 2)

            def rows_T(s, a, first):
                act.wait_ge(s_eT, s + 1)
                if not first:
                    act.wait_ge(s_h1, s - 1)
                act.activation(hTs[:, a, :], bank[a][:, 0:P], ACT.Copy).then_inc(s_eTc, 1)

            def rectify(s, a, first):
                act.wait_ge(s_hx, s + 1)
                if not first:
                    act.wait_ge(s_y2, s - 1)
                act.activation(hr[:, a, :], bank[4 + a][:, :], ACT.Relu).then_inc(s_hr, 1)

            rows_T(0, 0, True)
            rows_T(1, 1, True)
            for s in range(2):
                rows_T(s + 2, s % 2, False)
                rectify(s, s % 2, True)
            with act.Fori(1, (NSLOT - 2) // 2) as it:
                for a in range(2):
                    rows_T(2 * it + a + 2, a, False)
                    rectify(2 * it + a, a, False)
            for s in range((NSLOT - 2) // 2 * 2, NSLOT):
                if s + 2 < NSLOT:
                    rows_T(s + 2, s % 2, False)
                rectify(s, s % 2, False)

        @block.tensor
        def _(pe):
            pe.wait_ge(s_pool0, N_POOL0)
            pe.wait_ge(s_dve0, 1)
            for m in range(2):
                pe.matmul(bank[0][:, m * B:(m + 1) * B], wm[:, m * DM:(m + 1) * DM], csil[:, :], start=True, stop=True)
            for b in range(B):
                pe.matmul(bank[1 + 2 * b][:, 0:3 * DM], csil_bc[:, b, :], wm[:, 0:3 * DM], start=True, stop=True)
                last = pe.matmul(bank[2 + 2 * b][:, 0:3 * DM], csil_bc[:, b, :], wm[:, 3 * DM:6 * DM],
                                 start=True, stop=True)
            last.then_inc(s_pe0, 1)
            pe.wait_ge(s_dve0, N_DVE0)

            with pe.Fori(0, B) as b:
                def turn(i):
                    for j in range(BT):
                        n = BT * i + j
                        pe.wait_ge(s_xn, b * TPB + n + 1)
                        if i >= 2 and j == 0:
                            pe.wait_ge(s_hT, b * NBLK + i - 1)
                        pe.transpose(bank[i % 2][:, j * P:(j + 1) * P], xn[:, n % 4, :], ident[:, :]).then_inc(s_xT, 1)

                turn(0)
                for i in range(NBLK):
                    if i + 1 < NBLK:
                        turn(i + 1)
                    pe.wait_ge(s_hT, b * NBLK + i + 1)
                    for g in range(NG):
                        if i >= 1:
                            pe.wait_ge(s_raw, b * NBLK * NG + NG * (i - 1) + g + 1)
                        pe.matmul(bank[2 + g][:, :], wx[:, g * P:(g + 1) * P], hT[:, i % 2, :],
                                  start=True, stop=True).then_inc(s_rawmm, 1)
                    for j in range(BT):
                        n = BT * i + j
                        if n >= 3:
                            pe.wait_ge(s_z, b * TPB + n - 2)
                        pe.matmul(bank[5 + n % 3][:, 0:ZW], hT[:, i % 2, j * P:(j + 1) * P], wz[:, :],
                                  start=True, stop=True).then_inc(s_zmm, 1)
                pe.wait_ge(s_a, b + 1)
                W = NH * TPB
                for d in range(2):
                    for k, m in enumerate((incl[:, d, :], strict[:, d, :], ones[:, :])):
                        last = pe.matmul(bank[5][:, k * NQ + d * W:k * NQ + (d + 1) * W], m, av[:, d * W:(d + 1) * W],
                                         start=True, stop=True)
                last.then_inc(s_pfx, 1)
                phase_end(pe, b, 0)

                def prepare(q):
                    d, t = chunk_of(q)
                    s, j = q // BT, q % BT
                    c0 = (t % BT) * P
                    tx, sg = bank[q % 2], bank[2 + q % 2]
                    if j == 0:
                        pe.wait_ge(s_silu, b * STEPS + s + 1)
                    if q >= 2:
                        pe.wait_ge(s_xt, b * CHUNKS + q - 1)
                    for h in range(NH):
                        pe.transpose(tx[:, h * HD:(h + 1) * HD], cx[:, s % 2, h, c0:c0 + P], ident[:, :])
                    pe.transpose(tx[:, DI:DI + NS], bT[:, s % 2, c0:c0 + P], ident[0:NS, 0:NS]).then_inc(s_tx, 1)
                    if q >= 2:
                        pe.wait_ge(s_m, b * CHUNKS + q - 1)
                    pe.matmul(sg[:, DI:DI + P], bT[:, s % 2, c0:c0 + P], cT[:, s % 2, c0:c0 + P],
                              start=True, stop=True)
                    pe.matmul(sg[:, 0:DI], identb[:, :], negm[:, d, :, :].rearrange("p h i -> p (h i)"),
                              start=True, stop=False, skip_group_check=True)
                    pe.wait_ge(s_L, b * CHUNKS + q + 1)
                    for h in range(NH):
                        last = pe.matmul(sg[:, h * P:(h + 1) * P], lseg[:, q % 2, h, :], incl[:, d, :],
                                         start=False, stop=True, skip_group_check=True)
                    last.then_inc(s_sg, 1)

                def scan(q):
                    d, t = chunk_of(q)
                    s = q // BT
                    c0 = (t % BT) * P
                    ys, yo = bank[4 + q % 2], bank[6 + q % 2]
                    pe.wait_ge(s_xt, b * CHUNKS + q + 1)
                    pe.wait_ge(s_m, b * CHUNKS + q + 1)
                    if q >= 2:
                        pe.wait_ge(s_v, b * CHUNKS + q - 1)
                    for h in range(NH):
                        last = pe.matmul(ys[:, h * HD:(h + 1) * HD], ms[:, q % 2, h, :], xt[:, q % 2, h * HD:(h + 1) * HD],
                                         start=True, stop=True)
                    if q % TPB != TPB - 1:
                        for h in range(NH):
                            last = pe.matmul(ys[0:NS, DI + h * HD:DI + (h + 1) * HD], bs[:, q % 2, h, :],
                                             xt[:, q % 2, h * HD:(h + 1) * HD], start=True, stop=True)
                    last.then_inc(s_ys, 1)
                    if q >= 2:
                        pe.wait_ge(s_u, b * CHUNKS + q - 1)
                    if q >= 1:
                        pe.wait_ge(s_S, b * CHUNKS + q)
                    pe.matmul(yo[:, 0:DI], cT[:, s % 2, c0:c0 + P], st[:, q % 2, :], start=True,
                              stop=True).then_inc(s_yo, 1)

                prepare(0)
                for q in range(CHUNKS):
                    if q + 1 < CHUNKS:
                        prepare(q + 1)
                    scan(q)
                phase_end(pe, b, 1)

                def y_turn(t, m):
                    pe.wait_ge(s_ysum, m + 1)
                    if t >= 2:
                        pe.wait_ge(s_yT, m - 1)
                    for h in range(NH):
                        last = pe.transpose(bank[t % 2][:, h * P:(h + 1) * P], ysum[:, t % 2, h * P:(h + 1) * P],
                                            ident[:, :])
                    last.then_inc(s_yTm, 1)

                def project(t, m):
                    pe.wait_ge(s_yT, m + 1)
                    if t >= 2:
                        pe.wait_ge(s_o1, m - 1)
                    for h in range(NH):
                        last = pe.matmul(bank[2 + t % 2][:, 0:DM], yT[:, t % 2, h * P:(h + 1) * P], won[:, h, :],
                                         start=(h == 0), stop=(h == NH - 1))
                    last.then_inc(s_o, 1)

                def ranks(t, m):
                    pe.wait_ge(s_hot, m + 1)
                    bk = bank[6 + t % 2]
                    pe.matmul(bk[:, NE:2 * NE], strict[:, 1, :], hot[:, t % 2, :], start=True, stop=True)
                    pe.matmul(bk[:, 2 * NE:3 * NE], ones[:, :], hot[:, t % 2, :], start=True,
                              stop=True).then_inc(s_rank, 1)

                y_turn(0, b * TPB)
                project(0, b * TPB)
                for t in range(TPB):
                    m, a = b * TPB + t, t % 2
                    if t + 1 < TPB:
                        y_turn(t + 1, m + 1)
                        project(t + 1, m + 1)
                    if t >= 1:
                        ranks(t - 1, m - 1)
                    pe.wait_ge(s_h2, m + 1)
                    if t >= 2:
                        pe.wait_ge(s_h2c, m - 1)
                    pe.transpose(bank[4 + a][:, 0:P], rows[:, t % 4, 0:DM], ident[:, :]).then_inc(s_h2m, 1)
                    pe.wait_ge(s_h2c, m + 1)
                    if t >= 2:
                        pe.wait_ge(s_rt_dve, NR * (m - 1))
                    pe.matmul(bank[6 + a][:, 0:NE], h2c[:, a, :], gw[:, :], start=True, stop=True).then_inc(s_lgm, 1)
                ranks(TPB - 1, b * TPB + TPB - 1)
                phase_end(pe, b, 2)

            pe.wait_ge(s_wf, 64)
            pe.wait_ge(s_tabv, 1)

            def turn_rows(s, a, k, rk, first):
                pe.wait_ge(s_rb[k], rk)
                if not first:
                    pe.wait_ge(s_eTc, s - 1)
                pe.transpose(bank[a][:, 0:P], rh[:, k, :], ident[:, :]).then_inc(s_eT, 1)

            def hidden(s, a, first):
                e = pe.value_load(slot_r[0:1, 1, bass.ds(s, 1)], min_val=0, max_val=NE - 1)
                pe.wait_ge(s_eTc, s + 1)
                if not first:
                    pe.wait_ge(s_hb, s - 1)
                pe.matmul(bank[2 + a][:, :], hTs[:, a, :], w1s[:, bass.ds(e, 1), :].rearrange("p a f -> p (a f)"),
                          start=True, stop=True).then_inc(s_h1, 1)

            def turn_hidden(s, a, first):
                pe.wait_ge(s_hb, s + 1)
                if not first:
                    pe.wait_ge(s_hr, s - 1)
                for f in range(FC):
                    last = pe.transpose(bank[4 + a][:, f * P:(f + 1) * P], hb[:, a, f * P:(f + 1) * P], ident[:, :])
                last.then_inc(s_hx, 1)

            def down(s, a, first):
                e = pe.value_load(slot_r[0:1, 1, bass.ds(s, 1)], min_val=0, max_val=NE - 1)
                pe.wait_ge(s_hr, s + 1)
                if not first:
                    pe.wait_ge(s_yo1, s - 1)
                for f in range(FC):
                    last = pe.matmul(bank[6 + a][:, 0:DM], hr[:, a, f * P:(f + 1) * P],
                                     w2s[:, bass.ds(e, 1), f, :].rearrange("p a c -> p (a c)"),
                                     start=(f == 0), stop=(f == FC - 1))
                last.then_inc(s_y2, 1)

            def pe_step(r, k, it):
                if it is None:
                    if r + 2 < NSLOT:
                        turn_rows(r + 2, r % 2, (r + 2) % 4, 32 * ((r + 2) // 4) + 32, r < 0)
                    if 0 <= r + 1 < NSLOT:
                        hidden(r + 1, (r + 1) % 2, r + 1 < 2)
                    if 0 <= r < NSLOT:
                        turn_hidden(r, r % 2, r < 2)
                    if r >= 1:
                        down(r - 1, (r - 1) % 2, r - 1 < 2)
                else:
                    turn_rows(r + 2, k % 2, (k + 2) % 4, 32 * it + 32 * ((k + 2) // 4) + 32, False)
                    hidden(r + 1, (k + 1) % 2, False)
                    turn_hidden(r, k % 2, False)
                    down(r - 1, (k + 1) % 2, False)

            for r in range(-2, 4):
                pe_step(r, 0, None)
            with pe.Fori(1, (NSLOT - 2) // 4) as it:
                for k in range(4):
                    pe_step(4 * it + k, k, it)
            for r in range((NSLOT - 2) // 4 * 4, NSLOT + 1):
                pe_step(r, 0, None)

        @block.vector
        def _(dve):
            dve.wait_ge(s_act0, 2)
            dve.wait_ge(s_load, NLOAD)
            dve.wait_ge(s_pool0, N_POOL0)
            n0 = [0]

            def link0(ins):
                n0[0] += 1
                ins.then_inc(s_dve0, 1)
                dve.wait_ge(s_dve0, n0[0])

            for b in range(B):
                last = dve.tensor_scalar(csil_bc[:, b, :], ones[:, :], csil[:, b:b + 1], None, ALU.mult)
            link0(last)
            for h in range(NH):
                dve.tensor_scalar(won[:, h, :], wo[:, h, :], nw[:, h:h + 1], None, ALU.mult)
            dve.tensor_tensor(gb_sum[:, :], gbias[:, 0, :], gbias[:, 1, :], ALU.add)
            link0(dve.tensor_scalar(sp[:, 0, 0:2 * NH], ab[:, :, 0], -1.0, None, ALU.mult))
            for k in range(2 * NH):
                last = dve.tensor_scalar(ab[:, k, :], ones[:, 0:TPB], sp[:, 0, k:k + 1], None, ALU.mult)
            for g in range(NG):
                dve.memset(raw[:, g, 0:HALO], 0.0)
                dve.memset(raw[:, g, HALO + L:HALO + L + HALO], 0.0)
            link0(dve.memset(st[:, 0, :], 0.0))
            dve.wait_ge(s_pe0, 1)
            dve.tensor_copy(modc[:, 0, :], bank[0][:, 0:B])
            link0(dve.tensor_scalar(modc[:, 1, :], bank[0][:, B:2 * B], 1.0, None, ALU.add))
            for b in range(B):
                dve.tensor_copy(row[:, b, 0:3, :], bank[1 + 2 * b][:, 0:3 * DM].rearrange("p (k c) -> p k c", k=3))
                last = dve.tensor_copy(row[:, b, 3:6, :], bank[2 + 2 * b][:, 0:3 * DM].rearrange("p (k c) -> p k c", k=3))
            link0(last)
            for b in range(B):
                last = dve.tensor_scalar(row[:, b, 4, :], row[:, b, 4, :], 1.0, None, ALU.add)
            link0(last)
            for b in range(B):
                g2 = row[:, b, 2:6:3, :]
                link0(dve.tensor_scalar(gtmp[:, b], g2, -1.0, None, ALU.mult))
                link0(dve.tensor_tensor(gtmp[:, b], gtmp[:, b], g2, ALU.max))
                link0(dve.tensor_scalar(gtmp[:, b], gtmp[:, b], 0.25, None, ALU.max))
                link0(dve.tensor_scalar(g2, g2, 0.0, 2.0, ALU.is_ge, ALU.mult))
            for b in range(B):
                g2 = row[:, b, 2:6:3, :]
                last = dve.scalar_tensor_tensor(out=g2, in0=g2, scalar=-1.0, in1=gtmp[:, b], op0=ALU.add, op1=ALU.mult)
            last.then_inc(s_dve0, N_DVE0 - n0[0])
            dve.wait_ge(s_dve0, N_DVE0)
            dve.wait_ge(s_x, 64)

            with dve.Fori(0, B) as b:
                for t in range(TPB):
                    dve.bn_stats(stat[:, t, :], xs[:, b * TPB + t, :]).then_inc(s_st, 1)
                for t in range(TPB):
                    hold(dve, s_st, b * TPB + t + 1)
                    dve.bn_aggr(mv[:, t, :], stat[:, t, :]).then_inc(s_mv, 1)
                dve.wait_ge(s_rstd, b + 1)

                def normed(i):
                    for j in range(BT):
                        n, t = BT * i + j, BT * (NBLK - 1 - i) + j
                        if n >= 4:
                            dve.wait_ge(s_xT, b * TPB + n - 3)
                        dve.tensor_scalar(xn[:, n % 4, :], xs[:, b * TPB + t, :], mv[:, t, 0:1], rstd[:, t:t + 1],
                                          ALU.subtract, ALU.mult).then_inc(s_xn, 1)

                normed(0)
                for i in range(NBLK):
                    k = NBLK - 1 - i
                    if i + 1 < NBLK:
                        normed(i + 1)
                    for g in range(NG):
                        dve.wait_ge(s_rawmm, b * NBLK * NG + NG * i + g + 1)
                        dve.tensor_copy(raw[:, g, HALO + k * BLK:HALO + (k + 1) * BLK], bank[2 + g][:, :]).then_inc(s_raw, 1)

                NL = 7
                cnt = [0]

                def link(ins):
                    cnt[0] += 1
                    ins.then_inc(s_dve, 1)
                    dve.wait_ge(s_dve, b * NL + cnt[0])

                dve.wait_ge(s_z, b * TPB + TPB)
                for d in range(2):
                    last = dve.tensor_tensor(sp[:, 0, d * NH * TPB:(d + 1) * NH * TPB].rearrange("p (h t) -> p h t", h=NH),
                                             dtr[:, :, :].rearrange("p t h -> p h t"), biasb[:, d * NH:(d + 1) * NH, :],
                                             ALU.add)
                link(last)
                link(dve.tensor_scalar(sp[:, 5, :], sp[:, 0, :], -1.0, None, ALU.mult))
                dve.tensor_tensor(sp[:, 1, :], sp[:, 0, :], sp[:, 5, :], ALU.max).then_inc(s_spe, 1)
                dve.wait_ge(s_spe, b * 4 + 2)
                dve.tensor_scalar(sp[:, 3, :], sp[:, 2, :], 1.0, None, ALU.add).then_inc(s_spe, 1)
                dve.wait_ge(s_spe, b * 4 + 4)
                link(dve.tensor_scalar(sp[:, 5, :], sp[:, 3, :], -1.0, None, ALU.add))
                link(dve.tensor_scalar(sp[:, 6, :], sp[:, 5, :], 0.0, None, ALU.is_equal))
                link(dve.tensor_tensor(sp[:, 5, :], sp[:, 5, :], sp[:, 6, :], ALU.add))
                dve.reciprocal(sp[:, 7, :], sp[:, 5, :])
                dve.tensor_tensor(sp[:, 4, :], sp[:, 4, :], sp[:, 2, :], ALU.mult)
                link(dve.tensor_tensor(sp[:, 6, :], sp[:, 6, :], sp[:, 2, :], ALU.mult))
                dve.tensor_tensor(sp[:, 4, :], sp[:, 4, :], sp[:, 7, :], ALU.mult)
                link(dve.tensor_scalar(sp[:, 0, :], sp[:, 0, :], 0.0, None, ALU.max))
                assert cnt[0] == NL
                dve.tensor_tensor(sp[:, 4, :], sp[:, 4, :], sp[:, 6, :], ALU.add).then_inc(s_wB, 1)
                dve.wait_ge(s_wB, b * 4 + 1)
                dve.tensor_tensor(dtv[:, :], sp[:, 4, :], sp[:, 0, :], ALU.add).then_inc(s_wB, 1)
                dve.wait_ge(s_wB, b * 4 + 2)
                dve.tensor_tensor(av[:, :], dtv[:, :], ab[:, :, :].rearrange("p k t -> p (k t)"), ALU.mult).then_inc(s_a, 1)
                dve.wait_ge(s_etab, b + 1)
                dve.tensor_tensor(wB[:, :], etab[:, 1, :], dtv[:, :], ALU.mult).then_inc(s_wB, 2)
                phase_end(dve, b, 0)

                def taps(s, k):
                    d, blk = step_of(s)
                    off = (k - HALO) * (1 - 2 * d)
                    n = HALO - 1 - k
                    c0 = HALO + blk * BLK + off
                    for g in range(NG):
                        if n == 0:
                            dve.wait_ge(s_tap0, b * STEPS * NG + s * NG + g + 1)
                        else:
                            dve.wait_ge(s_tap, b * STEPS * 9 + 9 * s + 3 * (n - 1) + g + 1)
                        dve.scalar_tensor_tensor(out=acc[:, g, :], in0=raw[:, g, c0:c0 + BLK],
                                                 scalar=cw[:, d, g, k:k + 1], in1=acc[:, g, :],
                                                 op0=ALU.mult, op1=ALU.add).then_inc(s_tap, 1)

                def mix(q):
                    d, t = chunk_of(q)
                    dve.wait_ge(s_e, b * CHUNKS + q + 1)
                    if q >= 2:
                        dve.wait_ge(s_ys, b * CHUNKS + q - 1)
                    for h in range(NH):
                        last = dve.scalar_tensor_tensor(out=ms[:, q % 2, h, :], in0=es[:, q % 2, h, :],
                                                        scalar=dtv[:, col(d, h, t)], in1=bank[2 + q % 2][:, DI:DI + P],
                                                        op0=ALU.mult, op1=ALU.mult)
                    last.then_inc(s_m, 1)

                def carry(q):
                    d, t = chunk_of(q)
                    if q >= 1:
                        dve.wait_ge(s_yo, b * CHUNKS + q)
                    if q % TPB == TPB - 1:
                        dve.memset(st[:, (q + 1) % 2, :], 0.0).then_inc(s_S, 1)
                        return
                    for h in range(NH):
                        cs = slice(h * HD, (h + 1) * HD)
                        last = dve.scalar_tensor_tensor(out=st[:, (q + 1) % 2, cs], in0=st[:, q % 2, cs],
                                                        scalar=etab[0:NS, 2, col(d, h, t)],
                                                        in1=bank[4 + q % 2][0:NS, DI + h * HD:DI + (h + 1) * HD],
                                                        op0=ALU.mult, op1=ALU.add)
                    last.then_inc(s_S, 1)

                for k in (2, 1, 0):
                    taps(0, k)
                mix(0)
                for q in range(CHUNKS):
                    d, t = chunk_of(q)
                    s, j = q // BT, q % BT
                    if j < 3 and s + 1 < STEPS:
                        taps(s + 1, 2 - j)
                    if q + 1 < CHUNKS:
                        mix(q + 1)
                    dve.wait_ge(s_ys, b * CHUNKS + q + 1)
                    if q >= 1:
                        dve.wait_ge(s_S, b * CHUNKS + q)
                    carry(q)
                    dve.wait_ge(s_wu, b * CHUNKS + q + 1)
                    dve.tensor_tensor(vs[:, q % 2, :], bank[4 + q % 2][:, 0:DI], ws[:, q % 2, :], ALU.add).then_inc(s_v, 1)
                    dve.wait_ge(s_v, b * CHUNKS + q + 1)
                    dve.tensor_tensor(yz[:, d, t, :], vs[:, q % 2, :], zs[:, t, :], ALU.mult).then_inc(s_yz, 1)
                phase_end(dve, b, 1)

                dve.wait_ge(s_rn, b + 1)

                def both(t, m):
                    a = t % 2
                    dve.tensor_scalar(y1[:, a, :], yz[:, 0, t, :], rn[:, 0, t:t + 1], None, ALU.mult).then_inc(s_y1, 1)
                    dve.wait_ge(s_y1, m + 1)
                    if t >= 2:
                        dve.wait_ge(s_yTm, m - 1)
                    dve.scalar_tensor_tensor(out=ysum[:, a, :], in0=yz[:, 1, t, :], scalar=rn[:, 1, t:t + 1],
                                             in1=y1[:, a, :], op0=ALU.mult, op1=ALU.add).then_inc(s_ysum, 1)

                def route(t, m):
                    a = t % 2
                    dve.wait_ge(s_lgm, m + 1)

                    def step(ins, n):
                        ins.then_inc(s_rt_dve, 1)
                        dve.wait_ge(s_rt_dve, NR * m + n)

                    step(dve.tensor_tensor(lg[:, a, :], bank[6 + a][:, 0:NE], gb_sum[:, :], ALU.add), 1)
                    step(dve.tensor_reduce(mx[:, a, 0:1], lg[:, a, :], AX_X, ALU.max), 2)
                    step(dve.scalar_tensor_tensor(out=cand[:, a, :], in0=lg[:, a, :], scalar=mx[:, a, 0:1],
                                                  in1=rank8[:, :], op0=ALU.is_equal, op1=ALU.mult), 3)
                    step(dve.tensor_reduce(mx[:, a, 1:2], cand[:, a, :], AX_X, ALU.max), 4)
                    if t >= 2:
                        dve.wait_ge(s_rank, m - 1)
                    dve.tensor_scalar(hot[:, a, :], cand[:, a, :], mx[:, a, 1:2], None, ALU.is_equal).then_inc(s_hot, 1)
                    step(dve.tensor_tensor(base[:, :], region0[:, :], count[:, :], ALU.add), 5)
                    dve.wait_ge(s_rank, m + 1)
                    step(dve.tensor_tensor(pos[:, a, :], bank[6 + a][:, NE:2 * NE], base[:, :], ALU.add), 6)
                    step(dve.tensor_tensor(posj[:, a, :], pos[:, a, :], hot[:, a, :], ALU.mult), 7)
                    step(dve.tensor_reduce(posf[:, a, :], posj[:, a, :], AX_X, ALU.add), 8)
                    if t >= 4:
                        dve.wait_ge(s_scat[t % 4], b * 64 + 16 * (t // 4))
                    dve.tensor_copy(rowat[:, t % 4, :], posf[:, a, :]).then_inc(s_pos, 1)
                    step(dve.tensor_tensor(count[:, :], bank[6 + a][:, 2 * NE:3 * NE], count[:, :], ALU.add), 9)

                both(0, b * TPB)
                for t in range(TPB):
                    m, a = b * TPB + t, t % 2
                    if t + 1 < TPB:
                        both(t + 1, m + 1)
                    dve.wait_ge(s_o, m + 1)
                    dve.tensor_tensor(o1[:, a, :], bank[2 + a][:, 0:DM], row[:, b, 2, :], ALU.mult).then_inc(s_o1, 1)
                    dve.wait_ge(s_o1, m + 1)
                    if t >= 4:
                        dve.wait_ge(s_scat[t % 4], b * 64 + 16 * (t // 4))
                    x1 = rows[:, t % 4, DM:2 * DM]
                    dve.tensor_tensor(x1, xs[:, m, :], o1[:, a, :], ALU.add).then_inc(s_x1r, 1)
                    dve.wait_ge(s_x1r, m + 1)
                    dve.bn_stats(st2[:, a, :], x1).then_inc(s_st2, 1)
                    hold(dve, s_st2, m + 1)
                    dve.bn_aggr(mv2[:, a, :], st2[:, a, :]).then_inc(s_mv2, 1)
                    if t >= 1:
                        route(t - 1, m - 1)
                    dve.wait_ge(s_rs2, m + 1)
                    if t >= 2:
                        dve.wait_ge(s_h2a, m - 1)
                    dve.tensor_scalar(xn2[:, a, :], x1, mv2[:, a, 0:1], rs2[:, a, :],
                                      ALU.subtract, ALU.mult).then_inc(s_xn2, 1)
                route(TPB - 1, b * TPB + TPB - 1)
                phase_end(dve, b, 2)

            nt = [0]

            def tab(ins):
                nt[0] += 1
                ins.then_inc(s_tab, 1)
                dve.wait_ge(s_tab, 2 + nt[0])

            dve.wait_ge(s_tab, 2)
            dve.tensor_tensor(padf, region0[:, :], count[:, :], ALU.add)
            for e in range(NE):
                last = dve.tensor_scalar(tiles_gt[:, e, :], m128, count[:, e:e + 1], None, ALU.is_lt)
            tab(last)
            tab(dve.tensor_reduce(ntile, tiles_gt, AX_X, ALU.add))
            dve.tensor_scalar(padf, padf, pcol[:, 0:1], None, ALU.add)
            dve.tensor_scalar(coef, ntile, -float(P), float(REGION), ALU.mult, ALU.add)
            tab(dve.tensor_copy(cum[:, 0:1], ntile[:, 0:1]))
            dve.tensor_copy(padi, padf).then_inc(s_padi, 1)
            for e in range(1, NE):
                tab(dve.tensor_tensor(cum[:, e:e + 1], cum[:, e - 1:e], ntile[:, e:e + 1], ALU.add))
            for e in range(NE):
                dve.tensor_scalar(behind[:, 0, e, :], slot_i, cum[:, e:e + 1], coef[:, e:e + 1], ALU.is_ge, ALU.mult)
                last = dve.tensor_scalar(behind[:, 1, e, :], slot_i, cum[:, e:e + 1], None, ALU.is_ge)
            tab(last)
            for k in range(2):
                last = dve.tensor_reduce(slot_v[:, k, :], behind[:, k].rearrange("p e s -> p s e"), AX_X, ALU.add)
            tab(last)
            tab(dve.scalar_tensor_tensor(out=slot_v[:, 0, :], in0=slot_i, scalar=float(P), in1=slot_v[:, 0, :],
                                         op0=ALU.mult, op1=ALU.add))
            dve.tensor_scalar(slot_v[:, 0, :], slot_v[:, 0, :], float(NE * REGION), None, ALU.min)
            tab(dve.tensor_scalar(slot_v[:, 1, :], slot_v[:, 1, :], float(NE - 1), None, ALU.min))
            dve.tensor_copy(slot_r, slot_v).then_inc(s_tabv, 1)
            dve.wait_ge(s_tabv, 1)
            dve.tensor_tensor(gdiff, row[:, 1, 5, :], row[:, 0, 5, :], ALU.subtract).then_inc(s_gd, 1)
            dve.wait_ge(s_gd, 1)
            dve.wait_ge(s_wf, 64)

            def bias1(s, a, first):
                e = dve.value_load(slot_r[0:1, 1, bass.ds(s, 1)], min_val=0, max_val=NE - 1)
                dve.wait_ge(s_h1, s + 1)
                if not first:
                    dve.wait_ge(s_hx, s - 1)
                dve.tensor_tensor(hb[:, a, :], bank[2 + a][:, :], b1s[:, bass.ds(e, 1), :].rearrange("p a f -> p (a f)"),
                                  ALU.add).then_inc(s_hb, 1)

            def combine(s, a, k, rk, first, put16):
                e = dve.value_load(slot_r[0:1, 1, bass.ds(s, 1)], min_val=0, max_val=NE - 1)
                dve.wait_ge(s_rb[k], rk)
                dve.tensor_scalar(flag[:, a, :], xr[:, bass.ds(s, 1), DM:DM + 1].rearrange("p a c -> p (a c)"),
                                  float(L), None, ALU.is_ge).then_inc(s_flag, 1)
                dve.wait_ge(s_y2, s + 1)
                dve.tensor_tensor(yo1[:, a, :], bank[6 + a][:, 0:DM], b2s[:, bass.ds(e, 1), :].rearrange("p a c -> p (a c)"),
                                  ALU.add).then_inc(s_yo1, 1)
                dve.wait_ge(s_flag, s + 1)
                dve.scalar_tensor_tensor(out=gsel[:, a, :], in0=gdiff, scalar=flag[:, a, :],
                                         in1=row[:, 0, 5, :], op0=ALU.mult, op1=ALU.add).then_inc(s_gs, 1)
                dve.wait_ge(s_yo1, s + 1)
                dve.wait_ge(s_gs, s + 1)
                dve.tensor_tensor(yo2[:, a, :], yo1[:, a, :], gsel[:, a, :], ALU.mult).then_inc(s_yo2, 1)
                dve.wait_ge(s_yo2, s + 1)
                if not first:
                    dve.wait_ge(s_out[k], put16)
                dve.tensor_tensor(ob[:, k, :], yo2[:, a, :], xr[:, bass.ds(s, 1), 0:DM].rearrange("p a c -> p (a c)"),
                                  ALU.add).then_inc(s_ob, 1)

            def dve_step(r, k, it):
                if it is None:
                    if 0 <= r + 1 < NSLOT:
                        bias1(r + 1, (r + 1) % 2, r + 1 < 2)
                    if r >= 1:
                        combine(r - 1, (r - 1) % 2, (r - 1) % 4, 32 * ((r - 1) // 4) + 32, r - 1 < 4, 16 * ((r - 1) // 4))
                else:
                    bias1(r + 1, (k + 1) % 2, False)
                    combine(r - 1, (k + 1) % 2, (k + 3) % 4, 32 * it + 32 * ((k + 3) // 4), False,
                            16 * it + 16 * ((k + 3) // 4) - 16)

            for r in range(-1, 8):
                dve_step(r, 0, None)
            with dve.Fori(2, (NSLOT - 1) // 4) as it:
                for k in range(4):
                    dve_step(4 * it + k, k, it)
            for r in range((NSLOT - 1) // 4 * 4, NSLOT + 1):
                dve_step(r, 0, None)



_INS = ["u", "w_xbc", "w_zdt", "conv_w", "conv_b", "dt_bias", "a_log", "d_skip", "norm_w", "w_out", "gate_w", "gate_b",
        "w1", "b1", "w2", "b2", "c_t", "wmod"]


def kernel(**inputs):
    import numpy as _np
    import concourse.bacc as _bacc
    from concourse import mybir as _mybir
    from concourse.bass_utils import run_bass_kernel_spmd as _run

    x = {k: _np.asarray(v) for k, v in inputs.items()}
    wi = x["L0_attn_in_proj_w"]

    def channels(fw, bw):
        return _np.stack([v.reshape((NG, P) + v.shape[1:]) for v in (fw, bw)]).swapaxes(0, 2).swapaxes(1, 2)

    laid = {
        "u": x["L0_attn_u"],
        "w_xbc": wi[DI:DI + NG * P].T,
        "w_zdt": _np.concatenate([wi[0:DI], wi[DI + NG * P:]]).T,
        "conv_w": channels(x["L0_attn_conv_w"], x["L0_attn_conv_w_bw"]),
        "conv_b": channels(x["L0_attn_conv_b"], x["L0_attn_conv_b_bw"]),
        "dt_bias": _np.concatenate([x["L0_attn_dt_bias"], x["L0_attn_dt_bias_bw"]]),
        "a_log": _np.concatenate([x["L0_attn_A_log"], x["L0_attn_A_b_log"]]),
        "d_skip": _np.concatenate([x["L0_attn_D"], x["L0_attn_D_b"]]),
        "norm_w": x["L0_attn_norm_w"].reshape(NH, HD).T,
        "w_out": x["L0_attn_out_proj_w"].T.reshape(NH, HD, DM).swapaxes(0, 1),
        "gate_w": x["L0_ffn_gate_w"].T,
        "gate_b": _np.stack([x["L0_ffn_gate_b"], x["L0_ffn_expert_bias"]]),
        "w1": x["L0_ffn_w1"].transpose(1, 0, 2),
        "b1": x["L0_ffn_b1"],
        "w2": x["L0_ffn_w2"].reshape(NE, FC, P, DM).transpose(2, 0, 1, 3),
        "b2": x["L0_ffn_b2"],
        "c_t": x["L0_c"].T,
        "wmod": x["L0_wmod"],
    }
    nc = _bacc.Bacc("TRN2", target_bir_lowering=False, num_devices=1)
    arrays, args = {}, []
    for name in _INS:
        a = _np.ascontiguousarray(laid[name])
        arrays[f"in_{name}_dram"] = a
        args.append(nc.dram_tensor(f"in_{name}_dram", a.shape, _mybir.dt.from_np(a.dtype), kind="ExternalInput").ap())
    args.append(nc.dram_tensor("out_0_dram", (B, L, DM), F32, kind="ExternalOutput").ap())
    build(nc, *args)
    r = _run(nc, [arrays], core_ids=[0])
    return r.results[0]["out_0_dram"]
```

```python
from contextlib import ExitStack

import numpy as np

import concourse.bass as bass
from concourse import mybir

F32 = mybir.dt.float32
BF16 = mybir.dt.bfloat16
ALU = mybir.AluOpType
ACT = mybir.ActivationFunctionType
AX_X = mybir.AxisListType.X

P = 128
B, L, DM = 2, 2048, 128
NH, HD, NS = 2, 128, 64
DI = NH * HD
KC = 4
HALO = KC - 1
NE, FF = 8, 512
EPS = 1e-5
TPB = L // P
BT = 4
BLK = BT * P
NBLK = TPB // BT
NG = 3
STEPS = 2 * NBLK
CHUNKS = STEPS * BT
NDT = NH
ZW = DI + NDT
FC = FF // P
MASKED = -30000.0
NTOK = B * L
REGION = NTOK + P
NSLOT = NTOK // P + NE - 1
ROW = 2 * DM + 4


def step_of(s):
    return (1, NBLK - 1 - s) if s < NBLK else (0, s - NBLK)


def chunk_of(q):
    return (1, TPB - 1 - q) if q < TPB else (0, q - TPB)


def build(nc, u, w_xbc, w_zdt, conv_w, conv_b, dt_bias, a_log, d_skip, norm_w, w_out, gate_w, gate_b,
          w1, b1, w2, b2, c_t, wmod, out):
    ctx = ExitStack()
    with ctx:
        def sb(name, shape, dt=F32):
            return ctx.enter_context(nc.sbuf_tensor(name, shape, dt))

        def sem(name):
            return ctx.enter_context(nc.semaphore(name))

        bank = [ctx.enter_context(nc.psum_tensor(f"bank{i}", [P, 512], F32)) for i in range(8)]

        wx = sb("wx", [P, NG * P])
        wz = sb("wz", [P, ZW])
        cw = sb("cw", [P, 2, NG, KC])
        cb = sb("cb", [P, 2, NG])
        dtb = sb("dtb", [P, 2 * NH])
        alog = sb("alog", [P, 2 * NH])
        dsk = sb("dsk", [P, 2 * NH])
        nw = sb("nw", [P, NH])
        wo = sb("wo", [P, NH, DM])
        won = sb("won", [P, NH, DM])
        gw = sb("gw", [P, NE])
        gbias = sb("gbias", [P, 2, NE])
        gb_sum = sb("gb_sum", [P, NE])
        ct_in = sb("ct_in", [P, B])
        csil = sb("csil", [P, B])
        csil_bc = sb("csil_bc", [P, B, P])
        wm = sb("wm", [P, 6 * DM])
        modc = sb("modc", [P, 2, B])
        row = sb("row", [P, B, 6, DM])
        gtmp = sb("gtmp", [P, B, 2, DM])
        ident = sb("ident", [P, P])
        identb = sb("identb", [P, P], BF16)
        incl = sb("incl", [P, 2, P])
        strict = sb("strict", [P, 2, P])
        negm = sb("negm", [P, 2, 2, P], BF16)
        ones = sb("ones", [P, P])
        w1s = sb("w1s", [P, NE, FF])
        w2s = sb("w2s", [P, NE, FC, DM])
        b2s = sb("b2s", [P, NE, DM])
        padrow = sb("padrow", [P, ROW])
        pcol = sb("pcol", [P, 1])

        xs = sb("xs", [P, B * TPB, DM])
        ids = sb("ids", [P, B * TPB])
        count = sb("count", [P, NE])
        nextrow = sb("nextrow", [P, 2, BT, NE])
        region0 = sb("region0", [P, NE])

        ARENA = sb("arena", [P, 2 * TPB * DI + NG * (L + 2 * HALO)])
        yz = ARENA[:, 0:2 * TPB * DI].rearrange("p (d t c) -> p d t c", d=2, t=TPB)
        raw = ARENA[:, 2 * TPB * DI:].rearrange("p (g c) -> p g c", g=NG)
        zs = sb("zs", [P, TPB, DI])
        stat = sb("stat", [P, TPB, 6])
        mv = sb("mv", [P, TPB, 2])
        ve = sb("ve", [P, TPB])
        rstd = sb("rstd", [P, TPB])
        mhalf = sb("mhalf", [P, 2 * TPB])
        dtr = sb("dtr", [P, TPB, NDT])
        NQ = 2 * NH * TPB
        sp = sb("sp", [P, 8, NQ])
        biasb = sb("biasb", [P, 2 * NH, TPB])
        ab = sb("ab", [P, 2 * NH, TPB])
        dtv = sb("dtv", [P, NQ])
        av = sb("av", [P, NQ])
        etab = sb("etab", [P, 3, NQ])
        wB = sb("wB", [P, NQ])
        ssq = sb("ssq", [P, 2, TPB])
        rn = sb("rn", [P, 2, TPB])
        rt = sb("rt", [P, 2, TPB])

        xn = sb("xn", [P, 4, DM])
        hT = sb("hT", [P, 2, BLK])
        acc = sb("acc", [P, NG, BLK])
        cx = sb("cx", [P, 2, NH, BLK])
        bT = sb("bT", [NS, 2, BLK])
        cT = sb("cT", [NS, 2, BLK])
        lseg = sb("lseg", [P, 2, NH, P])
        xt = sb("xt", [P, 2, DI])
        bs = sb("bs", [P, 2, NH, NS])
        es = sb("es", [P, 2, NH, P])
        ms = sb("ms", [P, 2, NH, P])
        st = sb("st", [NS, 2, DI])
        us = sb("us", [P, 2, DI])
        ws = sb("ws", [P, 2, DI])
        vs = sb("vs", [P, 2, DI])
        junk = sb("junk", [P, DI])
        y1 = cx[:, 0].rearrange("p g c -> p (g c)").rearrange("p (j c) -> p j c", j=BT)
        ysum = cx[:, 1].rearrange("p g c -> p (g c)").rearrange("p (j c) -> p j c", j=BT)
        yT = acc[:, 0:2].rearrange("p g c -> p (g c)").rearrange("p (j c) -> p j c", j=BT)
        o1 = acc[:, 2].rearrange("p (j c) -> p j c", j=BT)
        xn2 = es[:, :].rearrange("p a h c -> p (a h) c")
        h2c = ms[:, :].rearrange("p a h c -> p (a h) c")
        rows = sb("rows", [P, 2 * BT, ROW])
        rowat = sb("rowat", [P, 2 * BT, 1], mybir.dt.int32)
        st2 = sb("st2", [P, BT, 6])
        mv2 = sb("mv2", [P, 2, BT, 2])
        ve2 = sb("ve2", [P, BT])
        rs2 = sb("rs2", [P, 2, BT])
        lg = sb("lg", [P, BT, NE])
        mx = sb("mx", [P, 2, BT])
        hot = sb("hot", [P, 2, BT, NE])
        pos = sb("pos", [P, BT, NE])
        posf = sb("posf", [P, BT])
        rank8 = sb("rank8", [P, NE])
        cand = sb("cand", [P, BT, NE])

        s_load = sem("s_load")
        s_x = sem("s_x")
        s_wf = sem("s_wf")
        s_pool0 = sem("s_pool0")
        s_act0 = sem("s_act0")
        s_pe0 = sem("s_pe0")
        s_dve0 = sem("s_dve0")
        s_phase = sem("s_phase")
        s_st = sem("s_st")
        s_mv = sem("s_mv")
        s_ve = sem("s_ve")
        s_rstd = sem("s_rstd")
        s_xn = sem("s_xn")
        s_xT = sem("s_xT")
        s_hT = sem("s_hT")
        s_rawmm = sem("s_rawmm")
        s_raw = sem("s_raw")
        s_zmm = sem("s_zmm")
        s_z = sem("s_z")
        s_dve = sem("s_dve")
        s_spe = sem("s_spe")
        s_a = sem("s_a")
        s_pfx = sem("s_pfx")
        s_etab = sem("s_etab")
        s_wB = sem("s_wB")
        s_tap0 = sem("s_tap0")
        s_tap = sem("s_tap")
        s_silu = sem("s_silu")
        s_L = sem("s_L")
        s_tx = sem("s_tx")
        s_sg = sem("s_sg")
        s_ys = sem("s_ys")
        s_yo = sem("s_yo")
        s_xt = sem("s_xt")
        s_e = sem("s_e")
        s_u = sem("s_u")
        s_m = sem("s_m")
        s_S = sem("s_S")
        s_v = sem("s_v")
        s_yz = sem("s_yz")
        s_sq = sem("s_sq")
        s_w = sem("s_w")
        s_wu = sem("s_wu")
        s_rt = sem("s_rt")
        s_rn = sem("s_rn")
        s_y1 = sem("s_y1")
        s_ysum = sem("s_ysum")
        s_yTm = sem("s_yTm")
        s_yT = sem("s_yT")
        s_o = sem("s_o")
        s_o1 = sem("s_o1")
        s_st2 = sem("s_st2")
        s_mv2 = sem("s_mv2")
        s_ve2 = sem("s_ve2")
        s_rs2 = sem("s_rs2")
        s_xn2 = sem("s_xn2")
        s_h2a = sem("s_h2a")
        s_h2 = sem("s_h2")
        s_h2m = sem("s_h2m")
        s_h2c = sem("s_h2c")
        s_lgm = sem("s_lgm")
        s_rt_dve = sem("s_rt_dve")
        s_hot = sem("s_hot")
        s_routed = sem("s_routed")
        s_rank = sem("s_rank")
        s_pos = sem("s_pos")
        s_x1r = sem("s_x1r")
        s_id = sem("s_id")
        s_scat = [sem(f"s_scat{i}") for i in range(2 * BT)]
        s_tab = sem("s_tab")
        s_tabv = sem("s_tabv")
        s_padi = sem("s_padi")
        s_pad = sem("s_pad")
        s_rb = [sem(f"s_rb{i}") for i in range(4)]
        s_eT = sem("s_eT")
        s_eTc = sem("s_eTc")
        s_h1 = sem("s_h1")
        s_hb = sem("s_hb")
        s_hx = sem("s_hx")
        s_hr = sem("s_hr")
        s_y2 = sem("s_y2")
        s_flag = sem("s_flag")
        s_gs = sem("s_gs")
        s_tok = sem("s_tok")
        s_gd = sem("s_gd")
        s_yo1 = sem("s_yo1")
        s_yo2 = sem("s_yo2")
        s_ob = sem("s_ob")
        s_out = [sem(f"s_out{i}") for i in range(4)]

        b1s = zs[:, :, :].rearrange("p t c -> p (t c)").rearrange("p (e f) -> p e f", e=NE)
        at = [0]

        def over(n):
            at[0] += n
            return ARENA[:, at[0] - n:at[0]]

        NM = NTOK // P
        tiles_gt = over(NE * NM).rearrange("p (e m) -> p e m", e=NE)
        m128 = over(NM)
        ntile = over(NE)
        cum = over(NE)
        coef = over(NE)
        slot_i = over(NSLOT)
        behind = over(2 * NE * NSLOT).rearrange("p (k e s) -> p k e s", k=2, e=NE)
        slot_v = over(2 * NSLOT).rearrange("p (k s) -> p k s", k=2)
        slot_r = over(2 * NSLOT).bitcast(mybir.dt.int32).rearrange("p (k s) -> p k s", k=2)
        padf = over(NE)
        padi = over(NE).bitcast(mybir.dt.int32)
        rh = over(4 * DM).rearrange("p (a c) -> p a c", a=4)
        XR = ROW - DM
        xr = over(NSLOT * XR).rearrange("p (s c) -> p s c", s=NSLOT)
        gdiff = over(DM)
        hTs = over(2 * P).rearrange("p (a c) -> p a c", a=2)
        hb = over(2 * FF).rearrange("p (a c) -> p a c", a=2)
        hr = over(2 * FF).rearrange("p (a c) -> p a c", a=2)
        flag = over(2).rearrange("p (a c) -> p a c", a=2)
        gsel = over(2 * DM).rearrange("p (a c) -> p a c", a=2)
        tok = over(4).bitcast(mybir.dt.int32).rearrange("p (a c) -> p a c", a=4)
        yo1 = over(2 * DM).rearrange("p (a c) -> p a c", a=2)
        yo2 = over(2 * DM).rearrange("p (a c) -> p a c", a=2)
        ob = over(4 * DM).rearrange("p (a c) -> p a c", a=4)

        routed = nc.dram_tensor("routed_rows", (NE * REGION + P, ROW), F32, kind="Internal").ap()
        N_POOL0 = 11 + 2 * (2 + 2 * NH) + 2 + 2 * 2 * NH
        N_DVE0 = 15

        s_held = sem("s_held")

        def hold(eng, signal, value):
            eng.wait_ge(signal, value)
            eng.sem_inc(s_held, 1)

        def phase_end(eng, b, n):
            eng.sem_inc(s_held, 1)
            eng.drain().then_inc(s_phase, 1)
            hold(eng, s_phase, b * 12 + 4 * (n + 1))

        def col(d, h, t):
            c = (d * NH + h) * TPB + t
            return slice(c, c + 1)

        out_rows = out.rearrange("b t d -> (b t) d")
        NR = 7 + BT

        block = ctx.enter_context(nc.Block())

        @block.sync
        def _(sp_):
            n = 0
            u_rows = u.rearrange("b (t p) d -> p (b t) d", p=P)
            for i in range(2 * B):
                h = TPB // 2
                sp_.dma_start(xs[:, i * h:(i + 1) * h, :], u_rows[:, i * h:(i + 1) * h, :]).then_inc(s_x, 16)
            for dst, src in (
                (wx[:, :], w_xbc), (wz[:, :], w_zdt), (cw[:, :, :, :], conv_w), (cb[:, :, :], conv_b),
                (dtb[:, :], dt_bias.partition_broadcast(P)), (alog[:, :], a_log.partition_broadcast(P)),
                (dsk[:, :], d_skip.partition_broadcast(P)),
                (nw[:, :], norm_w), (wo[:, :, :], w_out), (gw[:, :], gate_w),
                (gbias[:, :, :], gate_b.partition_broadcast(P)),
                (ct_in[:, :], c_t), (wm[:, :], wmod),
            ):
                sp_.dma_start(dst, src).then_inc(s_load, 16)
                n += 1
            assert n == 13
            for dst, src in ((w1s[:, :, :], w1), (w2s[:, :, :, :], w2), (b2s[:, :, :], b2.partition_broadcast(P))):
                sp_.dma_start(dst, src).then_inc(s_wf, 16)
            sp_.wait_ge(s_phase, 12 * (B - 1) + 8)
            sp_.dma_start(b1s, b1.partition_broadcast(P)).then_inc(s_wf, 16)

            sp_.wait_ge(s_phase, 12 * B)
            for i in range(2 * BT):
                sp_.wait_ge(s_scat[i], 16 * B * TPB // (2 * BT))
            sp_.wait_ge(s_pad, 16 * (NE + 1))
            sp_.wait_ge(s_tabv, 1)

            def load_rows(s, k):
                first = sp_.value_load(slot_r[0:1, 0, bass.ds(s, 1)], min_val=0, max_val=NE * REGION)
                sp_.dma_start(rh[:, k, :], routed[bass.ds(first, P), 0:DM]).then_inc(s_rb[k], 16)
                sp_.dma_start(xr[:, bass.ds(s, 1), :].rearrange("p a c -> p (a c)"),
                              routed[bass.ds(first, P), DM:ROW]).then_inc(s_rb[k], 16)

            for s in range(4):
                load_rows(s, s)
            with sp_.Fori(1, NSLOT // 4) as it:
                for k in range(4):
                    sp_.wait_ge(s_eT, 4 * it + k - 3)
                    load_rows(4 * it + k, k)
            for s in range(NSLOT // 4 * 4, NSLOT):
                sp_.wait_ge(s_eT, s - 3)
                load_rows(s, s % 4)

        NLOAD = 13 * 16

        @block.gpsimd
        def _(pool):
            n = [0]

            def link(ins):
                n[0] += 1
                ins.then_inc(s_pool0, 1)
                hold(pool, s_pool0, n[0])

            link(pool.memset(ident[:, :], 0.0))
            link(pool.affine_select(out=ident[:, :], in_=ident[:, :], compare_op=ALU.not_equal, fill=1.0, base=0,
                                    pattern=[[-1, P]], channel_multiplier=1))
            link(pool.tensor_copy(identb[:, :], ident[:, :]))
            link(pool.memset(ones[:, :], 1.0))
            for d in range(2):
                sgn = 1 - 2 * d
                link(pool.affine_select(out=incl[:, d, :], in_=ones[:, :], compare_op=ALU.is_ge, fill=0.0, base=0,
                                        pattern=[[sgn, P]], channel_multiplier=-sgn))
                link(pool.affine_select(out=strict[:, d, :], in_=ones[:, :], compare_op=ALU.is_gt, fill=0.0, base=0,
                                        pattern=[[-sgn, P]], channel_multiplier=sgn))
                for h in range(NH):
                    link(pool.memset(negm[:, d, h, :], 0.0))
                    link(pool.affine_select(out=negm[:, d, h, :], in_=negm[:, d, h, :], compare_op=ALU.is_ge,
                                            fill=MASKED, base=0, pattern=[[sgn, P]], channel_multiplier=-sgn))
            link(pool.memset(mhalf[:, :], -0.5))
            link(pool.iota(rank8[:, :], pattern=[[-1, NE]], base=NE, channel_multiplier=0,
                           allow_small_or_imprecise_dtypes=True))
            link(pool.iota(ids[:, :], pattern=[[P, B * TPB]], base=0, channel_multiplier=1,
                           allow_small_or_imprecise_dtypes=True))
            link(pool.iota(pcol[:, :], pattern=[[0, 1]], base=0, channel_multiplier=1,
                           allow_small_or_imprecise_dtypes=True))
            link(pool.iota(region0[:, :], pattern=[[REGION, NE]], base=0, channel_multiplier=0,
                           allow_small_or_imprecise_dtypes=True))
            link(pool.iota(nextrow[:, 0, 0, :], pattern=[[REGION, NE]], base=0, channel_multiplier=0,
                           allow_small_or_imprecise_dtypes=True))
            link(pool.memset(padrow[:, :], 0.0))
            link(pool.memset(padrow[:, 2 * DM:2 * DM + 1], float(NTOK)))
            link(pool.memset(rows[:, :, 2 * DM:], 0.0))
            hold(pool, s_load, NLOAD)
            for k in range(2 * NH):
                link(pool.memset(biasb[:, k, :], 0.0))
                link(pool.tensor_scalar(biasb[:, k, :], biasb[:, k, :], dtb[:, k:k + 1], 1.0, ALU.add, ALU.mult))
            assert n[0] == N_POOL0
            hold(pool, s_dve0, N_DVE0)

            with pool.Fori(0, B) as b:
                hold(pool, s_mv, b * TPB + TPB)
                pool.tensor_scalar(ve[:, :], mv[:, :, 1], EPS, 1.0, ALU.add, ALU.mult).then_inc(s_ve, 1)
                hold(pool, s_ve, b + 1)
                pool.tensor_tensor(rstd[:, :], ve[:, :], mhalf[:, 0:TPB], ALU.pow).then_inc(s_rstd, 1)
                phase_end(pool, b, 0)

                def decay_rows(q):
                    d, t = chunk_of(q)
                    if q >= 2:
                        hold(pool, s_sg, b * CHUNKS + q - 1)
                    for h in range(NH):
                        last = pool.tensor_scalar(lseg[:, q % 2, h, :], strict[:, d, :],
                                                  av[:, col(d, h, t)], 1.0, ALU.mult, ALU.mult)
                    last.then_inc(s_L, 1)

                decay_rows(0)
                decay_rows(1)
                for q in range(CHUNKS):
                    d, t = chunk_of(q)
                    if q + 2 < CHUNKS:
                        decay_rows(q + 2)
                    hold(pool, s_xt, b * CHUNKS + q + 1)
                    if q >= 2:
                        hold(pool, s_v, b * CHUNKS + q - 1)
                    for h in range(NH):
                        last = pool.tensor_scalar(ws[:, q % 2, h * HD:(h + 1) * HD], xt[:, q % 2, h * HD:(h + 1) * HD],
                                                  dsk[:, d * NH + h:d * NH + h + 1], 1.0, ALU.mult, ALU.mult)
                    last.then_inc(s_w, 1)
                    hold(pool, s_w, b * CHUNKS + q + 1)
                    hold(pool, s_u, b * CHUNKS + q + 1)
                    pool.tensor_tensor(ws[:, q % 2, :], ws[:, q % 2, :], us[:, q % 2, :], ALU.add).then_inc(s_wu, 1)
                phase_end(pool, b, 1)

                pool.tensor_scalar(rt[:, :, :], ssq[:, :, :], 1.0 / DI, EPS, ALU.mult, ALU.add).then_inc(s_rt, 1)
                hold(pool, s_rt, b + 1)
                pool.tensor_tensor(rn[:, :, :], rt[:, :, :], mhalf[:, :].rearrange("p (d t) -> p d t", d=2),
                                   ALU.pow).then_inc(s_rn, 1)

                def scatter(i):
                    hold(pool, s_pos, b * NBLK + i + 1)
                    hold(pool, s_x1r, b * NBLK + i + 1)
                    for j in range(BT):
                        k = (i % 2) * BT + j
                        pool.indirect_dma_start(routed[:, :], bass.IndirectOffsetOnAxis(ap=rowat[:, k, :].bitcast(mybir.dt.uint32), axis=0),
                                                rows[:, k, :], None).then_inc(s_scat[k], 16)

                for i in range(NBLK):
                    g, a = b * NBLK + i, i % 2
                    sl = slice(a * BT, (a + 1) * BT)
                    hold(pool, s_mv2, g + 1)
                    pool.tensor_scalar(ve2[:, :], mv2[:, a, :, 1], EPS, 1.0, ALU.add, ALU.mult).then_inc(s_ve2, 1)
                    hold(pool, s_ve2, g + 1)
                    if i >= 2:
                        hold(pool, s_xn2, g - 1)
                    pool.tensor_tensor(rs2[:, a, :], ve2[:, :], mhalf[:, 0:BT], ALU.pow).then_inc(s_rs2, 1)
                    hold(pool, s_h2a, g + 1)
                    pool.tensor_tensor(rows[:, sl, 0:DM], rows[:, sl, 0:DM],
                                       row[:, b, 3, :].unsqueeze(1).broadcast_to([P, BT, DM]), ALU.add).then_inc(s_h2, 1)
                    pool.tensor_copy(rows[:, sl, 2 * DM:2 * DM + 1].rearrange("p j c -> p (j c)"),
                                     ids[:, bass.ds(BT * g, BT)]).then_inc(s_id, 1)
                    hold(pool, s_id, g + 1)
                    hold(pool, s_h2, g + 1)
                    if i >= 1:
                        scatter(i - 1)
                scatter(NBLK - 1)
                phase_end(pool, b, 2)

            pool.dma_start(routed[NE * REGION:NE * REGION + P, :], padrow[:, :]).then_inc(s_pad, 16)
            pool.iota(m128, pattern=[[P, NM]], base=0, channel_multiplier=0,
                      allow_small_or_imprecise_dtypes=True).then_inc(s_tab, 1)
            pool.iota(slot_i, pattern=[[1, NSLOT]], base=0, channel_multiplier=0,
                      allow_small_or_imprecise_dtypes=True).then_inc(s_tab, 1)
            hold(pool, s_padi, 1)
            for e in range(NE):
                pool.indirect_dma_start(routed[:, :], bass.IndirectOffsetOnAxis(ap=padi[:, e:e + 1].bitcast(mybir.dt.uint32), axis=0),
                                        padrow[:, :], None).then_inc(s_pad, 16)

            def token_numbers(s, k, rk, free16):
                hold(pool, s_rb[k], rk)
                if free16 is not None:
                    hold(pool, s_out[k], free16)
                pool.tensor_copy(tok[:, k, :], xr[:, bass.ds(s, 1), DM:DM + 1].rearrange("p a c -> p (a c)")).then_inc(s_tok, 1)

            def put(s, k):
                hold(pool, s_ob, s + 1)
                hold(pool, s_tok, s + 1)
                pool.indirect_dma_start(out_rows, bass.IndirectOffsetOnAxis(ap=tok[:, k, :].bitcast(mybir.dt.uint32), axis=0),
                                        ob[:, k, :], None, bounds_check=NTOK - 1, oob_is_err=False).then_inc(s_out[k], 16)

            for s in range(4):
                token_numbers(s, s, 32, None)
                if s >= 1:
                    put(s - 1, s - 1)
            with pool.Fori(1, NSLOT // 4) as it:
                for k in range(4):
                    token_numbers(4 * it + k, k, 32 * it + 32, 16 * it)
                    put(4 * it + k - 1, (k + 3) % 4)
            for s in range(NSLOT // 4 * 4, NSLOT):
                token_numbers(s, s % 4, 32 * (s // 4) + 32, 16 * (s // 4))
                put(s - 1, (s - 1) % 4)
            put(NSLOT - 1, (NSLOT - 1) % 4)
            for k in range(4):
                hold(pool, s_out[k], 16 * ((NSLOT - k + 3) // 4))

        @block.scalar
        def _(act):
            act.wait_ge(s_load, NLOAD)
            act.activation(csil[:, :], ct_in[:, :], ACT.Silu).then_inc(s_act0, 1)
            act.activation(ab[:, :, 0], alog[:, :], ACT.Exp).then_inc(s_act0, 1)
            act.wait_ge(s_dve0, N_DVE0)

            with act.Fori(0, B) as b:
                def modulate(i):
                    hold(act, s_xT, b * TPB + 4 * i + 4)
                    if i >= 2:
                        hold(act, s_zmm, b * TPB + 4 * (i - 1))
                    act.activation(hT[:, i % 2, :], bank[i % 2][:, :], ACT.Identity,
                                   bias=modc[:, 0, bass.ds(b, 1)], scale=modc[:, 1, bass.ds(b, 1)]).then_inc(s_hT, 1)

                modulate(0)
                for i in range(NBLK):
                    if i + 1 < NBLK:
                        modulate(i + 1)
                    for j in range(BT):
                        n, t = BT * i + j, BT * (NBLK - 1 - i) + j
                        pz = bank[5 + n % 3]
                        act.wait_ge(s_zmm, b * TPB + n + 1)
                        act.activation(zs[:, t, :], pz[:, 0:DI], ACT.Silu)
                        act.activation(dtr[:, t, :], pz[:, DI:ZW], ACT.Identity).then_inc(s_z, 1)
                act.wait_ge(s_spe, b * 4 + 1)
                act.activation(sp[:, 2, :], sp[:, 1, :], ACT.Exp, scale=-1.0).then_inc(s_spe, 1)
                act.wait_ge(s_spe, b * 4 + 3)
                act.activation(sp[:, 4, :], sp[:, 3, :], ACT.Ln).then_inc(s_spe, 1)
                act.wait_ge(s_pfx, b + 1)
                act.activation(etab[:, :, :], bank[5][:, 0:3 * NQ].rearrange("p (k c) -> p k c", k=3),
                               ACT.Exp).then_inc(s_etab, 1)
                phase_end(act, b, 0)

                def tap0(s):
                    d, k = step_of(s)
                    if s >= 1:
                        act.wait_ge(s_silu, b * STEPS + s)
                    for g in range(NG):
                        act.activation(acc[:, g, :], raw[:, g, HALO + k * BLK:HALO + (k + 1) * BLK], ACT.Identity,
                                       bias=cb[:, d, g:g + 1], scale=cw[:, d, g, KC - 1:KC]).then_inc(s_tap0, 1)

                def silu(s):
                    act.wait_ge(s_tap, b * STEPS * 9 + 9 * (s + 1))
                    if s >= 2:
                        act.wait_ge(s_tx, b * CHUNKS + BT * (s - 1))
                        act.wait_ge(s_yo, b * CHUNKS + BT * (s - 1))
                    for g in range(NH):
                        act.activation(cx[:, s % 2, g, :], acc[:, g, :], ACT.Silu)
                    act.activation(bT[:, s % 2, :], acc[0:NS, NH, :], ACT.Silu)
                    act.activation(cT[:, s % 2, :], acc[NS:2 * NS, NH, :], ACT.Silu).then_inc(s_silu, 1)

                def tokens_major(q):
                    d, t = chunk_of(q)
                    tx = bank[q % 2]
                    act.wait_ge(s_tx, b * CHUNKS + q + 1)
                    if q >= 2:
                        act.wait_ge(s_ys, b * CHUNKS + q - 1)
                        act.wait_ge(s_w, b * CHUNKS + q - 1)
                    act.activation(xt[:, q % 2, :], tx[:, 0:DI], ACT.Copy)
                    for h in range(NH):
                        last = act.activation(bs[:, q % 2, h, :], tx[:, DI:DI + NS], ACT.Copy, scale=wB[:, col(d, h, t)])
                    last.then_inc(s_xt, 1)

                def decays(q):
                    act.wait_ge(s_sg, b * CHUNKS + q + 1)
                    if q >= 2:
                        act.wait_ge(s_m, b * CHUNKS + q - 1)
                    act.activation(es[:, q % 2, :, :], bank[2 + q % 2][:, 0:DI].rearrange("p (h i) -> p h i", h=NH),
                                   ACT.Exp).then_inc(s_e, 1)

                def carried(q):
                    d, t = chunk_of(q)
                    act.wait_ge(s_yo, b * CHUNKS + q + 1)
                    if q >= 2:
                        act.wait_ge(s_wu, b * CHUNKS + q - 1)
                    for h in range(NH):
                        last = act.activation(us[:, q % 2, h * HD:(h + 1) * HD],
                                              bank[6 + q % 2][:, h * HD:(h + 1) * HD], ACT.Copy,
                                              scale=etab[:, 0, col(d, h, t)])
                    last.then_inc(s_u, 1)

                def squares(q):
                    d, t = chunk_of(q)
                    act.wait_ge(s_yz, b * CHUNKS + q + 1)
                    if q >= 1:
                        act.wait_ge(s_sq, b * CHUNKS + q)
                    act.activation(junk[:, :], yz[:, d, t, :], ACT.Square,
                                   accum_out=ssq[:, d, t:t + 1]).then_inc(s_sq, 1)

                tap0(0)
                silu(0)
                tap0(1)
                tokens_major(0)
                decays(0)
                for q in range(CHUNKS):
                    s, j = q // BT, q % BT
                    if q + 1 < CHUNKS:
                        tokens_major(q + 1)
                        decays(q + 1)
                    if q >= 2:
                        squares(q - 2)
                    carried(q)
                    if j == 2 and s + 1 < STEPS:
                        silu(s + 1)
                        if s + 2 < STEPS:
                            tap0(s + 2)
                squares(CHUNKS - 2)
                squares(CHUNKS - 1)
                phase_end(act, b, 1)

                hold(act, s_rn, b + 1)

                def forward(i):
                    if i >= 1:
                        act.wait_ge(s_ysum, b * NBLK + i)
                    for j in range(BT):
                        t = BT * i + j
                        last = act.activation(y1[:, j, :], yz[:, 0, t, :], ACT.Copy, scale=rn[:, 0, t:t + 1])
                    last.then_inc(s_y1, 1)

                def out_T(i):
                    act.wait_ge(s_yTm, b * NBLK + i + 1)
                    if i >= 1:
                        act.wait_ge(s_o, b * NBLK + i)
                    for k in range(2):
                        last = act.activation(yT[:, 2 * k:2 * k + 2, :], bank[k][:, :].rearrange("p (j c) -> p j c", j=2),
                                              ACT.Copy)
                    last.then_inc(s_yT, 1)

                forward(0)
                forward(1)
                out_T(0)
                for i in range(NBLK):
                    g = b * NBLK + i
                    if i + 1 < NBLK:
                        out_T(i + 1)
                    if i + 2 < NBLK:
                        forward(i + 2)
                    act.wait_ge(s_h2m, g + 1)
                    if i >= 1:
                        act.wait_ge(s_lgm, g)
                    act.activation(h2c, bank[4 + i % 2][:, :].rearrange("p (j c) -> p j c", j=BT), ACT.Copy).then_inc(s_h2c, 1)
                phase_end(act, b, 2)

            def rows_T(s, a, first):
                act.wait_ge(s_eT, s + 1)
                if not first:
                    act.wait_ge(s_h1, s - 1)
                act.activation(hTs[:, a, :], bank[a][:, 0:P], ACT.Copy).then_inc(s_eTc, 1)

            def rectify(s, a, first):
                act.wait_ge(s_hx, s + 1)
                if not first:
                    act.wait_ge(s_y2, s - 1)
                act.activation(hr[:, a, :], bank[4 + a][:, :], ACT.Relu).then_inc(s_hr, 1)

            rows_T(0, 0, True)
            rows_T(1, 1, True)
            for s in range(2):
                rows_T(s + 2, s % 2, False)
                rectify(s, s % 2, True)
            with act.Fori(1, (NSLOT - 2) // 2) as it:
                for a in range(2):
                    rows_T(2 * it + a + 2, a, False)
                    rectify(2 * it + a, a, False)
            for s in range((NSLOT - 2) // 2 * 2, NSLOT):
                if s + 2 < NSLOT:
                    rows_T(s + 2, s % 2, False)
                rectify(s, s % 2, False)

        @block.tensor
        def _(pe):
            pe.wait_ge(s_pool0, N_POOL0)
            pe.wait_ge(s_dve0, 1)
            for m in range(2):
                pe.matmul(bank[0][:, m * B:(m + 1) * B], wm[:, m * DM:(m + 1) * DM], csil[:, :], start=True, stop=True)
            for b in range(B):
                pe.matmul(bank[1 + 2 * b][:, 0:3 * DM], csil_bc[:, b, :], wm[:, 0:3 * DM], start=True, stop=True)
                last = pe.matmul(bank[2 + 2 * b][:, 0:3 * DM], csil_bc[:, b, :], wm[:, 3 * DM:6 * DM],
                                 start=True, stop=True)
            last.then_inc(s_pe0, 1)
            pe.wait_ge(s_dve0, N_DVE0)

            with pe.Fori(0, B) as b:
                def turn(i):
                    for j in range(BT):
                        n = BT * i + j
                        pe.wait_ge(s_xn, b * TPB + n + 1)
                        if i >= 2 and j == 0:
                            pe.wait_ge(s_hT, b * NBLK + i - 1)
                        pe.transpose(bank[i % 2][:, j * P:(j + 1) * P], xn[:, n % 4, :], ident[:, :]).then_inc(s_xT, 1)

                turn(0)
                for i in range(NBLK):
                    if i + 1 < NBLK:
                        turn(i + 1)
                    pe.wait_ge(s_hT, b * NBLK + i + 1)
                    for g in range(NG):
                        if i >= 1:
                            pe.wait_ge(s_raw, b * NBLK * NG + NG * (i - 1) + g + 1)
                        pe.matmul(bank[2 + g][:, :], wx[:, g * P:(g + 1) * P], hT[:, i % 2, :],
                                  start=True, stop=True).then_inc(s_rawmm, 1)
                    for j in range(BT):
                        n = BT * i + j
                        if n >= 3:
                            pe.wait_ge(s_z, b * TPB + n - 2)
                        pe.matmul(bank[5 + n % 3][:, 0:ZW], hT[:, i % 2, j * P:(j + 1) * P], wz[:, :],
                                  start=True, stop=True).then_inc(s_zmm, 1)
                pe.wait_ge(s_a, b + 1)
                W = NH * TPB
                for d in range(2):
                    for k, m in enumerate((incl[:, d, :], strict[:, d, :], ones[:, :])):
                        last = pe.matmul(bank[5][:, k * NQ + d * W:k * NQ + (d + 1) * W], m, av[:, d * W:(d + 1) * W],
                                         start=True, stop=True)
                last.then_inc(s_pfx, 1)
                phase_end(pe, b, 0)

                def prepare(q):
                    d, t = chunk_of(q)
                    s, j = q // BT, q % BT
                    c0 = (t % BT) * P
                    tx, sg = bank[q % 2], bank[2 + q % 2]
                    if j == 0:
                        pe.wait_ge(s_silu, b * STEPS + s + 1)
                    if q >= 2:
                        pe.wait_ge(s_xt, b * CHUNKS + q - 1)
                    for h in range(NH):
                        pe.transpose(tx[:, h * HD:(h + 1) * HD], cx[:, s % 2, h, c0:c0 + P], ident[:, :])
                    pe.transpose(tx[:, DI:DI + NS], bT[:, s % 2, c0:c0 + P], ident[0:NS, 0:NS]).then_inc(s_tx, 1)
                    if q >= 2:
                        pe.wait_ge(s_m, b * CHUNKS + q - 1)
                    pe.matmul(sg[:, DI:DI + P], bT[:, s % 2, c0:c0 + P], cT[:, s % 2, c0:c0 + P],
                              start=True, stop=True)
                    pe.matmul(sg[:, 0:DI], identb[:, :], negm[:, d, :, :].rearrange("p h i -> p (h i)"),
                              start=True, stop=False, skip_group_check=True)
                    pe.wait_ge(s_L, b * CHUNKS + q + 1)
                    for h in range(NH):
                        last = pe.matmul(sg[:, h * P:(h + 1) * P], lseg[:, q % 2, h, :], incl[:, d, :],
                                         start=False, stop=True, skip_group_check=True)
                    last.then_inc(s_sg, 1)

                def scan(q):
                    d, t = chunk_of(q)
                    s = q // BT
                    c0 = (t % BT) * P
                    ys, yo = bank[4 + q % 2], bank[6 + q % 2]
                    pe.wait_ge(s_xt, b * CHUNKS + q + 1)
                    pe.wait_ge(s_m, b * CHUNKS + q + 1)
                    if q >= 2:
                        pe.wait_ge(s_v, b * CHUNKS + q - 1)
                    for h in range(NH):
                        last = pe.matmul(ys[:, h * HD:(h + 1) * HD], ms[:, q % 2, h, :], xt[:, q % 2, h * HD:(h + 1) * HD],
                                         start=True, stop=True)
                    if q % TPB != TPB - 1:
                        for h in range(NH):
                            last = pe.matmul(ys[0:NS, DI + h * HD:DI + (h + 1) * HD], bs[:, q % 2, h, :],
                                             xt[:, q % 2, h * HD:(h + 1) * HD], start=True, stop=True)
                    last.then_inc(s_ys, 1)
                    if q >= 2:
                        pe.wait_ge(s_u, b * CHUNKS + q - 1)
                    if q >= 1:
                        pe.wait_ge(s_S, b * CHUNKS + q)
                    pe.matmul(yo[:, 0:DI], cT[:, s % 2, c0:c0 + P], st[:, q % 2, :], start=True,
                              stop=True).then_inc(s_yo, 1)

                prepare(0)
                for q in range(CHUNKS):
                    if q + 1 < CHUNKS:
                        prepare(q + 1)
                    scan(q)
                phase_end(pe, b, 1)

                def y_turn(i):
                    pe.wait_ge(s_ysum, b * NBLK + i + 1)
                    if i >= 1:
                        pe.wait_ge(s_yT, b * NBLK + i)
                    for j in range(BT):
                        for h in range(NH):
                            c0 = (j % 2) * DI + h * P
                            last = pe.transpose(bank[j // 2][:, c0:c0 + P], ysum[:, j, h * P:(h + 1) * P], ident[:, :])
                    last.then_inc(s_yTm, 1)

                def project(i):
                    pe.wait_ge(s_yT, b * NBLK + i + 1)
                    if i >= 2:
                        pe.wait_ge(s_o1, b * NBLK + i - 1)
                    for j in range(BT):
                        for h in range(NH):
                            last = pe.matmul(bank[2 + i % 2][:, j * DM:(j + 1) * DM], yT[:, j, h * P:(h + 1) * P],
                                             won[:, h, :], start=(h == 0), stop=(h == NH - 1))
                    last.then_inc(s_o, 1)

                def ranks(i):
                    pe.wait_ge(s_hot, b * NBLK + i + 1)
                    bk = bank[6 + i % 2]
                    W = BT * NE
                    hv = hot[:, i % 2].rearrange("p j e -> p (j e)")
                    pe.matmul(bk[:, W:2 * W], strict[:, 1, :], hv, start=True, stop=True)
                    pe.matmul(bk[:, 2 * W:3 * W], ones[:, :], hv, start=True, stop=True).then_inc(s_rank, 1)

                y_turn(0)
                project(0)
                for i in range(NBLK):
                    g = b * NBLK + i
                    if i + 1 < NBLK:
                        y_turn(i + 1)
                        project(i + 1)
                    if i >= 1:
                        ranks(i - 1)
                    pe.wait_ge(s_h2, g + 1)
                    if i >= 2:
                        pe.wait_ge(s_h2c, g - 1)
                    for j in range(BT):
                        last = pe.transpose(bank[4 + i % 2][:, j * P:(j + 1) * P], rows[:, (i % 2) * BT + j, 0:DM],
                                            ident[:, :])
                    last.then_inc(s_h2m, 1)
                    pe.wait_ge(s_h2c, g + 1)
                    if i >= 2:
                        pe.wait_ge(s_routed, g - 1)
                    for j in range(BT):
                        last = pe.matmul(bank[6 + i % 2][:, j * NE:(j + 1) * NE], h2c[:, j, :], gw[:, :],
                                         start=True, stop=True)
                    last.then_inc(s_lgm, 1)
                ranks(NBLK - 1)
                phase_end(pe, b, 2)

            pe.wait_ge(s_wf, 64)
            pe.wait_ge(s_tabv, 1)

            def turn_rows(s, a, k, rk, first):
                pe.wait_ge(s_rb[k], rk)
                if not first:
                    pe.wait_ge(s_eTc, s - 1)
                pe.transpose(bank[a][:, 0:P], rh[:, k, :], ident[:, :]).then_inc(s_eT, 1)

            def hidden(s, a, first, e):
                pe.wait_ge(s_eTc, s + 1)
                if not first:
                    pe.wait_ge(s_hb, s - 1)
                pe.matmul(bank[2 + a][:, :], hTs[:, a, :], w1s[:, bass.ds(e, 1), :].rearrange("p a f -> p (a f)"),
                          start=True, stop=True).then_inc(s_h1, 1)

            def turn_hidden(s, a, first):
                pe.wait_ge(s_hb, s + 1)
                if not first:
                    pe.wait_ge(s_hr, s - 1)
                for f in range(FC):
                    last = pe.transpose(bank[4 + a][:, f * P:(f + 1) * P], hb[:, a, f * P:(f + 1) * P], ident[:, :])
                last.then_inc(s_hx, 1)

            def down(s, a, first, e):
                pe.wait_ge(s_hr, s + 1)
                if not first:
                    pe.wait_ge(s_yo1, s - 1)
                for f in range(FC):
                    last = pe.matmul(bank[6 + a][:, 0:DM], hr[:, a, f * P:(f + 1) * P],
                                     w2s[:, bass.ds(e, 1), f, :].rearrange("p a c -> p (a c)"),
                                     start=(f == 0), stop=(f == FC - 1))
                last.then_inc(s_y2, 1)

            def expert_of(s):
                return pe.value_load(slot_r[0:1, 1, bass.ds(s, 1)], min_val=0, max_val=NE - 1)

            def pe_step(r, k, it):
                if it is None:
                    eh = expert_of(r + 1) if 0 <= r + 1 < NSLOT else None
                    ed = expert_of(r - 1) if r >= 1 else None
                    if r + 2 < NSLOT:
                        turn_rows(r + 2, r % 2, (r + 2) % 4, 32 * ((r + 2) // 4) + 32, r < 0)
                    if 0 <= r + 1 < NSLOT:
                        hidden(r + 1, (r + 1) % 2, r + 1 < 2, eh)
                    if 0 <= r < NSLOT:
                        turn_hidden(r, r % 2, r < 2)
                    if r >= 1:
                        down(r - 1, (r - 1) % 2, r - 1 < 2, ed)
                else:
                    eh, ed = expert_of(r + 1), expert_of(r - 1)
                    turn_rows(r + 2, k % 2, (k + 2) % 4, 32 * it + 32 * ((k + 2) // 4) + 32, False)
                    hidden(r + 1, (k + 1) % 2, False, eh)
                    turn_hidden(r, k % 2, False)
                    down(r - 1, (k + 1) % 2, False, ed)

            for r in range(-2, 4):
                pe_step(r, 0, None)
            with pe.Fori(1, (NSLOT - 2) // 4) as it:
                for k in range(4):
                    pe_step(4 * it + k, k, it)
            for r in range((NSLOT - 2) // 4 * 4, NSLOT + 1):
                pe_step(r, 0, None)

        @block.vector
        def _(dve):
            dve.wait_ge(s_act0, 2)
            dve.wait_ge(s_load, NLOAD)
            dve.wait_ge(s_pool0, N_POOL0)
            n0 = [0]

            def link0(ins):
                n0[0] += 1
                ins.then_inc(s_dve0, 1)
                dve.wait_ge(s_dve0, n0[0])

            for b in range(B):
                last = dve.tensor_scalar(csil_bc[:, b, :], ones[:, :], csil[:, b:b + 1], None, ALU.mult)
            link0(last)
            for h in range(NH):
                dve.tensor_scalar(won[:, h, :], wo[:, h, :], nw[:, h:h + 1], None, ALU.mult)
            dve.tensor_tensor(gb_sum[:, :], gbias[:, 0, :], gbias[:, 1, :], ALU.add)
            link0(dve.tensor_scalar(sp[:, 0, 0:2 * NH], ab[:, :, 0], -1.0, None, ALU.mult))
            for k in range(2 * NH):
                last = dve.tensor_scalar(ab[:, k, :], ones[:, 0:TPB], sp[:, 0, k:k + 1], None, ALU.mult)
            for g in range(NG):
                dve.memset(raw[:, g, 0:HALO], 0.0)
                dve.memset(raw[:, g, HALO + L:HALO + L + HALO], 0.0)
            link0(dve.memset(st[:, 0, :], 0.0))
            dve.wait_ge(s_pe0, 1)
            dve.tensor_copy(modc[:, 0, :], bank[0][:, 0:B])
            link0(dve.tensor_scalar(modc[:, 1, :], bank[0][:, B:2 * B], 1.0, None, ALU.add))
            for b in range(B):
                dve.tensor_copy(row[:, b, 0:3, :], bank[1 + 2 * b][:, 0:3 * DM].rearrange("p (k c) -> p k c", k=3))
                last = dve.tensor_copy(row[:, b, 3:6, :], bank[2 + 2 * b][:, 0:3 * DM].rearrange("p (k c) -> p k c", k=3))
            link0(last)
            for b in range(B):
                last = dve.tensor_scalar(row[:, b, 4, :], row[:, b, 4, :], 1.0, None, ALU.add)
            link0(last)
            for b in range(B):
                g2 = row[:, b, 2:6:3, :]
                link0(dve.tensor_scalar(gtmp[:, b], g2, -1.0, None, ALU.mult))
                link0(dve.tensor_tensor(gtmp[:, b], gtmp[:, b], g2, ALU.max))
                link0(dve.tensor_scalar(gtmp[:, b], gtmp[:, b], 0.25, None, ALU.max))
                link0(dve.tensor_scalar(g2, g2, 0.0, 2.0, ALU.is_ge, ALU.mult))
            for b in range(B):
                g2 = row[:, b, 2:6:3, :]
                last = dve.scalar_tensor_tensor(out=g2, in0=g2, scalar=-1.0, in1=gtmp[:, b], op0=ALU.add, op1=ALU.mult)
            last.then_inc(s_dve0, N_DVE0 - n0[0])
            dve.wait_ge(s_dve0, N_DVE0)
            dve.wait_ge(s_x, 64)

            with dve.Fori(0, B) as b:
                for t in range(TPB):
                    dve.bn_stats(stat[:, t, :], xs[:, b * TPB + t, :]).then_inc(s_st, 1)
                for t in range(TPB):
                    hold(dve, s_st, b * TPB + t + 1)
                    dve.bn_aggr(mv[:, t, :], stat[:, t, :]).then_inc(s_mv, 1)
                dve.wait_ge(s_rstd, b + 1)

                def normed(i):
                    for j in range(BT):
                        n, t = BT * i + j, BT * (NBLK - 1 - i) + j
                        if n >= 4:
                            dve.wait_ge(s_xT, b * TPB + n - 3)
                        dve.tensor_scalar(xn[:, n % 4, :], xs[:, b * TPB + t, :], mv[:, t, 0:1], rstd[:, t:t + 1],
                                          ALU.subtract, ALU.mult).then_inc(s_xn, 1)

                normed(0)
                for i in range(NBLK):
                    k = NBLK - 1 - i
                    if i + 1 < NBLK:
                        normed(i + 1)
                    for g in range(NG):
                        dve.wait_ge(s_rawmm, b * NBLK * NG + NG * i + g + 1)
                        dve.tensor_copy(raw[:, g, HALO + k * BLK:HALO + (k + 1) * BLK], bank[2 + g][:, :]).then_inc(s_raw, 1)

                NL = 7
                cnt = [0]

                def link(ins):
                    cnt[0] += 1
                    ins.then_inc(s_dve, 1)
                    dve.wait_ge(s_dve, b * NL + cnt[0])

                dve.wait_ge(s_z, b * TPB + TPB)
                for d in range(2):
                    last = dve.tensor_tensor(sp[:, 0, d * NH * TPB:(d + 1) * NH * TPB].rearrange("p (h t) -> p h t", h=NH),
                                             dtr[:, :, :].rearrange("p t h -> p h t"), biasb[:, d * NH:(d + 1) * NH, :],
                                             ALU.add)
                link(last)
                link(dve.tensor_scalar(sp[:, 5, :], sp[:, 0, :], -1.0, None, ALU.mult))
                dve.tensor_tensor(sp[:, 1, :], sp[:, 0, :], sp[:, 5, :], ALU.max).then_inc(s_spe, 1)
                dve.wait_ge(s_spe, b * 4 + 2)
                dve.tensor_scalar(sp[:, 3, :], sp[:, 2, :], 1.0, None, ALU.add).then_inc(s_spe, 1)
                dve.wait_ge(s_spe, b * 4 + 4)
                link(dve.tensor_scalar(sp[:, 5, :], sp[:, 3, :], -1.0, None, ALU.add))
                link(dve.tensor_scalar(sp[:, 6, :], sp[:, 5, :], 0.0, None, ALU.is_equal))
                link(dve.tensor_tensor(sp[:, 5, :], sp[:, 5, :], sp[:, 6, :], ALU.add))
                dve.reciprocal(sp[:, 7, :], sp[:, 5, :])
                dve.tensor_tensor(sp[:, 4, :], sp[:, 4, :], sp[:, 2, :], ALU.mult)
                link(dve.tensor_tensor(sp[:, 6, :], sp[:, 6, :], sp[:, 2, :], ALU.mult))
                dve.tensor_tensor(sp[:, 4, :], sp[:, 4, :], sp[:, 7, :], ALU.mult)
                link(dve.tensor_scalar(sp[:, 0, :], sp[:, 0, :], 0.0, None, ALU.max))
                assert cnt[0] == NL
                dve.tensor_tensor(sp[:, 4, :], sp[:, 4, :], sp[:, 6, :], ALU.add).then_inc(s_wB, 1)
                dve.wait_ge(s_wB, b * 4 + 1)
                dve.tensor_tensor(dtv[:, :], sp[:, 4, :], sp[:, 0, :], ALU.add).then_inc(s_wB, 1)
                dve.wait_ge(s_wB, b * 4 + 2)
                dve.tensor_tensor(av[:, :], dtv[:, :], ab[:, :, :].rearrange("p k t -> p (k t)"), ALU.mult).then_inc(s_a, 1)
                dve.wait_ge(s_etab, b + 1)
                dve.tensor_tensor(wB[:, :], etab[:, 1, :], dtv[:, :], ALU.mult).then_inc(s_wB, 2)
                phase_end(dve, b, 0)

                def taps(s, k):
                    d, blk = step_of(s)
                    off = (k - HALO) * (1 - 2 * d)
                    n = HALO - 1 - k
                    c0 = HALO + blk * BLK + off
                    for g in range(NG):
                        if n == 0:
                            dve.wait_ge(s_tap0, b * STEPS * NG + s * NG + g + 1)
                        else:
                            dve.wait_ge(s_tap, b * STEPS * 9 + 9 * s + 3 * (n - 1) + g + 1)
                        dve.scalar_tensor_tensor(out=acc[:, g, :], in0=raw[:, g, c0:c0 + BLK],
                                                 scalar=cw[:, d, g, k:k + 1], in1=acc[:, g, :],
                                                 op0=ALU.mult, op1=ALU.add).then_inc(s_tap, 1)

                def mix(q):
                    d, t = chunk_of(q)
                    dve.wait_ge(s_e, b * CHUNKS + q + 1)
                    if q >= 2:
                        dve.wait_ge(s_ys, b * CHUNKS + q - 1)
                    for h in range(NH):
                        last = dve.scalar_tensor_tensor(out=ms[:, q % 2, h, :], in0=es[:, q % 2, h, :],
                                                        scalar=dtv[:, col(d, h, t)], in1=bank[2 + q % 2][:, DI:DI + P],
                                                        op0=ALU.mult, op1=ALU.mult)
                    last.then_inc(s_m, 1)

                def carry(q):
                    d, t = chunk_of(q)
                    if q >= 1:
                        dve.wait_ge(s_yo, b * CHUNKS + q)
                    if q % TPB == TPB - 1:
                        dve.memset(st[:, (q + 1) % 2, :], 0.0).then_inc(s_S, 1)
                        return
                    for h in range(NH):
                        cs = slice(h * HD, (h + 1) * HD)
                        last = dve.scalar_tensor_tensor(out=st[:, (q + 1) % 2, cs], in0=st[:, q % 2, cs],
                                                        scalar=etab[0:NS, 2, col(d, h, t)],
                                                        in1=bank[4 + q % 2][0:NS, DI + h * HD:DI + (h + 1) * HD],
                                                        op0=ALU.mult, op1=ALU.add)
                    last.then_inc(s_S, 1)

                for k in (2, 1, 0):
                    taps(0, k)
                mix(0)
                for q in range(CHUNKS):
                    d, t = chunk_of(q)
                    s, j = q // BT, q % BT
                    if j < 3 and s + 1 < STEPS:
                        taps(s + 1, 2 - j)
                    if q + 1 < CHUNKS:
                        mix(q + 1)
                    dve.wait_ge(s_ys, b * CHUNKS + q + 1)
                    if q >= 1:
                        dve.wait_ge(s_S, b * CHUNKS + q)
                    carry(q)
                    dve.wait_ge(s_wu, b * CHUNKS + q + 1)
                    dve.tensor_tensor(vs[:, q % 2, :], bank[4 + q % 2][:, 0:DI], ws[:, q % 2, :], ALU.add).then_inc(s_v, 1)
                    dve.wait_ge(s_v, b * CHUNKS + q + 1)
                    dve.tensor_tensor(yz[:, d, t, :], vs[:, q % 2, :], zs[:, t, :], ALU.mult).then_inc(s_yz, 1)
                phase_end(dve, b, 1)

                dve.wait_ge(s_rn, b + 1)

                def both(i):
                    dve.wait_ge(s_y1, b * NBLK + i + 1)
                    if i >= 1:
                        dve.wait_ge(s_yTm, b * NBLK + i)
                    for j in range(BT):
                        t = BT * i + j
                        last = dve.scalar_tensor_tensor(out=ysum[:, j, :], in0=yz[:, 1, t, :], scalar=rn[:, 1, t:t + 1],
                                                        in1=y1[:, j, :], op0=ALU.mult, op1=ALU.add)
                    last.then_inc(s_ysum, 1)

                def step(g, ins, n):
                    ins.then_inc(s_rt_dve, 1)
                    dve.wait_ge(s_rt_dve, NR * g + n)

                def choose(i):
                    g, a = b * NBLK + i, i % 2
                    wide = [P, BT, NE]
                    dve.wait_ge(s_lgm, g + 1)
                    step(g, dve.tensor_tensor(lg[:, :, :], bank[6 + a][:, 0:BT * NE].rearrange("p (j e) -> p j e", j=BT),
                                              gb_sum[:, :].unsqueeze(1).broadcast_to(wide), ALU.add), 1)
                    step(g, dve.tensor_reduce(mx[:, 0, :], lg[:, :, :], AX_X, ALU.max), 2)
                    step(g, dve.tensor_tensor(cand[:, :, :], lg[:, :, :], mx[:, 0, :].unsqueeze(2).broadcast_to(wide),
                                              ALU.is_equal), 3)
                    step(g, dve.tensor_tensor(cand[:, :, :], cand[:, :, :],
                                              rank8[:, :].unsqueeze(1).broadcast_to(wide), ALU.mult), 4)
                    step(g, dve.tensor_reduce(mx[:, 1, :], cand[:, :, :], AX_X, ALU.max), 5)
                    dve.tensor_tensor(hot[:, a, :, :], cand[:, :, :], mx[:, 1, :].unsqueeze(2).broadcast_to(wide),
                                      ALU.is_equal).then_inc(s_hot, 1)

                def place(i):
                    g, a = b * NBLK + i, i % 2
                    W = BT * NE
                    rank = bank[6 + a][:, W:2 * W].rearrange("p (j e) -> p j e", j=BT)
                    total = bank[6 + a][:, 2 * W:3 * W].rearrange("p (j e) -> p j e", j=BT)
                    dve.wait_ge(s_rank, g + 1)
                    for j in range(BT - 1):
                        step(g, dve.tensor_tensor(nextrow[:, a, j + 1, :], total[:, j, :], nextrow[:, a, j, :], ALU.add),
                             6 + j)
                    step(g, dve.tensor_tensor(nextrow[:, 1 - a, 0, :], total[:, BT - 1, :], nextrow[:, a, BT - 1, :],
                                              ALU.add), 5 + BT)
                    dve.tensor_tensor(pos[:, :, :], rank, nextrow[:, a, :, :], ALU.add).then_inc(s_routed, 1)
                    dve.wait_ge(s_routed, g + 1)
                    step(g, dve.tensor_tensor(pos[:, :, :], pos[:, :, :], hot[:, a, :, :], ALU.mult), 6 + BT)
                    step(g, dve.tensor_reduce(posf[:, :], pos[:, :, :], AX_X, ALU.add), 7 + BT)
                    if i >= 2:
                        for j in range(BT):
                            dve.wait_ge(s_scat[a * BT + j], b * 32 + 16 * (i // 2))
                    dve.tensor_copy(rowat[:, a * BT:(a + 1) * BT, :].rearrange("p j c -> p (j c)"),
                                    posf[:, :]).then_inc(s_pos, 1)

                both(0)
                for i in range(NBLK):
                    g, a = b * NBLK + i, i % 2
                    sl = slice(a * BT, (a + 1) * BT)
                    if i + 1 < NBLK:
                        both(i + 1)
                    dve.wait_ge(s_o, g + 1)
                    dve.tensor_tensor(o1, bank[2 + a][:, :].rearrange("p (j c) -> p j c", j=BT),
                                      row[:, b, 2, :].unsqueeze(1).broadcast_to([P, BT, DM]), ALU.mult).then_inc(s_o1, 1)
                    dve.wait_ge(s_o1, g + 1)
                    if i >= 2:
                        for j in range(BT):
                            dve.wait_ge(s_scat[a * BT + j], b * 32 + 16 * (i // 2))
                    dve.tensor_tensor(rows[:, sl, DM:2 * DM], xs[:, bass.ds(BT * g, BT), :], o1, ALU.add).then_inc(s_x1r, 1)
                    dve.wait_ge(s_x1r, g + 1)
                    for j in range(BT):
                        dve.bn_stats(st2[:, j, :], rows[:, a * BT + j, DM:2 * DM]).then_inc(s_st2, 1)
                    for j in range(BT):
                        hold(dve, s_st2, BT * g + j + 1)
                        last = dve.bn_aggr(mv2[:, a, j, :], st2[:, j, :])
                    last.then_inc(s_mv2, 1)
                    if i >= 1:
                        choose(i - 1)
                        place(i - 1)
                    dve.wait_ge(s_rs2, g + 1)
                    for j in range(BT):
                        last = dve.tensor_scalar(xn2[:, j, :], rows[:, a * BT + j, DM:2 * DM], mv2[:, a, j, 0:1],
                                                 rs2[:, a, j:j + 1], ALU.subtract, ALU.mult)
                    last.then_inc(s_xn2, 1)
                    dve.wait_ge(s_xn2, g + 1)
                    dve.tensor_tensor(rows[:, sl, 0:DM], xn2, row[:, b, 4, :].unsqueeze(1).broadcast_to([P, BT, DM]),
                                      ALU.mult).then_inc(s_h2a, 1)
                choose(NBLK - 1)
                place(NBLK - 1)
                phase_end(dve, b, 2)

            nt = [0]

            def tab(ins):
                nt[0] += 1
                ins.then_inc(s_tab, 1)
                dve.wait_ge(s_tab, 2 + nt[0])

            dve.wait_ge(s_tab, 2)
            dve.tensor_tensor(count[:, :], nextrow[:, 0, 0, :], region0[:, :], ALU.subtract).then_inc(s_gd, 1)
            dve.wait_ge(s_gd, 1)
            dve.tensor_scalar(padf, nextrow[:, 0, 0, :], pcol[:, 0:1], None, ALU.add)
            for e in range(NE):
                last = dve.tensor_scalar(tiles_gt[:, e, :], m128, count[:, e:e + 1], None, ALU.is_lt)
            tab(last)
            tab(dve.tensor_reduce(ntile, tiles_gt, AX_X, ALU.add))
            dve.tensor_scalar(coef, ntile, -float(P), float(REGION), ALU.mult, ALU.add)
            tab(dve.tensor_copy(cum[:, 0:1], ntile[:, 0:1]))
            dve.tensor_copy(padi, padf).then_inc(s_padi, 1)
            for e in range(1, NE):
                tab(dve.tensor_tensor(cum[:, e:e + 1], cum[:, e - 1:e], ntile[:, e:e + 1], ALU.add))
            for e in range(NE):
                dve.tensor_scalar(behind[:, 0, e, :], slot_i, cum[:, e:e + 1], coef[:, e:e + 1], ALU.is_ge, ALU.mult)
                last = dve.tensor_scalar(behind[:, 1, e, :], slot_i, cum[:, e:e + 1], None, ALU.is_ge)
            tab(last)
            for k in range(2):
                last = dve.tensor_reduce(slot_v[:, k, :], behind[:, k].rearrange("p e s -> p s e"), AX_X, ALU.add)
            tab(last)
            tab(dve.scalar_tensor_tensor(out=slot_v[:, 0, :], in0=slot_i, scalar=float(P), in1=slot_v[:, 0, :],
                                         op0=ALU.mult, op1=ALU.add))
            dve.tensor_scalar(slot_v[:, 0, :], slot_v[:, 0, :], float(NE * REGION), None, ALU.min)
            tab(dve.tensor_scalar(slot_v[:, 1, :], slot_v[:, 1, :], float(NE - 1), None, ALU.min))
            dve.tensor_copy(slot_r, slot_v).then_inc(s_tabv, 1)
            dve.wait_ge(s_tabv, 1)
            dve.tensor_tensor(gdiff, row[:, 1, 5, :], row[:, 0, 5, :], ALU.subtract).then_inc(s_gd, 1)
            dve.wait_ge(s_gd, 2)
            dve.wait_ge(s_wf, 64)

            def bias1(s, a, first):
                e = dve.value_load(slot_r[0:1, 1, bass.ds(s, 1)], min_val=0, max_val=NE - 1)
                dve.wait_ge(s_h1, s + 1)
                if not first:
                    dve.wait_ge(s_hx, s - 1)
                dve.tensor_tensor(hb[:, a, :], bank[2 + a][:, :], b1s[:, bass.ds(e, 1), :].rearrange("p a f -> p (a f)"),
                                  ALU.add).then_inc(s_hb, 1)

            def combine(s, a, k, rk, first, put16):
                e = dve.value_load(slot_r[0:1, 1, bass.ds(s, 1)], min_val=0, max_val=NE - 1)
                dve.wait_ge(s_rb[k], rk)
                dve.tensor_scalar(flag[:, a, :], xr[:, bass.ds(s, 1), DM:DM + 1].rearrange("p a c -> p (a c)"),
                                  float(L), None, ALU.is_ge).then_inc(s_flag, 1)
                dve.wait_ge(s_y2, s + 1)
                dve.tensor_tensor(yo1[:, a, :], bank[6 + a][:, 0:DM], b2s[:, bass.ds(e, 1), :].rearrange("p a c -> p (a c)"),
                                  ALU.add).then_inc(s_yo1, 1)
                dve.wait_ge(s_flag, s + 1)
                dve.scalar_tensor_tensor(out=gsel[:, a, :], in0=gdiff, scalar=flag[:, a, :],
                                         in1=row[:, 0, 5, :], op0=ALU.mult, op1=ALU.add).then_inc(s_gs, 1)
                dve.wait_ge(s_yo1, s + 1)
                dve.wait_ge(s_gs, s + 1)
                dve.tensor_tensor(yo2[:, a, :], yo1[:, a, :], gsel[:, a, :], ALU.mult).then_inc(s_yo2, 1)
                dve.wait_ge(s_yo2, s + 1)
                if not first:
                    dve.wait_ge(s_out[k], put16)
                dve.tensor_tensor(ob[:, k, :], yo2[:, a, :], xr[:, bass.ds(s, 1), 0:DM].rearrange("p a c -> p (a c)"),
                                  ALU.add).then_inc(s_ob, 1)

            def dve_step(r, k, it):
                if it is None:
                    if 0 <= r + 1 < NSLOT:
                        bias1(r + 1, (r + 1) % 2, r + 1 < 2)
                    if r >= 1:
                        combine(r - 1, (r - 1) % 2, (r - 1) % 4, 32 * ((r - 1) // 4) + 32, r - 1 < 4, 16 * ((r - 1) // 4))
                else:
                    bias1(r + 1, (k + 1) % 2, False)
                    combine(r - 1, (k + 1) % 2, (k + 3) % 4, 32 * it + 32 * ((k + 3) // 4), False,
                            16 * it + 16 * ((k + 3) // 4) - 16)

            for r in range(-1, 8):
                dve_step(r, 0, None)
            with dve.Fori(2, (NSLOT - 1) // 4) as it:
                for k in range(4):
                    dve_step(4 * it + k, k, it)
            for r in range((NSLOT - 1) // 4 * 4, NSLOT + 1):
                dve_step(r, 0, None)



_INS = ["u", "w_xbc", "w_zdt", "conv_w", "conv_b", "dt_bias", "a_log", "d_skip", "norm_w", "w_out", "gate_w", "gate_b",
        "w1", "b1", "w2", "b2", "c_t", "wmod"]


def kernel(**inputs):
    import numpy as _np
    import concourse.bacc as _bacc
    from concourse import mybir as _mybir
    from concourse.bass_utils import run_bass_kernel_spmd as _run

    x = {k: _np.asarray(v) for k, v in inputs.items()}
    wi = x["L0_attn_in_proj_w"]

    def channels(fw, bw):
        return _np.stack([v.reshape((NG, P) + v.shape[1:]) for v in (fw, bw)]).swapaxes(0, 2).swapaxes(1, 2)

    laid = {
        "u": x["L0_attn_u"],
        "w_xbc": wi[DI:DI + NG * P].T,
        "w_zdt": _np.concatenate([wi[0:DI], wi[DI + NG * P:]]).T,
        "conv_w": channels(x["L0_attn_conv_w"], x["L0_attn_conv_w_bw"]),
        "conv_b": channels(x["L0_attn_conv_b"], x["L0_attn_conv_b_bw"]),
        "dt_bias": _np.concatenate([x["L0_attn_dt_bias"], x["L0_attn_dt_bias_bw"]]),
        "a_log": _np.concatenate([x["L0_attn_A_log"], x["L0_attn_A_b_log"]]),
        "d_skip": _np.concatenate([x["L0_attn_D"], x["L0_attn_D_b"]]),
        "norm_w": x["L0_attn_norm_w"].reshape(NH, HD).T,
        "w_out": x["L0_attn_out_proj_w"].T.reshape(NH, HD, DM).swapaxes(0, 1),
        "gate_w": x["L0_ffn_gate_w"].T,
        "gate_b": _np.stack([x["L0_ffn_gate_b"], x["L0_ffn_expert_bias"]]),
        "w1": x["L0_ffn_w1"].transpose(1, 0, 2),
        "b1": x["L0_ffn_b1"],
        "w2": x["L0_ffn_w2"].reshape(NE, FC, P, DM).transpose(2, 0, 1, 3),
        "b2": x["L0_ffn_b2"],
        "c_t": x["L0_c"].T,
        "wmod": x["L0_wmod"],
    }
    nc = _bacc.Bacc("TRN2", target_bir_lowering=False, num_devices=1)
    arrays, args = {}, []
    for name in _INS:
        a = _np.ascontiguousarray(laid[name])
        arrays[f"in_{name}_dram"] = a
        args.append(nc.dram_tensor(f"in_{name}_dram", a.shape, _mybir.dt.from_np(a.dtype), kind="ExternalInput").ap())
    args.append(nc.dram_tensor("out_0_dram", (B, L, DM), F32, kind="ExternalOutput").ap())
    build(nc, *args)
    r = _run(nc, [arrays], core_ids=[0])
    return r.results[0]["out_0_dram"]
```

```python
from contextlib import ExitStack

import numpy as np

import concourse.bass as bass
from concourse import mybir

F32 = mybir.dt.float32
BF16 = mybir.dt.bfloat16
ALU = mybir.AluOpType
ACT = mybir.ActivationFunctionType
AX_X = mybir.AxisListType.X

P = 128
B, L, DM = 2, 2048, 128
NH, HD, NS = 2, 128, 64
DI = NH * HD
KC = 4
HALO = KC - 1
NE, FF = 8, 512
EPS = 1e-5
TPB = L // P
BT = 4
BLK = BT * P
NBLK = TPB // BT
NG = 3
STEPS = 2 * NBLK
CHUNKS = STEPS * BT
NDT = NH
ZW = DI + NDT
FC = FF // P
MASKED = -30000.0
NTOK = B * L
REGION = NTOK + P
NSLOT = NTOK // P + NE - 1
ROW = 2 * DM + 4


def step_of(s):
    return (1, NBLK - 1 - s) if s < NBLK else (0, s - NBLK)


def chunk_of(q):
    return (1, TPB - 1 - q) if q < TPB else (0, q - TPB)


def build(nc, u, w_xbc, w_zdt, conv_w, conv_b, dt_bias, a_log, d_skip, norm_w, w_out, gate_w, gate_b,
          w1, b1, w2, b2, c_t, wmod, out):
    ctx = ExitStack()
    with ctx:
        def sb(name, shape, dt=F32):
            return ctx.enter_context(nc.sbuf_tensor(name, shape, dt))

        def sem(name):
            return ctx.enter_context(nc.semaphore(name))

        bank = [ctx.enter_context(nc.psum_tensor(f"bank{i}", [P, 512], F32)) for i in range(8)]

        wx = sb("wx", [P, NG * P])
        wz = sb("wz", [P, ZW])
        cw = sb("cw", [P, 2, NG, KC])
        cb = sb("cb", [P, 2, NG])
        dtb = sb("dtb", [P, 2 * NH])
        alog = sb("alog", [P, 2 * NH])
        dsk = sb("dsk", [P, 2 * NH])
        nw = sb("nw", [P, NH])
        won = sb("won", [P, NH, DM])
        gw = sb("gw", [P, NE])
        gbias = sb("gbias", [P, 2, NE])
        gb_sum = sb("gb_sum", [P, NE])
        ct_in = sb("ct_in", [P, B])
        csil = sb("csil", [P, B])
        modc = sb("modc", [P, 2, B])
        row = sb("row", [P, B, 6, DM])
        ident = sb("ident", [P, P])
        identb = sb("identb", [P, P], BF16)
        incl = sb("incl", [P, 2, P])
        strict = sb("strict", [P, 2, P])
        negm = sb("negm", [P, 2, 2, P], BF16)
        ones = sb("ones", [P, P])
        w1s = sb("w1s", [P, NE, FF])
        w2s = sb("w2s", [P, NE, FC, DM])
        b2s = sb("b2s", [P, NE, DM])
        padrow = sb("padrow", [P, ROW])
        pcol = sb("pcol", [P, 1])

        xs = sb("xs", [P, B * TPB, DM])
        ids = sb("ids", [P, B * TPB])
        count = sb("count", [P, NE])
        nextrow = sb("nextrow", [P, 2, BT, NE])
        region0 = sb("region0", [P, NE])

        ARENA = sb("arena", [P, 2 * TPB * DI + NG * (L + 2 * HALO)])
        yz = ARENA[:, 0:2 * TPB * DI].rearrange("p (d t c) -> p d t c", d=2, t=TPB)
        raw = ARENA[:, 2 * TPB * DI:].rearrange("p (g c) -> p g c", g=NG)
        wm = ARENA[:, 0:6 * DM]
        wo = ARENA[:, 6 * DM:8 * DM].rearrange("p (h c) -> p h c", h=NH)
        gtmp = ARENA[:, 8 * DM:12 * DM].rearrange("p (b k c) -> p b k c", b=B, k=2)
        erow = ARENA[0:3 * NH * TPB, 12 * DM:12 * DM + 5 * P].rearrange("p (k c) -> p k c", k=5)
        xn = ARENA[:, 20 * DM:24 * DM].rearrange("p (k c) -> p k c", k=4)
        sp = ARENA[:, 24 * DM:24 * DM + 8 * 2 * NH * TPB].rearrange("p (k c) -> p k c", k=8)
        e0rep = ARENA[:, 32 * DM:32 * DM + 2 * 3 * NH * TPB].rearrange("p (d c k) -> p d c k", d=2, c=3)
        csil_bc = ARENA[:, 38 * DM:40 * DM].rearrange("p (b c) -> p b c", b=B)
        esplit = ARENA[0:3 * NH * TPB, 40 * DM:41 * DM].bitcast(BF16).rearrange("p (k c) -> p k c", k=2)
        zs = sb("zs", [P, TPB, DI])
        stat = sb("stat", [P, TPB, 6])
        mv = sb("mv", [P, TPB, 2])
        ve = sb("ve", [P, TPB])
        rstd = sb("rstd", [P, TPB])
        mhalf = sb("mhalf", [P, 2 * TPB])
        dtr = sb("dtr", [P, TPB, NDT])
        NQ = 2 * NH * TPB
        biasb = sb("biasb", [P, 2 * NH, TPB])
        ab = sb("ab", [P, 2 * NH, TPB])
        dtv = sb("dtv", [P, NQ])
        av = sb("av", [P, NQ])
        etab = sb("etab", [P, 2, NQ])
        wB = sb("wB", [P, NQ])
        ssq = sb("ssq", [P, 2, TPB])
        rn = sb("rn", [P, 2, TPB])
        rt = sb("rt", [P, 2, TPB])

        hT = sb("hT", [P, 2, BLK])
        acc = sb("acc", [P, NG, BLK])
        accb = sb("accb", [P, BLK])
        acc_bc = (acc[:, NH, :], accb[:, :])
        cx = sb("cx", [P, 2, NH, BLK])
        bc = sb("bc", [P, 2, BLK])
        cc = sb("cc", [P, 2, BLK])
        cs = sb("cs", [P, 2, P])
        lseg = sb("lseg", [P, 2, NH, P])
        TM = 3
        xt = sb("xt", [P, TM, DI])
        bs = sb("bs", [P, TM, NH, NH, NS])
        es = sb("es", [P, 2, NH, P])
        ms = sb("ms", [P, 2, NH, P])
        st = sb("st", [P, 2, DI])
        etot = sb("etot", [P, 2, TPB])
        eparts = sb("eparts", [3 * NH * TPB, 2, P], BF16)
        pick = sb("pick", [3 * NH * TPB, TPB, P], BF16)
        ws = sb("ws", [P, TM, DI])
        vs = sb("vs", [P, 2, DI])
        junk = sb("junk", [P, DI])
        prod = sb("prod", [P, BLK])
        y1 = cx[:, 0].rearrange("p g c -> p (g c)").rearrange("p (j c) -> p j c", j=BT)
        ysum = cx[:, 1].rearrange("p g c -> p (g c)").rearrange("p (j c) -> p j c", j=BT)
        yT = acc[:, 0:2].rearrange("p g c -> p (g c)").rearrange("p (j c) -> p j c", j=BT)
        o1 = acc[:, 2].rearrange("p (j c) -> p j c", j=BT)
        xn2 = es[:, :].rearrange("p a h c -> p (a h) c")
        h2c = ms[:, :].rearrange("p a h c -> p (a h) c")
        rows = sb("rows", [P, 2 * BT, ROW])
        rowat = sb("rowat", [P, 2 * BT, 1], mybir.dt.int32)
        st2 = sb("st2", [P, BT, 6])
        mv2 = sb("mv2", [P, 2, BT, 2])
        ve2 = sb("ve2", [P, BT])
        rs2 = sb("rs2", [P, 2, BT])
        lg = sb("lg", [P, BT, NE])
        mx = sb("mx", [P, 2, BT])
        hot = sb("hot", [P, 2, BT, NE])
        pos = sb("pos", [P, BT, NE])
        posf = sb("posf", [P, BT])
        rank8 = sb("rank8", [P, NE])
        cand = sb("cand", [P, BT, NE])

        s_load = sem("s_load")
        s_x = sem("s_x")
        s_wf = sem("s_wf")
        s_pool0 = sem("s_pool0")
        s_act0 = sem("s_act0")
        s_pe0 = sem("s_pe0")
        s_dve0 = sem("s_dve0")
        s_phase = sem("s_phase")
        s_st = sem("s_st")
        s_mv = sem("s_mv")
        s_ve = sem("s_ve")
        s_rstd = sem("s_rstd")
        s_xn = sem("s_xn")
        s_xT = sem("s_xT")
        s_hT = sem("s_hT")
        s_rawmm = sem("s_rawmm")
        s_raw = sem("s_raw")
        s_zmm = sem("s_zmm")
        s_z = sem("s_z")
        s_dve = sem("s_dve")
        s_spe = sem("s_spe")
        s_a = sem("s_a")
        s_pfx = sem("s_pfx")
        s_etab = sem("s_etab")
        s_wB = sem("s_wB")
        s_tap0 = sem("s_tap0")
        s_tap0b = sem("s_tap0b")
        s_tap = sem("s_tap")
        s_tapb = sem("s_tapb")
        s_prod = sem("s_prod")
        s_th = sem("s_th")
        s_thb = sem("s_thb")
        s_gx1 = sem("s_gx1")
        s_gx = sem("s_gx")
        s_bc = sem("s_bc")
        s_cc = sem("s_cc")
        s_sn = sem("s_sn")
        s_rep = sem("s_rep")
        s_erow = sem("s_erow")
        s_split = sem("s_split")
        s_L = sem("s_L")
        s_tx = sem("s_tx")
        s_sg = sem("s_sg")
        s_ys = sem("s_ys")
        s_xt = sem("s_xt")
        s_e = sem("s_e")
        s_m = sem("s_m")
        s_S = sem("s_S")
        s_v = sem("s_v")
        s_yz = sem("s_yz")
        s_sq = sem("s_sq")
        s_rt = sem("s_rt")
        s_rn = sem("s_rn")
        s_y1 = sem("s_y1")
        s_ysum = sem("s_ysum")
        s_yTm = sem("s_yTm")
        s_yT = sem("s_yT")
        s_o = sem("s_o")
        s_o1 = sem("s_o1")
        s_st2 = sem("s_st2")
        s_mv2 = sem("s_mv2")
        s_ve2 = sem("s_ve2")
        s_rs2 = sem("s_rs2")
        s_xn2 = sem("s_xn2")
        s_h2a = sem("s_h2a")
        s_h2 = sem("s_h2")
        s_h2m = sem("s_h2m")
        s_h2c = sem("s_h2c")
        s_lgm = sem("s_lgm")
        s_rt_dve = sem("s_rt_dve")
        s_hot = sem("s_hot")
        s_routed = sem("s_routed")
        s_rank = sem("s_rank")
        s_pos = sem("s_pos")
        s_x1r = sem("s_x1r")
        s_id = sem("s_id")
        s_scat = [sem(f"s_scat{i}") for i in range(2 * BT)]
        s_tab = sem("s_tab")
        s_tabv = sem("s_tabv")
        s_padi = sem("s_padi")
        s_pad = sem("s_pad")
        s_rb = [sem(f"s_rb{i}") for i in range(4)]
        s_eT = sem("s_eT")
        s_eTc = sem("s_eTc")
        s_h1 = sem("s_h1")
        s_hb = sem("s_hb")
        s_hx = sem("s_hx")
        s_hr = sem("s_hr")
        s_y2 = sem("s_y2")
        s_flag = sem("s_flag")
        s_gs = sem("s_gs")
        s_tok = sem("s_tok")
        s_gd = sem("s_gd")
        s_yo1 = sem("s_yo1")
        s_yo2 = sem("s_yo2")
        s_ob = sem("s_ob")
        s_out = [sem(f"s_out{i}") for i in range(4)]

        b1s = zs[:, :, :].rearrange("p t c -> p (t c)").rearrange("p (e f) -> p e f", e=NE)
        at = [0]

        def over(n):
            at[0] += n
            return ARENA[:, at[0] - n:at[0]]

        NM = NTOK // P
        tiles_gt = over(NE * NM).rearrange("p (e m) -> p e m", e=NE)
        m128 = over(NM)
        ntile = over(NE)
        cum = over(NE)
        coef = over(NE)
        slot_i = over(NSLOT)
        behind = over(2 * NE * NSLOT).rearrange("p (k e s) -> p k e s", k=2, e=NE)
        slot_v = over(2 * NSLOT).rearrange("p (k s) -> p k s", k=2)
        slot_r = over(2 * NSLOT).bitcast(mybir.dt.int32).rearrange("p (k s) -> p k s", k=2)
        padf = over(NE)
        padi = over(NE).bitcast(mybir.dt.int32)
        rh = over(4 * DM).rearrange("p (a c) -> p a c", a=4)
        XR = ROW - DM
        xr = over(NSLOT * XR).rearrange("p (s c) -> p s c", s=NSLOT)
        gdiff = over(DM)
        hTs = over(2 * P).rearrange("p (a c) -> p a c", a=2)
        hb = over(2 * FF).rearrange("p (a c) -> p a c", a=2)
        hr = over(2 * FF).rearrange("p (a c) -> p a c", a=2)
        flag = over(2).rearrange("p (a c) -> p a c", a=2)
        gsel = over(2 * DM).rearrange("p (a c) -> p a c", a=2)
        tok = over(4).bitcast(mybir.dt.int32).rearrange("p (a c) -> p a c", a=4)
        yo1 = over(2 * DM).rearrange("p (a c) -> p a c", a=2)
        yo2 = over(2 * DM).rearrange("p (a c) -> p a c", a=2)
        ob = over(4 * DM).rearrange("p (a c) -> p a c", a=4)

        routed = nc.dram_tensor("routed_rows", (NE * REGION + P, ROW), F32, kind="Internal").ap()
        N_POOL0 = 20 + 2 * (2 + 2 * NH) + 2 + 2 * 2 * NH
        N_DVE0 = 15

        s_held = sem("s_held")

        def hold(eng, signal, value):
            eng.wait_ge(signal, value)
            eng.sem_inc(s_held, 1)

        def phase_end(eng, b, n):
            eng.sem_inc(s_held, 1)
            eng.drain().then_inc(s_phase, 1)
            hold(eng, s_phase, b * 12 + 4 * (n + 1))

        def col(d, h, t):
            c = (d * NH + h) * TPB + t
            return slice(c, c + 1)

        out_rows = out.rearrange("b t d -> (b t) d")
        NR = 7 + BT

        block = ctx.enter_context(nc.Block())

        @block.sync
        def _(sp_):
            n = 0
            u_rows = u.rearrange("b (t p) d -> p (b t) d", p=P)
            for i in range(2 * B):
                h = TPB // 2
                sp_.dma_start(xs[:, i * h:(i + 1) * h, :], u_rows[:, i * h:(i + 1) * h, :]).then_inc(s_x, 16)
            for dst, src in (
                (wx[:, :], w_xbc), (wz[:, :], w_zdt), (cw[:, :, :, :], conv_w), (cb[:, :, :], conv_b),
                (dtb[:, :], dt_bias.partition_broadcast(P)), (alog[:, :], a_log.partition_broadcast(P)),
                (dsk[:, :], d_skip.partition_broadcast(P)),
                (nw[:, :], norm_w), (wo[:, :, :], w_out), (gw[:, :], gate_w),
                (gbias[:, :, :], gate_b.partition_broadcast(P)),
                (ct_in[:, :], c_t), (wm[:, :], wmod),
            ):
                sp_.dma_start(dst, src).then_inc(s_load, 16)
                n += 1
            assert n == 13
            for dst, src in ((w1s[:, :, :], w1), (w2s[:, :, :, :], w2), (b2s[:, :, :], b2.partition_broadcast(P))):
                sp_.dma_start(dst, src).then_inc(s_wf, 16)
            sp_.wait_ge(s_phase, 12 * (B - 1) + 8)
            sp_.dma_start(b1s, b1.partition_broadcast(P)).then_inc(s_wf, 16)

            sp_.wait_ge(s_phase, 12 * B)
            for i in range(2 * BT):
                sp_.wait_ge(s_scat[i], 16 * B * TPB // (2 * BT))
            sp_.wait_ge(s_pad, 16 * (NE + 1))
            sp_.wait_ge(s_tabv, 1)

            def load_rows(s, k):
                first = sp_.value_load(slot_r[0:1, 0, bass.ds(s, 1)], min_val=0, max_val=NE * REGION)
                sp_.dma_start(rh[:, k, :], routed[bass.ds(first, P), 0:DM]).then_inc(s_rb[k], 16)
                sp_.dma_start(xr[:, bass.ds(s, 1), :].rearrange("p a c -> p (a c)"),
                              routed[bass.ds(first, P), DM:ROW]).then_inc(s_rb[k], 16)

            for s in range(4):
                load_rows(s, s)
            with sp_.Fori(1, NSLOT // 4) as it:
                for k in range(4):
                    sp_.wait_ge(s_eT, 4 * it + k - 3)
                    load_rows(4 * it + k, k)
            for s in range(NSLOT // 4 * 4, NSLOT):
                sp_.wait_ge(s_eT, s - 3)
                load_rows(s, s % 4)

        NLOAD = 13 * 16

        @block.gpsimd
        def _(pool):
            n = [0]

            def link(ins):
                n[0] += 1
                ins.then_inc(s_pool0, 1)
                hold(pool, s_pool0, n[0])

            link(pool.memset(ident[:, :], 0.0))
            link(pool.affine_select(out=ident[:, :], in_=ident[:, :], compare_op=ALU.not_equal, fill=1.0, base=0,
                                    pattern=[[-1, P]], channel_multiplier=1))
            link(pool.tensor_copy(identb[:, :], ident[:, :]))
            link(pool.memset(ones[:, :], 1.0))
            for d in range(2):
                sgn = 1 - 2 * d
                link(pool.affine_select(out=incl[:, d, :], in_=ones[:, :], compare_op=ALU.is_ge, fill=0.0, base=0,
                                        pattern=[[sgn, P]], channel_multiplier=-sgn))
                link(pool.affine_select(out=strict[:, d, :], in_=ones[:, :], compare_op=ALU.is_gt, fill=0.0, base=0,
                                        pattern=[[-sgn, P]], channel_multiplier=sgn))
                for h in range(NH):
                    link(pool.memset(negm[:, d, h, :], 0.0))
                    link(pool.affine_select(out=negm[:, d, h, :], in_=negm[:, d, h, :], compare_op=ALU.is_ge,
                                            fill=MASKED, base=0, pattern=[[sgn, P]], channel_multiplier=-sgn))
            link(pool.memset(mhalf[:, :], -0.5))
            link(pool.iota(rank8[:, :], pattern=[[-1, NE]], base=NE, channel_multiplier=0,
                           allow_small_or_imprecise_dtypes=True))
            link(pool.iota(ids[:, :], pattern=[[P, B * TPB]], base=0, channel_multiplier=1,
                           allow_small_or_imprecise_dtypes=True))
            link(pool.iota(pcol[:, :], pattern=[[0, 1]], base=0, channel_multiplier=1,
                           allow_small_or_imprecise_dtypes=True))
            link(pool.iota(region0[:, :], pattern=[[REGION, NE]], base=0, channel_multiplier=0,
                           allow_small_or_imprecise_dtypes=True))
            link(pool.iota(nextrow[:, 0, 0, :], pattern=[[REGION, NE]], base=0, channel_multiplier=0,
                           allow_small_or_imprecise_dtypes=True))
            link(pool.memset(padrow[:, :], 0.0))
            link(pool.memset(padrow[:, 2 * DM:2 * DM + 1], float(NTOK)))
            link(pool.memset(rows[:, :, 2 * DM:], 0.0))
            W = NH * TPB
            for c in range(3):
                pv = pick[c * W:(c + 1) * W, :, :].rearrange("k t (h n) -> k t h n", h=NH)
                link(pool.memset(pick[c * W:(c + 1) * W, :, :], 0.0))
                for h in range(NH):
                    link(pool.affine_select(out=pv[:, :, h, :], in_=pv[:, :, h, :], compare_op=ALU.not_equal, fill=1.0,
                                            base=-h * TPB, pattern=[[-1, TPB], [0, NS]], channel_multiplier=1))
            hold(pool, s_load, NLOAD)
            for k in range(2 * NH):
                link(pool.memset(biasb[:, k, :], 0.0))
                link(pool.tensor_scalar(biasb[:, k, :], biasb[:, k, :], dtb[:, k:k + 1], 1.0, ALU.add, ALU.mult))
            assert n[0] == N_POOL0
            pool.dma_start(routed[NE * REGION:NE * REGION + P, :], padrow[:, :]).then_inc(s_pad, 16)
            hold(pool, s_dve0, N_DVE0)

            with pool.Fori(0, B) as b:
                hold(pool, s_mv, b * TPB + TPB)
                pool.tensor_scalar(ve[:, :], mv[:, :, 1], EPS, 1.0, ALU.add, ALU.mult).then_inc(s_ve, 1)
                hold(pool, s_ve, b + 1)
                pool.tensor_tensor(rstd[:, :], ve[:, :], mhalf[:, 0:TPB], ALU.pow).then_inc(s_rstd, 1)
                phase_end(pool, b, 0)

                def decay_rows(q):
                    d, t = chunk_of(q)
                    if q >= 2:
                        hold(pool, s_sg, b * CHUNKS + q - 1)
                    for h in range(NH):
                        last = pool.tensor_scalar(lseg[:, q % 2, h, :], strict[:, d, :],
                                                  av[:, col(d, h, t)], 1.0, ALU.mult, ALU.mult)
                    last.then_inc(s_L, 1)

                def taps_bc(s, k):
                    d, blk = step_of(s)
                    c0 = HALO + blk * BLK + (k - HALO) * (1 - 2 * d)
                    done = b * STEPS * HALO + HALO * s + HALO - 1 - k
                    if s > 0 or k < HALO - 1:
                        hold(pool, s_tapb, done)
                    pool.tensor_scalar(prod[:, :], raw[:, NH, c0:c0 + BLK], cw[:, d, NH, k:k + 1], 1.0,
                                       ALU.mult, ALU.mult).then_inc(s_prod, 1)
                    if k == HALO - 1:
                        hold(pool, s_tap0b, b * STEPS + s + 1)
                    hold(pool, s_prod, done + 1)
                    pool.tensor_tensor(acc_bc[s % 2], acc_bc[s % 2], prod[:, :], ALU.add).then_inc(s_tapb, 1)

                def gate_x(s):
                    for g in range(NH):
                        hold(pool, s_th, b * STEPS * NH + s * NH + g + 1)
                        pool.tensor_scalar(cx[:, s % 2, g, :], cx[:, s % 2, g, :], 1.0, 1.0,
                                           ALU.add, ALU.mult).then_inc(s_gx1, 1)
                    for g in range(NH):
                        hold(pool, s_gx1, b * STEPS * NH + s * NH + g + 1)
                        pool.tensor_tensor(cx[:, s % 2, g, :], cx[:, s % 2, g, :], acc[:, g, :],
                                           ALU.mult).then_inc(s_gx, 1)

                def norms(n, d, t0, t1):
                    hold(pool, s_sq, b * CHUNKS + (t1 if d == 0 else 0) + TPB)
                    pool.tensor_scalar(rt[:, d, t0:t1], ssq[:, d, t0:t1], 1.0 / DI, EPS, ALU.mult,
                                       ALU.add).then_inc(s_rt, 1)
                    hold(pool, s_rt, 4 * b + n + 1)
                    pool.tensor_tensor(rn[:, d, t0:t1], rt[:, d, t0:t1], mhalf[:, 0:t1 - t0], ALU.pow).then_inc(s_rn, 1)

                for k in (2, 1, 0):
                    taps_bc(0, k)
                decay_rows(0)
                gate_x(0)
                decay_rows(1)
                for k in (2, 1, 0):
                    taps_bc(1, k)
                for q in range(CHUNKS):
                    s, j = q // BT, q % BT
                    if q + 2 < CHUNKS:
                        decay_rows(q + 2)
                    if j == 1 and s + 1 < STEPS:
                        gate_x(s + 1)
                    if j != 1 and s + 2 < STEPS:
                        taps_bc(s + 2, {0: 2, 2: 1, 3: 0}[j])
                    if q == TPB + 6:
                        norms(0, 1, 0, TPB)
                norms(1, 0, 0, TPB // 2)
                norms(2, 0, TPB // 2, TPB // 4 * 3)
                phase_end(pool, b, 1)
                norms(3, 0, TPB // 4 * 3, TPB)

                def scatter(i):
                    hold(pool, s_pos, b * NBLK + i + 1)
                    hold(pool, s_x1r, b * NBLK + i + 1)
                    for j in range(BT):
                        k = (i % 2) * BT + j
                        pool.indirect_dma_start(routed[:, :], bass.IndirectOffsetOnAxis(ap=rowat[:, k, :].bitcast(mybir.dt.uint32), axis=0),
                                                rows[:, k, :], None).then_inc(s_scat[k], 16)

                for i in range(NBLK):
                    g, a = b * NBLK + i, i % 2
                    sl = slice(a * BT, (a + 1) * BT)
                    hold(pool, s_mv2, g + 1)
                    pool.tensor_scalar(ve2[:, :], mv2[:, a, :, 1], EPS, 1.0, ALU.add, ALU.mult).then_inc(s_ve2, 1)
                    hold(pool, s_ve2, g + 1)
                    if i >= 2:
                        hold(pool, s_xn2, g - 1)
                    pool.tensor_tensor(rs2[:, a, :], ve2[:, :], mhalf[:, 0:BT], ALU.pow).then_inc(s_rs2, 1)
                    hold(pool, s_h2a, g + 1)
                    pool.tensor_tensor(rows[:, sl, 0:DM], rows[:, sl, 0:DM],
                                       row[:, b, 3, :].unsqueeze(1).broadcast_to([P, BT, DM]), ALU.add).then_inc(s_h2, 1)
                    pool.tensor_copy(rows[:, sl, 2 * DM:2 * DM + 1].rearrange("p j c -> p (j c)"),
                                     ids[:, bass.ds(BT * g, BT)]).then_inc(s_id, 1)
                    hold(pool, s_id, g + 1)
                    hold(pool, s_h2, g + 1)
                    if i >= 1:
                        scatter(i - 1)
                scatter(NBLK - 1)
                phase_end(pool, b, 2)

            pool.iota(m128, pattern=[[P, NM]], base=0, channel_multiplier=0,
                      allow_small_or_imprecise_dtypes=True).then_inc(s_tab, 1)
            pool.iota(slot_i, pattern=[[1, NSLOT]], base=0, channel_multiplier=0,
                      allow_small_or_imprecise_dtypes=True).then_inc(s_tab, 1)
            hold(pool, s_padi, 1)
            for e in range(NE):
                pool.indirect_dma_start(routed[:, :], bass.IndirectOffsetOnAxis(ap=padi[:, e:e + 1].bitcast(mybir.dt.uint32), axis=0),
                                        padrow[:, :], None).then_inc(s_pad, 16)

            def token_numbers(s, k, rk, free16):
                hold(pool, s_rb[k], rk)
                if free16 is not None:
                    hold(pool, s_out[k], free16)
                pool.tensor_copy(tok[:, k, :], xr[:, bass.ds(s, 1), DM:DM + 1].rearrange("p a c -> p (a c)")).then_inc(s_tok, 1)

            def put(s, k):
                hold(pool, s_ob, s + 1)
                hold(pool, s_tok, s + 1)
                pool.indirect_dma_start(out_rows, bass.IndirectOffsetOnAxis(ap=tok[:, k, :].bitcast(mybir.dt.uint32), axis=0),
                                        ob[:, k, :], None, bounds_check=NTOK - 1, oob_is_err=False).then_inc(s_out[k], 16)

            for s in range(4):
                token_numbers(s, s, 32, None)
                if s >= 1:
                    put(s - 1, s - 1)
            with pool.Fori(1, NSLOT // 4) as it:
                for k in range(4):
                    token_numbers(4 * it + k, k, 32 * it + 32, 16 * it)
                    put(4 * it + k - 1, (k + 3) % 4)
            for s in range(NSLOT // 4 * 4, NSLOT):
                token_numbers(s, s % 4, 32 * (s // 4) + 32, 16 * (s // 4))
                put(s - 1, (s - 1) % 4)
            put(NSLOT - 1, (NSLOT - 1) % 4)
            for k in range(4):
                hold(pool, s_out[k], 16 * ((NSLOT - k + 3) // 4))

        @block.scalar
        def _(act):
            act.wait_ge(s_load, NLOAD)
            act.activation(csil[:, :], ct_in[:, :], ACT.Silu).then_inc(s_act0, 1)
            act.activation(ab[:, :, 0], alog[:, :], ACT.Exp).then_inc(s_act0, 1)
            act.wait_ge(s_dve0, N_DVE0)

            with act.Fori(0, B) as b:
                def modulate(i):
                    hold(act, s_xT, b * TPB + 4 * i + 4)
                    if i >= 2:
                        hold(act, s_zmm, b * TPB + 4 * (i - 1))
                    act.activation(hT[:, i % 2, :], bank[i % 2][:, :], ACT.Identity,
                                   bias=modc[:, 0, bass.ds(b, 1)], scale=modc[:, 1, bass.ds(b, 1)]).then_inc(s_hT, 1)

                modulate(0)
                for i in range(NBLK):
                    if i + 1 < NBLK:
                        modulate(i + 1)
                    for j in range(BT):
                        n, t = BT * i + j, BT * (NBLK - 1 - i) + j
                        pz = bank[5 + n % 3]
                        act.wait_ge(s_zmm, b * TPB + n + 1)
                        act.activation(zs[:, t, :], pz[:, 0:DI], ACT.Silu)
                        act.activation(dtr[:, t, :], pz[:, DI:ZW], ACT.Identity).then_inc(s_z, 1)
                act.wait_ge(s_spe, b * 4 + 1)
                act.activation(sp[:, 2, :], sp[:, 1, :], ACT.Exp, scale=-1.0).then_inc(s_spe, 1)
                act.wait_ge(s_spe, b * 4 + 3)
                act.activation(sp[:, 4, :], sp[:, 3, :], ACT.Ln).then_inc(s_spe, 1)
                act.wait_ge(s_pfx, b + 1)
                act.activation(etab[:, :, :], bank[5][:, 0:2 * NQ].rearrange("p (k c) -> p k c", k=2), ACT.Exp)
                act.activation(etot[:, :, :], bank[5][:, 2 * NQ:2 * NQ + 2 * TPB].rearrange("p (d t) -> p d t", d=2),
                               ACT.Exp).then_inc(s_etab, 1)
                phase_end(act, b, 0)

                def tap0_bc(s):
                    d, k = step_of(s)
                    if s >= 2:
                        act.wait_ge(s_bc, b * STEPS + s - 1)
                    act.activation(acc_bc[s % 2], raw[:, NH, HALO + k * BLK:HALO + (k + 1) * BLK], ACT.Identity,
                                   bias=cb[:, d, NH:NG], scale=cw[:, d, NH, KC - 1:KC]).then_inc(s_tap0b, 1)

                def tap0(s):
                    d, k = step_of(s)
                    if s >= 1:
                        act.wait_ge(s_gx, b * STEPS * NH + NH * s)
                    for g in range(NH):
                        act.activation(acc[:, g, :], raw[:, g, HALO + k * BLK:HALO + (k + 1) * BLK], ACT.Identity,
                                       bias=cb[:, d, g:g + 1], scale=cw[:, d, g, KC - 1:KC]).then_inc(s_tap0, 1)

                def tanhs(s):
                    if s >= 2:
                        act.wait_ge(s_sg, b * CHUNKS + BT * (s - 1))
                    act.wait_ge(s_tapb, b * STEPS * HALO + HALO * (s + 1))
                    act.activation(bc[:, s % 2, :], acc_bc[s % 2], ACT.Tanh).then_inc(s_thb, 1)
                    act.wait_ge(s_tap, b * STEPS * 6 + 6 * (s + 1))
                    for g in range(NH):
                        act.activation(cx[:, s % 2, g, :], acc[:, g, :], ACT.Tanh).then_inc(s_th, 1)

                def two_c(s):
                    act.wait_ge(s_bc, b * STEPS + s + 1)
                    if s >= 2:
                        act.wait_ge(s_m, b * CHUNKS + BT * (s - 1))
                    act.activation(cc[0:NS, s % 2, :], bc[NS:2 * NS, s % 2, :], ACT.Copy)
                    act.activation(cc[NS:2 * NS, s % 2, :], bc[NS:2 * NS, s % 2, :], ACT.Copy).then_inc(s_cc, 1)

                def tokens_major(q):
                    d, t = chunk_of(q)
                    tx = bank[q % 2]
                    act.wait_ge(s_tx, b * CHUNKS + q + 1)
                    if q >= TM:
                        act.wait_ge(s_ys, b * CHUNKS + q - TM + 1)
                        act.wait_ge(s_v, b * CHUNKS + q - TM + 1)
                    act.activation(xt[:, q % TM, :], tx[:, 0:DI], ACT.Copy)
                    for h in range(NH):
                        act.activation(bs[:, q % TM, h, h, :], tx[:, DI:DI + NS], ACT.Copy, scale=wB[:, col(d, h, t)])
                    for h in range(NH):
                        last = act.activation(ws[:, q % TM, h * HD:(h + 1) * HD], tx[:, h * HD:(h + 1) * HD], ACT.Copy,
                                              scale=dsk[:, d * NH + h:d * NH + h + 1])
                    last.then_inc(s_xt, 1)

                def decays(q):
                    act.wait_ge(s_sg, b * CHUNKS + q + 1)
                    if q >= 2:
                        act.wait_ge(s_m, b * CHUNKS + q - 1)
                    act.activation(es[:, q % 2, :, :], bank[2 + q % 2][:, 0:DI].rearrange("p (h i) -> p h i", h=NH),
                                   ACT.Exp).then_inc(s_e, 1)

                def squares(q):
                    d, t = chunk_of(q)
                    act.wait_ge(s_yz, b * CHUNKS + q + 1)
                    if q >= 1:
                        act.wait_ge(s_sq, b * CHUNKS + q)
                    act.activation(junk[:, :], yz[:, d, t, :], ACT.Square,
                                   accum_out=ssq[:, d, t:t + 1]).then_inc(s_sq, 1)

                tap0_bc(0)
                tap0(0)
                tap0_bc(1)
                tanhs(0)
                two_c(0)
                tap0(1)
                tap0_bc(2)
                decays(0)
                tokens_major(0)
                for q in range(CHUNKS):
                    s, j = q // BT, q % BT
                    if q + 1 < CHUNKS:
                        decays(q + 1)
                        tokens_major(q + 1)
                    if q >= 2:
                        squares(q - 2)
                    if j == 0 and s + 1 < STEPS:
                        tanhs(s + 1)
                    if j == 1 and s + 1 < STEPS:
                        two_c(s + 1)
                    if j == 2 and s + 2 < STEPS:
                        tap0(s + 2)
                    if j == 3 and s + 3 < STEPS:
                        tap0_bc(s + 3)
                squares(CHUNKS - 2)
                squares(CHUNKS - 1)
                phase_end(act, b, 1)

                hold(act, s_rn, 4 * b + 3)

                def forward(i):
                    if i >= 1:
                        act.wait_ge(s_ysum, b * NBLK + i)
                    for j in range(BT):
                        t = BT * i + j
                        last = act.activation(y1[:, j, :], yz[:, 0, t, :], ACT.Copy, scale=rn[:, 0, t:t + 1])
                    last.then_inc(s_y1, 1)

                def out_T(i):
                    act.wait_ge(s_yTm, b * NBLK + i + 1)
                    if i >= 1:
                        act.wait_ge(s_o, b * NBLK + i)
                    for k in range(2):
                        last = act.activation(yT[:, 2 * k:2 * k + 2, :], bank[k][:, :].rearrange("p (j c) -> p j c", j=2),
                                              ACT.Copy)
                    last.then_inc(s_yT, 1)

                forward(0)
                forward(1)
                out_T(0)
                for i in range(NBLK):
                    g = b * NBLK + i
                    if i + 1 < NBLK:
                        out_T(i + 1)
                    if i + 2 == NBLK - 1:
                        hold(act, s_rn, 4 * b + 4)
                    if i + 2 < NBLK:
                        forward(i + 2)
                    act.wait_ge(s_h2m, g + 1)
                    if i >= 1:
                        act.wait_ge(s_lgm, g)
                    act.activation(h2c, bank[4 + i % 2][:, :].rearrange("p (j c) -> p j c", j=BT), ACT.Copy).then_inc(s_h2c, 1)
                phase_end(act, b, 2)

            def rows_T(s, a, first):
                act.wait_ge(s_eT, s + 1)
                if not first:
                    act.wait_ge(s_h1, s - 1)
                act.activation(hTs[:, a, :], bank[a][:, 0:P], ACT.Copy).then_inc(s_eTc, 1)

            def rectify(s, a, first):
                act.wait_ge(s_hx, s + 1)
                if not first:
                    act.wait_ge(s_y2, s - 1)
                act.activation(hr[:, a, :], bank[4 + a][:, :], ACT.Relu).then_inc(s_hr, 1)

            rows_T(0, 0, True)
            rows_T(1, 1, True)
            for s in range(2):
                rows_T(s + 2, s % 2, False)
                rectify(s, s % 2, True)
            with act.Fori(1, (NSLOT - 2) // 2) as it:
                for a in range(2):
                    rows_T(2 * it + a + 2, a, False)
                    rectify(2 * it + a, a, False)
            for s in range((NSLOT - 2) // 2 * 2, NSLOT):
                if s + 2 < NSLOT:
                    rows_T(s + 2, s % 2, False)
                rectify(s, s % 2, False)

        @block.tensor
        def _(pe):
            pe.wait_ge(s_pool0, N_POOL0)
            pe.wait_ge(s_dve0, 1)
            for m in range(2):
                pe.matmul(bank[0][:, m * B:(m + 1) * B], wm[:, m * DM:(m + 1) * DM], csil[:, :], start=True, stop=True)
            for b in range(B):
                pe.matmul(bank[1 + 2 * b][:, 0:3 * DM], csil_bc[:, b, :], wm[:, 0:3 * DM], start=True, stop=True)
                last = pe.matmul(bank[2 + 2 * b][:, 0:3 * DM], csil_bc[:, b, :], wm[:, 3 * DM:6 * DM],
                                 start=True, stop=True)
            last.then_inc(s_pe0, 1)
            pe.wait_ge(s_dve0, N_DVE0)

            with pe.Fori(0, B) as b:
                def turn(i):
                    for j in range(BT):
                        n = BT * i + j
                        pe.wait_ge(s_xn, b * TPB + n + 1)
                        if i >= 2 and j == 0:
                            pe.wait_ge(s_hT, b * NBLK + i - 1)
                        pe.transpose(bank[i % 2][:, j * P:(j + 1) * P], xn[:, n % 4, :], ident[:, :]).then_inc(s_xT, 1)

                turn(0)
                for i in range(NBLK):
                    if i + 1 < NBLK:
                        turn(i + 1)
                    pe.wait_ge(s_hT, b * NBLK + i + 1)
                    for g in range(NG):
                        if i >= 1:
                            pe.wait_ge(s_raw, b * NBLK * NG + NG * (i - 1) + g + 1)
                        pe.matmul(bank[2 + g][:, :], wx[:, g * P:(g + 1) * P], hT[:, i % 2, :],
                                  start=True, stop=True).then_inc(s_rawmm, 1)
                    for j in range(BT):
                        n = BT * i + j
                        if n >= 3:
                            pe.wait_ge(s_z, b * TPB + n - 2)
                        pe.matmul(bank[5 + n % 3][:, 0:ZW], hT[:, i % 2, j * P:(j + 1) * P], wz[:, :],
                                  start=True, stop=True).then_inc(s_zmm, 1)
                pe.wait_ge(s_a, b + 1)
                W = NH * TPB
                for d in range(2):
                    for k, m in enumerate((incl[:, d, :], strict[:, d, :])):
                        pe.matmul(bank[5][:, k * NQ + d * W:k * NQ + (d + 1) * W], m, av[:, d * W:(d + 1) * W],
                                  start=True, stop=True)
                    for h in range(NH):
                        last = pe.matmul(bank[5][h * NS:(h + 1) * NS, 2 * NQ + d * TPB:2 * NQ + (d + 1) * TPB],
                                         ones[:, 0:NS], av[:, d * W + h * TPB:d * W + (h + 1) * TPB],
                                         start=True, stop=True)
                last.then_inc(s_pfx, 1)
                pe.wait_ge(s_rep, b + 1)
                for d in range(2):
                    last = pe.transpose(bank[6][0:3 * W, d * P:(d + 1) * P], e0rep[:, d].rearrange("p c k -> p (c k)"),
                                        ident[:, :])
                last.then_inc(s_erow, 1)
                phase_end(pe, b, 0)

                def prepare(q):
                    d, t = chunk_of(q)
                    s, j = q // BT, q % BT
                    c0 = (t % BT) * P
                    tx, sg = bank[q % 2], bank[2 + q % 2]
                    if j == 0:
                        pe.wait_ge(s_gx, b * STEPS * NH + NH * (s + 1))
                        pe.wait_ge(s_cc, b * STEPS + s + 1)
                    if q >= 2:
                        pe.wait_ge(s_xt, b * CHUNKS + q - 1)
                    for h in range(NH):
                        pe.transpose(tx[:, h * HD:(h + 1) * HD], cx[:, s % 2, h, c0:c0 + P], ident[:, :])
                    pe.transpose(tx[:, DI:DI + NS], bc[0:NS, s % 2, c0:c0 + P], ident[0:NS, 0:NS]).then_inc(s_tx, 1)
                    if q >= 2:
                        pe.wait_ge(s_m, b * CHUNKS + q - 1)
                    pe.matmul(sg[:, DI:DI + P], bc[0:NS, s % 2, c0:c0 + P], cc[0:NS, s % 2, c0:c0 + P],
                              start=True, stop=True)
                    pe.matmul(sg[:, DI + P:DI + 2 * P], pick[:, t, :], eparts[:, d, :], start=True, stop=True)
                    pe.matmul(sg[:, 0:DI], identb[:, :], negm[:, d, :, :].rearrange("p h i -> p (h i)"),
                              start=True, stop=False, skip_group_check=True)
                    pe.wait_ge(s_L, b * CHUNKS + q + 1)
                    for h in range(NH):
                        last = pe.matmul(sg[:, h * P:(h + 1) * P], lseg[:, q % 2, h, :], incl[:, d, :],
                                         start=False, stop=True, skip_group_check=True)
                    last.then_inc(s_sg, 1)

                def scan(q):
                    d, t = chunk_of(q)
                    ys, sn = bank[4 + q % 2], bank[6 + q % 2]
                    pe.wait_ge(s_xt, b * CHUNKS + q + 1)
                    if q >= 2:
                        pe.wait_ge(s_S, b * CHUNKS + q - 1)
                    if q % TPB != TPB - 1:
                        for h in range(NH):
                            last = pe.matmul(sn[:, h * HD:(h + 1) * HD], bs[:, q % TM, h].rearrange("p g n -> p (g n)"),
                                             xt[:, q % TM, h * HD:(h + 1) * HD], start=True, stop=True)
                        last.then_inc(s_sn, 1)
                    pe.wait_ge(s_m, b * CHUNKS + q + 1)
                    if q >= 2:
                        pe.wait_ge(s_v, b * CHUNKS + q - 1)
                    for h in range(NH):
                        pe.matmul(ys[:, h * HD:(h + 1) * HD], ms[:, q % 2, h, :], xt[:, q % TM, h * HD:(h + 1) * HD],
                                  start=(h == 0), stop=False, skip_group_check=True)
                    if q >= 1:
                        pe.wait_ge(s_S, b * CHUNKS + q)
                    pe.matmul(ys[:, 0:DI], cs[:, q % 2, :], st[:, q % 2, :], start=False, stop=True,
                              skip_group_check=True).then_inc(s_ys, 1)

                prepare(0)
                for q in range(CHUNKS):
                    if q + 1 < CHUNKS:
                        prepare(q + 1)
                    scan(q)
                phase_end(pe, b, 1)

                def y_turn(i):
                    pe.wait_ge(s_ysum, b * NBLK + i + 1)
                    if i >= 1:
                        pe.wait_ge(s_yT, b * NBLK + i)
                    for j in range(BT):
                        for h in range(NH):
                            c0 = (j % 2) * DI + h * P
                            last = pe.transpose(bank[j // 2][:, c0:c0 + P], ysum[:, j, h * P:(h + 1) * P], ident[:, :])
                    last.then_inc(s_yTm, 1)

                def project(i):
                    pe.wait_ge(s_yT, b * NBLK + i + 1)
                    if i >= 2:
                        pe.wait_ge(s_o1, b * NBLK + i - 1)
                    for j in range(BT):
                        for h in range(NH):
                            last = pe.matmul(bank[2 + i % 2][:, j * DM:(j + 1) * DM], yT[:, j, h * P:(h + 1) * P],
                                             won[:, h, :], start=(h == 0), stop=(h == NH - 1))
                    last.then_inc(s_o, 1)

                def ranks(i):
                    pe.wait_ge(s_hot, b * NBLK + i + 1)
                    bk = bank[6 + i % 2]
                    W = BT * NE
                    hv = hot[:, i % 2].rearrange("p j e -> p (j e)")
                    pe.matmul(bk[:, W:2 * W], strict[:, 1, :], hv, start=True, stop=True)
                    pe.matmul(bk[:, 2 * W:3 * W], ones[:, :], hv, start=True, stop=True).then_inc(s_rank, 1)

                y_turn(0)
                project(0)
                for i in range(NBLK):
                    g = b * NBLK + i
                    if i + 1 < NBLK:
                        y_turn(i + 1)
                    if i >= 1:
                        ranks(i - 1)
                    if i + 1 < NBLK:
                        project(i + 1)
                    pe.wait_ge(s_h2, g + 1)
                    if i >= 2:
                        pe.wait_ge(s_h2c, g - 1)
                    for j in range(BT):
                        last = pe.transpose(bank[4 + i % 2][:, j * P:(j + 1) * P], rows[:, (i % 2) * BT + j, 0:DM],
                                            ident[:, :])
                    last.then_inc(s_h2m, 1)
                    pe.wait_ge(s_h2c, g + 1)
                    if i >= 2:
                        pe.wait_ge(s_routed, g - 1)
                    for j in range(BT):
                        last = pe.matmul(bank[6 + i % 2][:, j * NE:(j + 1) * NE], h2c[:, j, :], gw[:, :],
                                         start=True, stop=True)
                    last.then_inc(s_lgm, 1)
                ranks(NBLK - 1)
                phase_end(pe, b, 2)

            pe.wait_ge(s_wf, 64)
            pe.wait_ge(s_tabv, 1)

            def turn_rows(s, a, k, rk, first):
                pe.wait_ge(s_rb[k], rk)
                if not first:
                    pe.wait_ge(s_eTc, s - 1)
                pe.transpose(bank[a][:, 0:P], rh[:, k, :], ident[:, :]).then_inc(s_eT, 1)

            def hidden(s, a, first, e):
                pe.wait_ge(s_eTc, s + 1)
                if not first:
                    pe.wait_ge(s_hb, s - 1)
                pe.matmul(bank[2 + a][:, :], hTs[:, a, :], w1s[:, bass.ds(e, 1), :].rearrange("p a f -> p (a f)"),
                          start=True, stop=True).then_inc(s_h1, 1)

            def turn_hidden(s, a, first):
                pe.wait_ge(s_hb, s + 1)
                if not first:
                    pe.wait_ge(s_hr, s - 1)
                for f in range(FC):
                    last = pe.transpose(bank[4 + a][:, f * P:(f + 1) * P], hb[:, a, f * P:(f + 1) * P], ident[:, :])
                last.then_inc(s_hx, 1)

            def down(s, a, first, e):
                pe.wait_ge(s_hr, s + 1)
                if not first:
                    pe.wait_ge(s_yo1, s - 1)
                for f in range(FC):
                    last = pe.matmul(bank[6 + a][:, 0:DM], hr[:, a, f * P:(f + 1) * P],
                                     w2s[:, bass.ds(e, 1), f, :].rearrange("p a c -> p (a c)"),
                                     start=(f == 0), stop=(f == FC - 1))
                last.then_inc(s_y2, 1)

            def expert_of(s):
                return pe.value_load(slot_r[0:1, 1, bass.ds(s, 1)], min_val=0, max_val=NE - 1)

            def pe_step(r, k, it, experts=None):
                if it is None:
                    eh = expert_of(r + 1) if 0 <= r + 1 < NSLOT else None
                    ed = expert_of(r - 1) if r >= 1 else None
                    if r + 2 < NSLOT:
                        turn_rows(r + 2, r % 2, (r + 2) % 4, 32 * ((r + 2) // 4) + 32, r < 0)
                    if 0 <= r + 1 < NSLOT:
                        hidden(r + 1, (r + 1) % 2, r + 1 < 2, eh)
                    if 0 <= r < NSLOT:
                        turn_hidden(r, r % 2, r < 2)
                    if r >= 1:
                        down(r - 1, (r - 1) % 2, r - 1 < 2, ed)
                else:
                    experts.append(expert_of(r + 1))
                    eh, ed = experts[k], expert_of(r - 1) if k < 2 else experts[k - 2]
                    turn_rows(r + 2, k % 2, (k + 2) % 4, 32 * it + 32 * ((k + 2) // 4) + 32, False)
                    hidden(r + 1, (k + 1) % 2, False, eh)
                    turn_hidden(r, k % 2, False)
                    down(r - 1, (k + 1) % 2, False, ed)

            for r in range(-2, 4):
                pe_step(r, 0, None)
            with pe.Fori(1, (NSLOT - 2) // 4) as it:
                experts = []
                for k in range(4):
                    pe_step(4 * it + k, k, it, experts)
            for r in range((NSLOT - 2) // 4 * 4, NSLOT + 1):
                pe_step(r, 0, None)

        @block.vector
        def _(dve):
            dve.wait_ge(s_act0, 2)
            dve.wait_ge(s_load, NLOAD)
            dve.wait_ge(s_pool0, N_POOL0)
            n0 = [0]

            def link0(ins):
                n0[0] += 1
                ins.then_inc(s_dve0, 1)
                dve.wait_ge(s_dve0, n0[0])

            for b in range(B):
                last = dve.tensor_scalar(csil_bc[:, b, :], ones[:, :], csil[:, b:b + 1], None, ALU.mult)
            link0(last)
            for h in range(NH):
                dve.tensor_scalar(won[:, h, :], wo[:, h, :], nw[:, h:h + 1], None, ALU.mult)
            dve.tensor_scalar(cw[:, :, :, :], cw[:, :, :, :], 0.5, None, ALU.mult)
            dve.tensor_scalar(cb[:, :, :], cb[:, :, :], 0.5, None, ALU.mult)
            dve.tensor_tensor(gb_sum[:, :], gbias[:, 0, :], gbias[:, 1, :], ALU.add)
            link0(dve.tensor_scalar(sp[:, 0, 0:2 * NH], ab[:, :, 0], -1.0, None, ALU.mult))
            for k in range(2 * NH):
                last = dve.tensor_scalar(ab[:, k, :], ones[:, 0:TPB], sp[:, 0, k:k + 1], None, ALU.mult)
            for g in range(NG):
                dve.memset(raw[:, g, 0:HALO], 0.0)
                dve.memset(raw[:, g, HALO + L:HALO + L + HALO], 0.0)
            dve.memset(bs[:, :, :, :, :], 0.0)
            link0(dve.memset(st[:, 0, :], 0.0))
            dve.wait_ge(s_pe0, 1)
            dve.tensor_copy(modc[:, 0, :], bank[0][:, 0:B])
            link0(dve.tensor_scalar(modc[:, 1, :], bank[0][:, B:2 * B], 1.0, None, ALU.add))
            for b in range(B):
                dve.tensor_copy(row[:, b, 0:3, :], bank[1 + 2 * b][:, 0:3 * DM].rearrange("p (k c) -> p k c", k=3))
                last = dve.tensor_copy(row[:, b, 3:6, :], bank[2 + 2 * b][:, 0:3 * DM].rearrange("p (k c) -> p k c", k=3))
            link0(last)
            for b in range(B):
                last = dve.tensor_scalar(row[:, b, 4, :], row[:, b, 4, :], 1.0, None, ALU.add)
            link0(last)
            for b in range(B):
                g2 = row[:, b, 2:6:3, :]
                link0(dve.tensor_scalar(gtmp[:, b], g2, -1.0, None, ALU.mult))
                link0(dve.tensor_tensor(gtmp[:, b], gtmp[:, b], g2, ALU.max))
                link0(dve.tensor_scalar(gtmp[:, b], gtmp[:, b], 0.25, None, ALU.max))
                link0(dve.tensor_scalar(g2, g2, 0.0, 2.0, ALU.is_ge, ALU.mult))
            for b in range(B):
                g2 = row[:, b, 2:6:3, :]
                last = dve.scalar_tensor_tensor(out=g2, in0=g2, scalar=-1.0, in1=gtmp[:, b], op0=ALU.add, op1=ALU.mult)
            last.then_inc(s_dve0, N_DVE0 - n0[0])
            dve.wait_ge(s_dve0, N_DVE0)
            dve.wait_ge(s_x, 64)

            with dve.Fori(0, B) as b:
                for t in range(TPB):
                    dve.bn_stats(stat[:, t, :], xs[:, b * TPB + t, :]).then_inc(s_st, 1)
                for t in range(TPB):
                    hold(dve, s_st, b * TPB + t + 1)
                    dve.bn_aggr(mv[:, t, :], stat[:, t, :]).then_inc(s_mv, 1)
                dve.wait_ge(s_rstd, b + 1)

                def normed(i):
                    for j in range(BT):
                        n, t = BT * i + j, BT * (NBLK - 1 - i) + j
                        if n >= 4:
                            dve.wait_ge(s_xT, b * TPB + n - 3)
                        dve.tensor_scalar(xn[:, n % 4, :], xs[:, b * TPB + t, :], mv[:, t, 0:1], rstd[:, t:t + 1],
                                          ALU.subtract, ALU.mult).then_inc(s_xn, 1)

                normed(0)
                for i in range(NBLK):
                    k = NBLK - 1 - i
                    if i + 1 < NBLK:
                        normed(i + 1)
                    for g in range(NG):
                        dve.wait_ge(s_rawmm, b * NBLK * NG + NG * i + g + 1)
                        dve.tensor_copy(raw[:, g, HALO + k * BLK:HALO + (k + 1) * BLK], bank[2 + g][:, :]).then_inc(s_raw, 1)

                NL = 7
                cnt = [0]

                def link(ins):
                    cnt[0] += 1
                    ins.then_inc(s_dve, 1)
                    dve.wait_ge(s_dve, b * NL + cnt[0])

                dve.wait_ge(s_z, b * TPB + TPB)
                for d in range(2):
                    last = dve.tensor_tensor(sp[:, 0, d * NH * TPB:(d + 1) * NH * TPB].rearrange("p (h t) -> p h t", h=NH),
                                             dtr[:, :, :].rearrange("p t h -> p h t"), biasb[:, d * NH:(d + 1) * NH, :],
                                             ALU.add)
                link(last)
                link(dve.tensor_scalar(sp[:, 5, :], sp[:, 0, :], -1.0, None, ALU.mult))
                dve.tensor_tensor(sp[:, 1, :], sp[:, 0, :], sp[:, 5, :], ALU.max).then_inc(s_spe, 1)
                dve.wait_ge(s_spe, b * 4 + 2)
                dve.tensor_scalar(sp[:, 3, :], sp[:, 2, :], 1.0, None, ALU.add).then_inc(s_spe, 1)
                dve.wait_ge(s_spe, b * 4 + 4)
                link(dve.tensor_scalar(sp[:, 5, :], sp[:, 3, :], -1.0, None, ALU.add))
                link(dve.tensor_scalar(sp[:, 6, :], sp[:, 5, :], 0.0, None, ALU.is_equal))
                link(dve.tensor_tensor(sp[:, 5, :], sp[:, 5, :], sp[:, 6, :], ALU.add))
                dve.reciprocal(sp[:, 7, :], sp[:, 5, :])
                dve.tensor_tensor(sp[:, 4, :], sp[:, 4, :], sp[:, 2, :], ALU.mult)
                link(dve.tensor_tensor(sp[:, 6, :], sp[:, 6, :], sp[:, 2, :], ALU.mult))
                dve.tensor_tensor(sp[:, 4, :], sp[:, 4, :], sp[:, 7, :], ALU.mult)
                link(dve.tensor_scalar(sp[:, 0, :], sp[:, 0, :], 0.0, None, ALU.max))
                assert cnt[0] == NL
                dve.tensor_tensor(sp[:, 4, :], sp[:, 4, :], sp[:, 6, :], ALU.add).then_inc(s_wB, 1)
                dve.wait_ge(s_wB, b * 4 + 1)
                dve.tensor_tensor(dtv[:, :], sp[:, 4, :], sp[:, 0, :], ALU.add).then_inc(s_wB, 1)
                dve.wait_ge(s_wB, b * 4 + 2)
                dve.tensor_tensor(av[:, :], dtv[:, :], ab[:, :, :].rearrange("p k t -> p (k t)"), ALU.mult).then_inc(s_a, 1)
                dve.wait_ge(s_etab, b + 1)
                for c in range(3):
                    last = dve.tensor_copy(e0rep[:, :, c, :], etab[:, 0, :].rearrange("p (d k) -> p d k", d=2))
                last.then_inc(s_rep, 1)
                dve.tensor_tensor(wB[:, :], etab[:, 1, :], dtv[:, :], ALU.mult).then_inc(s_wB, 2)
                dve.wait_ge(s_erow, b + 1)
                W = NH * TPB

                def split(ins, n):
                    ins.then_inc(s_split, 1)
                    dve.wait_ge(s_split, b * 10 + n)

                for d in range(2):
                    er = erow[:, :, :]
                    split(dve.tensor_copy(er[:, 0, :], bank[6][0:3 * W, d * P:(d + 1) * P]), 5 * d + 1)
                    split(dve.tensor_copy(esplit[:, 0, :], er[:, 0, :]), 5 * d + 2)
                    split(dve.tensor_tensor(er[:, 1, :], er[:, 0, :], esplit[:, 0, :], ALU.subtract), 5 * d + 3)
                    split(dve.tensor_copy(esplit[:, 1, :], er[:, 1, :]), 5 * d + 4)
                    dve.tensor_copy(eparts[0:W, d, :], esplit[0:W, 0, :])
                    dve.tensor_copy(eparts[W:2 * W, d, :], esplit[W:2 * W, 1, :])
                    split(dve.tensor_tensor(er[:, 2, :], er[:, 1, :], esplit[:, 1, :], ALU.subtract), 5 * d + 5)
                    dve.tensor_copy(eparts[2 * W:3 * W, d, :], er[2 * W:3 * W, 2, :])
                phase_end(dve, b, 0)

                def taps(s, k):
                    d, blk = step_of(s)
                    off = (k - HALO) * (1 - 2 * d)
                    n = HALO - 1 - k
                    c0 = HALO + blk * BLK + off
                    for g in range(NH):
                        if n == 0:
                            dve.wait_ge(s_tap0, b * STEPS * NH + s * NH + g + 1)
                        else:
                            dve.wait_ge(s_tap, b * STEPS * 6 + 6 * s + 2 * (n - 1) + g + 1)
                        dve.scalar_tensor_tensor(out=acc[:, g, :], in0=raw[:, g, c0:c0 + BLK],
                                                 scalar=cw[:, d, g, k:k + 1], in1=acc[:, g, :],
                                                 op0=ALU.mult, op1=ALU.add).then_inc(s_tap, 1)

                def gate_bc(s):
                    dve.wait_ge(s_thb, b * STEPS + s + 1)
                    dve.scalar_tensor_tensor(out=bc[:, s % 2, :], in0=bc[:, s % 2, :], scalar=1.0, in1=acc_bc[s % 2],
                                             op0=ALU.add, op1=ALU.mult).then_inc(s_bc, 1)

                def mix(q):
                    d, t = chunk_of(q)
                    sg = bank[2 + q % 2]
                    c0 = (t % BT) * P
                    dve.wait_ge(s_e, b * CHUNKS + q + 1)
                    if q >= 2:
                        dve.wait_ge(s_ys, b * CHUNKS + q - 1)
                    for h in range(NH):
                        dve.scalar_tensor_tensor(out=ms[:, q % 2, h, :], in0=es[:, q % 2, h, :],
                                                 scalar=dtv[:, col(d, h, t)], in1=sg[:, DI:DI + P],
                                                 op0=ALU.mult, op1=ALU.mult)
                    dve.tensor_tensor(cs[:, q % 2, :], cc[:, (q // BT) % 2, c0:c0 + P], sg[:, DI + P:DI + 2 * P],
                                      ALU.mult).then_inc(s_m, 1)

                def carry(q):
                    d, t = chunk_of(q)
                    if q >= 1:
                        dve.wait_ge(s_ys, b * CHUNKS + q)
                        dve.wait_ge(s_S, b * CHUNKS + q)
                    if q % TPB == TPB - 1:
                        dve.memset(st[:, (q + 1) % 2, :], 0.0).then_inc(s_S, 1)
                        return
                    dve.wait_ge(s_sn, b * (CHUNKS - 2) + q + 1 - q // TPB)
                    dve.scalar_tensor_tensor(out=st[:, (q + 1) % 2, :], in0=st[:, q % 2, :], scalar=etot[:, d, t:t + 1],
                                             in1=bank[6 + q % 2][:, 0:DI], op0=ALU.mult, op1=ALU.add).then_inc(s_S, 1)

                for k in (2, 1, 0):
                    taps(0, k)
                gate_bc(0)
                taps(1, 2)
                taps(1, 1)
                mix(0)
                for q in range(CHUNKS):
                    d, t = chunk_of(q)
                    s, j = q // BT, q % BT
                    if j == 0 and s + 1 < STEPS:
                        taps(s + 1, 0)
                    if q + 1 < CHUNKS:
                        mix(q + 1)
                    carry(q)
                    if j == 1 and s + 1 < STEPS:
                        gate_bc(s + 1)
                    if j == 3 and s + 2 < STEPS:
                        taps(s + 2, 2)
                        taps(s + 2, 1)
                    dve.wait_ge(s_xt, b * CHUNKS + q + 1)
                    dve.wait_ge(s_ys, b * CHUNKS + q + 1)
                    dve.tensor_tensor(vs[:, q % 2, :], bank[4 + q % 2][:, 0:DI], ws[:, q % TM, :], ALU.add).then_inc(s_v, 1)
                    dve.wait_ge(s_v, b * CHUNKS + q + 1)
                    dve.tensor_tensor(yz[:, d, t, :], vs[:, q % 2, :], zs[:, t, :], ALU.mult).then_inc(s_yz, 1)
                phase_end(dve, b, 1)

                dve.wait_ge(s_rn, 4 * b + 1)

                def both(i):
                    dve.wait_ge(s_y1, b * NBLK + i + 1)
                    if i >= 1:
                        dve.wait_ge(s_yTm, b * NBLK + i)
                    for j in range(BT):
                        t = BT * i + j
                        last = dve.scalar_tensor_tensor(out=ysum[:, j, :], in0=yz[:, 1, t, :], scalar=rn[:, 1, t:t + 1],
                                                        in1=y1[:, j, :], op0=ALU.mult, op1=ALU.add)
                    last.then_inc(s_ysum, 1)

                def step(g, ins, n):
                    ins.then_inc(s_rt_dve, 1)
                    dve.wait_ge(s_rt_dve, NR * g + n)

                def choose(i):
                    g, a = b * NBLK + i, i % 2
                    wide = [P, BT, NE]
                    dve.wait_ge(s_lgm, g + 1)
                    step(g, dve.tensor_tensor(lg[:, :, :], bank[6 + a][:, 0:BT * NE].rearrange("p (j e) -> p j e", j=BT),
                                              gb_sum[:, :].unsqueeze(1).broadcast_to(wide), ALU.add), 1)
                    step(g, dve.tensor_reduce(mx[:, 0, :], lg[:, :, :], AX_X, ALU.max), 2)
                    step(g, dve.tensor_tensor(cand[:, :, :], lg[:, :, :], mx[:, 0, :].unsqueeze(2).broadcast_to(wide),
                                              ALU.is_equal), 3)
                    step(g, dve.tensor_tensor(cand[:, :, :], cand[:, :, :],
                                              rank8[:, :].unsqueeze(1).broadcast_to(wide), ALU.mult), 4)
                    step(g, dve.tensor_reduce(mx[:, 1, :], cand[:, :, :], AX_X, ALU.max), 5)
                    dve.tensor_tensor(hot[:, a, :, :], cand[:, :, :], mx[:, 1, :].unsqueeze(2).broadcast_to(wide),
                                      ALU.is_equal).then_inc(s_hot, 1)

                def place(i):
                    g, a = b * NBLK + i, i % 2
                    W = BT * NE
                    rank = bank[6 + a][:, W:2 * W].rearrange("p (j e) -> p j e", j=BT)
                    total = bank[6 + a][:, 2 * W:3 * W].rearrange("p (j e) -> p j e", j=BT)
                    dve.wait_ge(s_rank, g + 1)
                    for j in range(BT - 1):
                        step(g, dve.tensor_tensor(nextrow[:, a, j + 1, :], total[:, j, :], nextrow[:, a, j, :], ALU.add),
                             6 + j)
                    step(g, dve.tensor_tensor(nextrow[:, 1 - a, 0, :], total[:, BT - 1, :], nextrow[:, a, BT - 1, :],
                                              ALU.add), 5 + BT)
                    dve.tensor_tensor(pos[:, :, :], rank, nextrow[:, a, :, :], ALU.add).then_inc(s_routed, 1)
                    dve.wait_ge(s_routed, g + 1)
                    step(g, dve.tensor_tensor(pos[:, :, :], pos[:, :, :], hot[:, a, :, :], ALU.mult), 6 + BT)
                    step(g, dve.tensor_reduce(posf[:, :], pos[:, :, :], AX_X, ALU.add), 7 + BT)
                    if i >= 2:
                        for j in range(BT):
                            dve.wait_ge(s_scat[a * BT + j], b * 32 + 16 * (i // 2))
                    dve.tensor_copy(rowat[:, a * BT:(a + 1) * BT, :].rearrange("p j c -> p (j c)"),
                                    posf[:, :]).then_inc(s_pos, 1)

                both(0)
                for i in range(NBLK):
                    g, a = b * NBLK + i, i % 2
                    sl = slice(a * BT, (a + 1) * BT)
                    if i + 1 < NBLK:
                        both(i + 1)
                    dve.wait_ge(s_o, g + 1)
                    dve.tensor_tensor(o1, bank[2 + a][:, :].rearrange("p (j c) -> p j c", j=BT),
                                      row[:, b, 2, :].unsqueeze(1).broadcast_to([P, BT, DM]), ALU.mult).then_inc(s_o1, 1)
                    dve.wait_ge(s_o1, g + 1)
                    if i >= 2:
                        for j in range(BT):
                            dve.wait_ge(s_scat[a * BT + j], b * 32 + 16 * (i // 2))
                    dve.tensor_tensor(rows[:, sl, DM:2 * DM], xs[:, bass.ds(BT * g, BT), :], o1, ALU.add).then_inc(s_x1r, 1)
                    dve.wait_ge(s_x1r, g + 1)
                    for j in range(BT):
                        dve.bn_stats(st2[:, j, :], rows[:, a * BT + j, DM:2 * DM]).then_inc(s_st2, 1)
                    for j in range(BT):
                        hold(dve, s_st2, BT * g + j + 1)
                        last = dve.bn_aggr(mv2[:, a, j, :], st2[:, j, :])
                    last.then_inc(s_mv2, 1)
                    if i >= 1:
                        choose(i - 1)
                    dve.wait_ge(s_rs2, g + 1)
                    for j in range(BT):
                        last = dve.tensor_scalar(xn2[:, j, :], rows[:, a * BT + j, DM:2 * DM], mv2[:, a, j, 0:1],
                                                 rs2[:, a, j:j + 1], ALU.subtract, ALU.mult)
                    last.then_inc(s_xn2, 1)
                    dve.wait_ge(s_xn2, g + 1)
                    dve.tensor_tensor(rows[:, sl, 0:DM], xn2, row[:, b, 4, :].unsqueeze(1).broadcast_to([P, BT, DM]),
                                      ALU.mult).then_inc(s_h2a, 1)
                    if i >= 1:
                        place(i - 1)
                choose(NBLK - 1)
                place(NBLK - 1)
                phase_end(dve, b, 2)

            nt = [0]

            def tab(ins):
                nt[0] += 1
                ins.then_inc(s_tab, 1)
                dve.wait_ge(s_tab, 2 + nt[0])

            dve.wait_ge(s_tab, 2)
            dve.tensor_tensor(count[:, :], nextrow[:, 0, 0, :], region0[:, :], ALU.subtract).then_inc(s_gd, 1)
            dve.wait_ge(s_gd, 1)
            dve.tensor_scalar(padf, nextrow[:, 0, 0, :], pcol[:, 0:1], None, ALU.add)
            for e in range(NE):
                last = dve.tensor_scalar(tiles_gt[:, e, :], m128, count[:, e:e + 1], None, ALU.is_lt)
            tab(last)
            tab(dve.tensor_reduce(ntile, tiles_gt, AX_X, ALU.add))
            dve.tensor_scalar(coef, ntile, -float(P), float(REGION), ALU.mult, ALU.add)
            tab(dve.tensor_copy(cum[:, 0:1], ntile[:, 0:1]))
            dve.tensor_copy(padi, padf).then_inc(s_padi, 1)
            for e in range(1, NE):
                tab(dve.tensor_tensor(cum[:, e:e + 1], cum[:, e - 1:e], ntile[:, e:e + 1], ALU.add))
            for e in range(NE):
                dve.tensor_scalar(behind[:, 0, e, :], slot_i, cum[:, e:e + 1], coef[:, e:e + 1], ALU.is_ge, ALU.mult)
                last = dve.tensor_scalar(behind[:, 1, e, :], slot_i, cum[:, e:e + 1], None, ALU.is_ge)
            tab(last)
            for k in range(2):
                last = dve.tensor_reduce(slot_v[:, k, :], behind[:, k].rearrange("p e s -> p s e"), AX_X, ALU.add)
            tab(last)
            tab(dve.scalar_tensor_tensor(out=slot_v[:, 0, :], in0=slot_i, scalar=float(P), in1=slot_v[:, 0, :],
                                         op0=ALU.mult, op1=ALU.add))
            dve.tensor_scalar(slot_v[:, 0, :], slot_v[:, 0, :], float(NE * REGION), None, ALU.min)
            tab(dve.tensor_scalar(slot_v[:, 1, :], slot_v[:, 1, :], float(NE - 1), None, ALU.min))
            dve.tensor_copy(slot_r, slot_v).then_inc(s_tabv, 1)
            dve.wait_ge(s_tabv, 1)
            dve.tensor_tensor(gdiff, row[:, 1, 5, :], row[:, 0, 5, :], ALU.subtract).then_inc(s_gd, 1)
            dve.wait_ge(s_gd, 2)
            dve.wait_ge(s_wf, 64)

            def expert_of(s):
                return dve.value_load(slot_r[0:1, 1, bass.ds(s, 1)], min_val=0, max_val=NE - 1)

            def bias1(s, a, first, e):
                dve.wait_ge(s_h1, s + 1)
                if not first:
                    dve.wait_ge(s_hx, s - 1)
                dve.tensor_tensor(hb[:, a, :], bank[2 + a][:, :], b1s[:, bass.ds(e, 1), :].rearrange("p a f -> p (a f)"),
                                  ALU.add).then_inc(s_hb, 1)

            def combine(s, a, k, rk, first, put16, e):
                dve.wait_ge(s_rb[k], rk)
                dve.tensor_scalar(flag[:, a, :], xr[:, bass.ds(s, 1), DM:DM + 1].rearrange("p a c -> p (a c)"),
                                  float(L), None, ALU.is_ge).then_inc(s_flag, 1)
                dve.wait_ge(s_y2, s + 1)
                dve.tensor_tensor(yo1[:, a, :], bank[6 + a][:, 0:DM], b2s[:, bass.ds(e, 1), :].rearrange("p a c -> p (a c)"),
                                  ALU.add).then_inc(s_yo1, 1)
                dve.wait_ge(s_flag, s + 1)
                dve.scalar_tensor_tensor(out=gsel[:, a, :], in0=gdiff, scalar=flag[:, a, :],
                                         in1=row[:, 0, 5, :], op0=ALU.mult, op1=ALU.add).then_inc(s_gs, 1)
                dve.wait_ge(s_yo1, s + 1)
                dve.wait_ge(s_gs, s + 1)
                dve.tensor_tensor(yo2[:, a, :], yo1[:, a, :], gsel[:, a, :], ALU.mult).then_inc(s_yo2, 1)
                dve.wait_ge(s_yo2, s + 1)
                if not first:
                    dve.wait_ge(s_out[k], put16)
                dve.tensor_tensor(ob[:, k, :], yo2[:, a, :], xr[:, bass.ds(s, 1), 0:DM].rearrange("p a c -> p (a c)"),
                                  ALU.add).then_inc(s_ob, 1)

            def dve_step(r, k, it, experts=None):
                if it is None:
                    if 0 <= r + 1 < NSLOT:
                        bias1(r + 1, (r + 1) % 2, r + 1 < 2, expert_of(r + 1))
                    if r >= 1:
                        combine(r - 1, (r - 1) % 2, (r - 1) % 4, 32 * ((r - 1) // 4) + 32, r - 1 < 4,
                                16 * ((r - 1) // 4), expert_of(r - 1))
                else:
                    experts.append(expert_of(r + 1))
                    ed = expert_of(r - 1) if k < 2 else experts[k - 2]
                    bias1(r + 1, (k + 1) % 2, False, experts[k])
                    combine(r - 1, (k + 1) % 2, (k + 3) % 4, 32 * it + 32 * ((k + 3) // 4), False,
                            16 * it + 16 * ((k + 3) // 4) - 16, ed)

            for r in range(-1, 8):
                dve_step(r, 0, None)
            with dve.Fori(2, (NSLOT - 1) // 4) as it:
                experts = []
                for k in range(4):
                    dve_step(4 * it + k, k, it, experts)
            for r in range((NSLOT - 1) // 4 * 4, NSLOT + 1):
                dve_step(r, 0, None)



_INS = ["u", "w_xbc", "w_zdt", "conv_w", "conv_b", "dt_bias", "a_log", "d_skip", "norm_w", "w_out", "gate_w", "gate_b",
        "w1", "b1", "w2", "b2", "c_t", "wmod"]


def kernel(**inputs):
    import numpy as _np
    import concourse.bacc as _bacc
    from concourse import mybir as _mybir
    from concourse.bass_utils import run_bass_kernel_spmd as _run

    x = {k: _np.asarray(v) for k, v in inputs.items()}
    wi = x["L0_attn_in_proj_w"]

    def channels(fw, bw):
        return _np.stack([v.reshape((NG, P) + v.shape[1:]) for v in (fw, bw)]).swapaxes(0, 2).swapaxes(1, 2)

    laid = {
        "u": x["L0_attn_u"],
        "w_xbc": wi[DI:DI + NG * P].T,
        "w_zdt": _np.concatenate([wi[0:DI], wi[DI + NG * P:]]).T,
        "conv_w": channels(x["L0_attn_conv_w"], x["L0_attn_conv_w_bw"]),
        "conv_b": channels(x["L0_attn_conv_b"], x["L0_attn_conv_b_bw"]),
        "dt_bias": _np.concatenate([x["L0_attn_dt_bias"], x["L0_attn_dt_bias_bw"]]),
        "a_log": _np.concatenate([x["L0_attn_A_log"], x["L0_attn_A_b_log"]]),
        "d_skip": _np.concatenate([x["L0_attn_D"], x["L0_attn_D_b"]]),
        "norm_w": x["L0_attn_norm_w"].reshape(NH, HD).T,
        "w_out": x["L0_attn_out_proj_w"].T.reshape(NH, HD, DM).swapaxes(0, 1),
        "gate_w": x["L0_ffn_gate_w"].T,
        "gate_b": _np.stack([x["L0_ffn_gate_b"], x["L0_ffn_expert_bias"]]),
        "w1": x["L0_ffn_w1"].transpose(1, 0, 2),
        "b1": x["L0_ffn_b1"],
        "w2": x["L0_ffn_w2"].reshape(NE, FC, P, DM).transpose(2, 0, 1, 3),
        "b2": x["L0_ffn_b2"],
        "c_t": x["L0_c"].T,
        "wmod": x["L0_wmod"],
    }
    nc = _bacc.Bacc("TRN2", target_bir_lowering=False, num_devices=1)
    arrays, args = {}, []
    for name in _INS:
        a = _np.ascontiguousarray(laid[name])
        arrays[f"in_{name}_dram"] = a
        args.append(nc.dram_tensor(f"in_{name}_dram", a.shape, _mybir.dt.from_np(a.dtype), kind="ExternalInput").ap())
    args.append(nc.dram_tensor("out_0_dram", (B, L, DM), F32, kind="ExternalOutput").ap())
    build(nc, *args)
    r = _run(nc, [arrays], core_ids=[0])
    return r.results[0]["out_0_dram"]
```
